# Optimizing a Trainium2 kernel written in Bass

```python
import numpy as np
import jax
import jax.numpy as jnp

def _softmax(x, axis=-1):
    return jax.nn.softmax(x, axis=axis)

def _gelu(x):
    return jax.nn.gelu(x, approximate=True)

def _silu(x):
    return jax.nn.silu(x)

def _sigmoid(x):
    return jax.nn.sigmoid(x)

def _layernorm(x, axis=-1, eps=1e-05):
    m = jnp.mean(x, axis=axis, keepdims=True)
    v = jnp.var(x, axis=axis, keepdims=True)
    return (x - m) / jnp.sqrt(v + eps)

def _scatter_add(tgt, idx, src, axis=0):
    return tgt.at[idx].add(src)

def _segment_sum(src, seg, n):
    return jax.ops.segment_sum(src, seg, n)
kernel_name = 'mk_decoder_postln_d1_seqx_r4_15b2f5'

def setup_inputs(seed: int=0):
    np.random.seed(seed)
    _w = jnp.asarray

    def _rec_inputs():
        import jax
        import jax.numpy as jnp
        _rk = jax.random.key(seed)
        x = 7.22e-05 + 1 * jax.random.normal(jax.random.fold_in(_rk, 1), (16, 256, 256), jnp.float32)
        _lenS = 256 - jax.random.randint(jax.random.fold_in(_rk, 7), (16,), 0, max(1, 256 // 4) + 1, jnp.int32)
        _lenS2 = 120 - jax.random.randint(jax.random.fold_in(_rk, 8), (16,), 0, max(1, 120 // 4) + 1, jnp.int32)
        _ctx_1024P = jax.random.normal(jax.random.fold_in(_rk, 11), (16, 16, 256), jnp.float32)
        _ctx_1024c = jax.random.dirichlet(jax.random.fold_in(_rk, 511), 0.3 * jnp.ones((16,), jnp.float32), (16, 120))
        _ctx_1024t = jnp.einsum('bsk,bkd->bsd', _ctx_1024c, _ctx_1024P)
        _ctx_1024t = _ctx_1024t * jax.lax.rsqrt(jnp.mean(jnp.square(_ctx_1024t)) + 1e-12) * 0.953939
        ctx_1024 = -0.000514642 + 1.00011 * (_ctx_1024t + 0.3 * jax.random.normal(jax.random.fold_in(_rk, 611), (16, 120, 256), jnp.float32))
        return (x, ctx_1024)
    x, ctx_1024 = _rec_inputs()

    def _L0_attn_setup():
        import jax, jax.numpy as jnp
        import numpy as np
        D = 256

        def _layernorm(x, gamma, beta, eps=1e-05):
            mu = jnp.mean(x, axis=-1, keepdims=True)
            var = jnp.var(x, axis=-1, keepdims=True)
            return (x - mu) * jax.lax.rsqrt(var + eps) * gamma + beta
        key = jax.random.key(seed)
        ks = jax.random.split(key, 8)
        B, S = (4, 1024)
        hidden_states = jax.random.normal(ks[0], (B, S, D), dtype=jnp.float32)
        attention_mask = jnp.ones((B, S), dtype=jnp.int32)
        scale = 0.02
        Wq = jax.random.normal(ks[1], (D, D), jnp.float32) * scale
        bq = jnp.zeros((D,), jnp.float32)
        Wk = jax.random.normal(ks[2], (D, D), jnp.float32) * scale
        bk = jnp.zeros((D,), jnp.float32)
        Wv = jax.random.normal(ks[3], (D, D), jnp.float32) * scale
        bv = jnp.zeros((D,), jnp.float32)
        Wqa = jnp.zeros((D, D), jnp.float32)
        bqa = jnp.ones((D,), jnp.float32)
        Wka = jnp.zeros((D, D), jnp.float32)
        bka = jnp.ones((D,), jnp.float32)
        gamma = jnp.ones((D,), jnp.float32)
        beta = jnp.zeros((D,), jnp.float32)
        return {'hidden_states': hidden_states, 'attention_mask': attention_mask, 'Wq': Wq, 'bq': bq, 'Wqa': Wqa, 'bqa': bqa, 'Wk': Wk, 'bk': bk, 'Wka': Wka, 'bka': bka, 'Wv': Wv, 'bv': bv, 'gamma': gamma, 'beta': beta}
    _L0_attn_all = _L0_attn_setup()
    _L0_attn_in = {k: v for k, v in _L0_attn_all.items() if k in ('attention_mask', 'Wq', 'bq', 'Wqa', 'bqa', 'Wk', 'bk', 'Wka', 'bka', 'Wv', 'bv', 'gamma', 'beta')}
    del _L0_attn_all

    def _L0_xattn_setup():
        import jax, jax.numpy as jnp
        import numpy as np
        B, L_ENC, L_DEC, D = (16, 128, 128, 256)
        key = jax.random.key(seed)
        k1, k2, k3, k4, k5, k6 = jax.random.split(key, 6)
        encoder_hc = jax.random.normal(k1, (B, L_ENC, D), dtype=jnp.float32)
        decoder_hq = jax.random.normal(k2, (B, L_DEC, D), dtype=jnp.float32)
        w_sim = jax.random.normal(k3, (3 * D,), dtype=jnp.float32) * 0.02
        b_sim = jax.random.normal(k4, (1,), dtype=jnp.float32) * 0.02
        W_qv = jax.random.normal(k5, (4 * D, D), dtype=jnp.float32) * 0.02
        b_qv = jax.random.normal(k6, (D,), dtype=jnp.float32) * 0.02
        return {'encoder_hc': encoder_hc, 'decoder_hq': decoder_hq, 'w_sim': w_sim, 'b_sim': b_sim, 'W_qv': W_qv, 'b_qv': b_qv}
    _L0_xattn_all = _L0_xattn_setup()
    _L0_xattn_in = {k: v for k, v in _L0_xattn_all.items() if k in ('w_sim', 'b_sim', 'W_qv', 'b_qv')}
    del _L0_xattn_all

    def _L0_ffn_setup():
        import jax, jax.numpy as jnp
        import numpy as np
        EPS = 1e-05
        N_HEADS = 16
        TOP_K = 2

        def _ln(x, g, b):
            m = x.mean(-1, keepdims=True)
            v = ((x - m) ** 2).mean(-1, keepdims=True)
            return (x - m) / jnp.sqrt(v + EPS) * g + b

        def _block_fwd(x, ln1_g, ln1_b, ln2_g, ln2_b, Wq, bq, Wk, bk, Wv, bv, Wo, bo, Wr, br, e_w1, e_b1, e_w2, e_b2):
            B, S, D = x.shape
            H = N_HEADS
            hd = D // H
            h = _ln(x, ln1_g, ln1_b)
            q = (h @ Wq + bq).reshape(B, S, H, hd).transpose(0, 2, 1, 3)
            k = (h @ Wk + bk).reshape(B, S, H, hd).transpose(0, 2, 1, 3)
            v = (h @ Wv + bv).reshape(B, S, H, hd).transpose(0, 2, 1, 3)
            scores = jnp.einsum('bhqd,bhkd->bhqk', q, k) / hd ** 0.5
            causal = jnp.tril(jnp.ones((S, S), dtype=bool))
            scores = jnp.where(causal, scores, -jnp.inf)
            attn = jax.nn.softmax(scores, axis=-1)
            o = jnp.einsum('bhqk,bhkd->bhqd', attn, v).transpose(0, 2, 1, 3).reshape(B, S, D)
            a = o @ Wo + bo + x
            h2 = _ln(a, ln2_g, ln2_b)
            logits = h2 @ Wr + br
            topv = jax.lax.top_k(logits, TOP_K)[0]
            kmask = logits >= topv[..., -1:]
            w = jax.nn.softmax(jnp.where(kmask, logits, -jnp.inf), axis=-1)
            mid = jax.nn.gelu(jnp.einsum('bsd,edf->bsef', h2, e_w1) + e_b1, approximate=False)
            eo = jnp.einsum('bsef,efd->bsed', mid, e_w2) + e_b2
            moe = jnp.einsum('bse,bsed->bsd', w, eo)
            return moe + a
        key = jax.random.key(seed)
        B, S, D, E = (1, 512, 256, 8)
        F = 4 * D
        ks = jax.random.split(key, 8)

        def n(k, shape):
            return jax.random.normal(k, shape, jnp.float32) * 0.02
        return dict(x=jax.random.normal(ks[0], (B, S, D), jnp.float32), ln1_g=jnp.ones((D,), jnp.float32), ln1_b=jnp.zeros((D,), jnp.float32), ln2_g=jnp.ones((D,), jnp.float32), ln2_b=jnp.zeros((D,), jnp.float32), Wq=n(ks[1], (D, D)), bq=jnp.zeros((D,), jnp.float32), Wk=n(ks[2], (D, D)), bk=jnp.zeros((D,), jnp.float32), Wv=n(ks[3], (D, D)), bv=jnp.zeros((D,), jnp.float32), Wo=n(ks[4], (D, D)), bo=jnp.zeros((D,), jnp.float32), Wr=n(ks[5], (D, E)), br=jnp.zeros((E,), jnp.float32), e_w1=n(ks[6], (E, D, F)), e_b1=jnp.zeros((E, F), jnp.float32), e_w2=n(ks[7], (E, F, D)), e_b2=jnp.zeros((E, D), jnp.float32))
    _L0_ffn_all = _L0_ffn_setup()
    _L0_ffn_in = {k: v for k, v in _L0_ffn_all.items() if k in ('ln1_g', 'ln1_b', 'ln2_g', 'ln2_b', 'Wq', 'bq', 'Wk', 'bk', 'Wv', 'bv', 'Wo', 'bo', 'Wr', 'br', 'e_w1', 'e_b1', 'e_w2', 'e_b2')}
    del _L0_ffn_all
    return {'x': x, 'ctx_1024': ctx_1024, 'L0_attn_attention_mask': _L0_attn_in['attention_mask'], 'L0_attn_Wq': _L0_attn_in['Wq'], 'L0_attn_bq': _L0_attn_in['bq'], 'L0_attn_Wqa': _L0_attn_in['Wqa'], 'L0_attn_bqa': _L0_attn_in['bqa'], 'L0_attn_Wk': _L0_attn_in['Wk'], 'L0_attn_bk': _L0_attn_in['bk'], 'L0_attn_Wka': _L0_attn_in['Wka'], 'L0_attn_bka': _L0_attn_in['bka'], 'L0_attn_Wv': _L0_attn_in['Wv'], 'L0_attn_bv': _L0_attn_in['bv'], 'L0_attn_gamma': _L0_attn_in['gamma'], 'L0_attn_beta': _L0_attn_in['beta'], 'L0_xattn_w_sim': _L0_xattn_in['w_sim'], 'L0_xattn_b_sim': _L0_xattn_in['b_sim'], 'L0_xattn_W_qv': _L0_xattn_in['W_qv'], 'L0_xattn_b_qv': _L0_xattn_in['b_qv'], 'L0_ffn_ln1_g': _L0_ffn_in['ln1_g'], 'L0_ffn_ln1_b': _L0_ffn_in['ln1_b'], 'L0_ffn_ln2_g': _L0_ffn_in['ln2_g'], 'L0_ffn_ln2_b': _L0_ffn_in['ln2_b'], 'L0_ffn_Wq': _L0_ffn_in['Wq'], 'L0_ffn_bq': _L0_ffn_in['bq'], 'L0_ffn_Wk': _L0_ffn_in['Wk'], 'L0_ffn_bk': _L0_ffn_in['bk'], 'L0_ffn_Wv': _L0_ffn_in['Wv'], 'L0_ffn_bv': _L0_ffn_in['bv'], 'L0_ffn_Wo': _L0_ffn_in['Wo'], 'L0_ffn_bo': _L0_ffn_in['bo'], 'L0_ffn_Wr': _L0_ffn_in['Wr'], 'L0_ffn_br': _L0_ffn_in['br'], 'L0_ffn_e_w1': _L0_ffn_in['e_w1'], 'L0_ffn_e_b1': _L0_ffn_in['e_b1'], 'L0_ffn_e_w2': _L0_ffn_in['e_w2'], 'L0_ffn_e_b2': _L0_ffn_in['e_b2']}

def reference(x, ctx_1024, L0_attn_attention_mask, L0_attn_Wq, L0_attn_bq, L0_attn_Wqa, L0_attn_bqa, L0_attn_Wk, L0_attn_bk, L0_attn_Wka, L0_attn_bka, L0_attn_Wv, L0_attn_bv, L0_attn_gamma, L0_attn_beta, L0_xattn_w_sim, L0_xattn_b_sim, L0_xattn_W_qv, L0_xattn_b_qv, L0_ffn_ln1_g, L0_ffn_ln1_b, L0_ffn_ln2_g, L0_ffn_ln2_b, L0_ffn_Wq, L0_ffn_bq, L0_ffn_Wk, L0_ffn_bk, L0_ffn_Wv, L0_ffn_bv, L0_ffn_Wo, L0_ffn_bo, L0_ffn_Wr, L0_ffn_br, L0_ffn_e_w1, L0_ffn_e_b1, L0_ffn_e_w2, L0_ffn_e_b2):
    import jax
    import jax.numpy as jnp

    def _L0_attn_ref(hidden_states, attention_mask, Wq, bq, Wqa, bqa, Wk, bk, Wka, bka, Wv, bv, gamma, beta):
        import jax, jax.numpy as jnp
        import numpy as np
        D = 256

        def _layernorm(x, gamma, beta, eps=1e-05):
            mu = jnp.mean(x, axis=-1, keepdims=True)
            var = jnp.var(x, axis=-1, keepdims=True)
            return (x - mu) * jax.lax.rsqrt(var + eps) * gamma + beta
        h = _layernorm(hidden_states, gamma, beta)
        B, S, d_model = h.shape
        inv_sqrt_d = 1.0 / jnp.sqrt(jnp.float32(d_model))
        query = h @ Wq + bq
        keys = h @ Wk + bk
        values = h @ Wv + bv
        scaling = jnp.arange(1, S + 1, dtype=h.dtype).reshape(1, S, 1)
        query_weight = jax.nn.softmax((query @ Wqa + bqa) * inv_sqrt_d, axis=-1)
        pooled_query = jnp.cumsum(query_weight * query, axis=1) / scaling
        mixed_keys = pooled_query * keys
        keys_weight = jax.nn.softmax((mixed_keys @ Wka + bka) * inv_sqrt_d, axis=-1)
        pooled_keys = jnp.cumsum(keys_weight * mixed_keys, axis=1) / scaling
        return pooled_keys * values

    def _L0_xattn_ref(encoder_hc, decoder_hq, w_sim, b_sim, W_qv, b_qv):
        import jax, jax.numpy as jnp
        import numpy as np
        B, L_ENC, L_DEC, D = (16, 128, 128, 256)
        d = encoder_hc.shape[-1]
        w1, w2, w3 = (w_sim[:d], w_sim[d:2 * d], w_sim[2 * d:])
        Sim = (encoder_hc @ w1)[:, :, None] + (decoder_hq @ w2)[:, None, :] + jnp.einsum('bid,bjd->bij', encoder_hc * w3, decoder_hq) + b_sim[0]
        A = jax.nn.softmax(Sim, axis=2)
        hq_hat = jnp.einsum('bij,bjd->bid', A, decoder_hq)
        Batt = jax.nn.softmax(jnp.max(Sim, axis=2), axis=1)
        hc_bar = jnp.einsum('bi,bid->bd', Batt, encoder_hc)[:, None, :]
        hc_hat = jnp.broadcast_to(hc_bar, encoder_hc.shape)
        feats = jnp.concatenate([encoder_hc, hq_hat, encoder_hc * hq_hat, encoder_hc * hc_hat], axis=-1)
        hcq = feats @ W_qv + b_qv
        return hcq

    def _L0_ffn_ref(x, ln1_g, ln1_b, ln2_g, ln2_b, Wq, bq, Wk, bk, Wv, bv, Wo, bo, Wr, br, e_w1, e_b1, e_w2, e_b2):
        import jax, jax.numpy as jnp
        import numpy as np
        EPS = 1e-05
        N_HEADS = 16
        TOP_K = 2

        def _ln(x, g, b):
            m = x.mean(-1, keepdims=True)
            v = ((x - m) ** 2).mean(-1, keepdims=True)
            return (x - m) / jnp.sqrt(v + EPS) * g + b

        def _block_fwd(x, ln1_g, ln1_b, ln2_g, ln2_b, Wq, bq, Wk, bk, Wv, bv, Wo, bo, Wr, br, e_w1, e_b1, e_w2, e_b2):
            B, S, D = x.shape
            H = N_HEADS
            hd = D // H
            h = _ln(x, ln1_g, ln1_b)
            q = (h @ Wq + bq).reshape(B, S, H, hd).transpose(0, 2, 1, 3)
            k = (h @ Wk + bk).reshape(B, S, H, hd).transpose(0, 2, 1, 3)
            v = (h @ Wv + bv).reshape(B, S, H, hd).transpose(0, 2, 1, 3)
            scores = jnp.einsum('bhqd,bhkd->bhqk', q, k) / hd ** 0.5
            causal = jnp.tril(jnp.ones((S, S), dtype=bool))
            scores = jnp.where(causal, scores, -jnp.inf)
            attn = jax.nn.softmax(scores, axis=-1)
            o = jnp.einsum('bhqk,bhkd->bhqd', attn, v).transpose(0, 2, 1, 3).reshape(B, S, D)
            a = o @ Wo + bo + x
            h2 = _ln(a, ln2_g, ln2_b)
            logits = h2 @ Wr + br
            topv = jax.lax.top_k(logits, TOP_K)[0]
            kmask = logits >= topv[..., -1:]
            w = jax.nn.softmax(jnp.where(kmask, logits, -jnp.inf), axis=-1)
            mid = jax.nn.gelu(jnp.einsum('bsd,edf->bsef', h2, e_w1) + e_b1, approximate=False)
            eo = jnp.einsum('bsef,efd->bsed', mid, e_w2) + e_b2
            moe = jnp.einsum('bse,bsed->bsd', w, eo)
            return moe + a
        return _block_fwd(x, ln1_g, ln1_b, ln2_g, ln2_b, Wq, bq, Wk, bk, Wv, bv, Wo, bo, Wr, br, e_w1, e_b1, e_w2, e_b2)
    x = _layernorm(x + _L0_attn_ref(x, L0_attn_attention_mask, L0_attn_Wq, L0_attn_bq, L0_attn_Wqa, L0_attn_bqa, L0_attn_Wk, L0_attn_bk, L0_attn_Wka, L0_attn_bka, L0_attn_Wv, L0_attn_bv, L0_attn_gamma, L0_attn_beta), axis=-1)
    x = _layernorm(x + _L0_xattn_ref(x, ctx_1024, L0_xattn_w_sim, L0_xattn_b_sim, L0_xattn_W_qv, L0_xattn_b_qv), axis=-1)
    x = _layernorm(x + _L0_ffn_ref(x, L0_ffn_ln1_g, L0_ffn_ln1_b, L0_ffn_ln2_g, L0_ffn_ln2_b, L0_ffn_Wq, L0_ffn_bq, L0_ffn_Wk, L0_ffn_bk, L0_ffn_Wv, L0_ffn_bv, L0_ffn_Wo, L0_ffn_bo, L0_ffn_Wr, L0_ffn_br, L0_ffn_e_w1, L0_ffn_e_b1, L0_ffn_e_w2, L0_ffn_e_b2), axis=-1)
    return x

_drawn_inputs = setup_inputs


def setup_inputs(seed=0):
    import zlib

    import numpy as np

    out = dict(_drawn_inputs(seed))
    spreads = {'L0_attn_bq': (0.0, 2.0),
     'L0_attn_Wqa': (0.0, 2.0),
     'L0_attn_bqa': (1.0, 0.6),
     'L0_attn_bk': (0.0, 2.0),
     'L0_attn_Wka': (0.0, 2.0),
     'L0_attn_bka': (1.0, 0.6),
     'L0_attn_bv': (0.0, 2.0),
     'L0_attn_gamma': (1.0, 0.6),
     'L0_attn_beta': (0.0, 2.0),
     'L0_ffn_ln1_g': (1.0, 0.6),
     'L0_ffn_ln1_b': (0.0, 0.8),
     'L0_ffn_ln2_g': (1.0, 0.6),
     'L0_ffn_ln2_b': (0.0, 0.487),
     'L0_ffn_bq': (0.0, 0.8),
     'L0_ffn_bk': (0.0, 2.0),
     'L0_ffn_bv': (0.0, 0.488),
     'L0_ffn_bo': (0.0, 0.1),
     'L0_ffn_br': (0.0, 0.1),
     'L0_ffn_e_b1': (0.0, 0.628),
     'L0_ffn_e_b2': (0.0, 0.1)}
    factors = {'L0_attn_Wq': 64.0,
     'L0_attn_Wk': 64.0,
     'L0_attn_Wv': 64.0,
     'L0_xattn_b_qv': 2.81,
     'L0_ffn_Wq': 8.0,
     'L0_ffn_Wk': 8.0,
     'L0_ffn_Wv': 3.795}
    for name, (base, spread) in spreads.items():
        noise = np.random.default_rng([zlib.crc32(name.encode()), seed]).standard_normal(out[name].shape)
        drawn = base * np.exp(spread * noise) if base else spread * noise
        out[name] = jnp.asarray(drawn.astype(out[name].dtype))
    for name, factor in factors.items():
        out[name] = (out[name] * factor).astype(out[name].dtype)
    return out
```

```python
from contextlib import ExitStack

import concourse.bass as bass
from concourse import mybir

F32 = mybir.dt.float32
F32R = mybir.dt.float32r
BF16 = mybir.dt.bfloat16
ALU = mybir.AluOpType
ACT = mybir.ActivationFunctionType
AX = mybir.AxisListType

P = 128
B, S, D = 16, 256, 256
T = B * S
NT = T // P
TB = 4
BLK = TB * P
NBLK = T // BLK
SB = BLK // S
KC = D // P
C = 120
H, HD = 16, 16
E, F = 8, 1024
FT = F // P
EPS = 1e-5

COLS = ["bq", "bk", "gamma", "beta", "w1", "w2", "w3", "g1", "b1", "g2", "b2", "fbq", "fbk", "even", "odd"]
ROWS = {"bv": D, "bqa": D, "bka": D, "bqv": D, "fbv": D, "bo": D, "br": E, "bs": 1}
MATS = ["Wq", "Wqa", "Wk", "Wka", "Wv", "Wf0", "Wf1", "Wf2", "Wf3", "fWq", "fWk", "fWv", "fWo"]


class Count:

    def __init__(self, sem, per):
        self.sem, self.per = sem, per

    def at(self, it, k=None):
        return it * self.per + (self.per if k is None else k)


def decoder_kernel(nc, x, ctx_in, mats_in, cols_in, rows_in, wr_in, ident_in, tri_in, mask_in,
                   w1_in, w2_in, eb1_in, eb2_in, out):
    with ExitStack() as stack:
        def sb(name, shape, dt=F32):
            return stack.enter_context(nc.sbuf_tensor(name, shape, dt))

        def signal(name, per=1):
            return Count(stack.enter_context(nc.semaphore(name)), per)

        ps = stack.enter_context(nc.psum_tensor("ps", [P, 8, 512], F32))

        def pair(bank):
            return ps[:, bank:bank + 2, :].rearrange("p b (t d) -> p (b t) d", t=2)

        def wait_apart(eng, sem, value):
            value = eng.to_reg(value)
            eng.wait_ge(c_loaded.sem, 16)
            eng.wait_ge(sem, value)

        def tile_of(bank, t):
            return ps[:, bank + t // 2, (t % 2) * D:(t % 2 + 1) * D]

        acc = sb("acc", [P, NT, D])
        wts = sb("wts", [P, NT, E])
        h2hi = sb("h2hi", [P, KC, T], F32R)
        h2lo = sb("h2lo", [P, KC, T], F32R)
        eb1 = sb("expert_b1", [P, E, FT])

        c_loaded = signal("consts_loaded", 16)
        block_done = signal("blocks_done")
        eps_t = sb("eps_half", [P, TB])

        with ExitStack() as front:
            def fb(name, shape, dt=F32):
                return front.enter_context(nc.sbuf_tensor(name, shape, dt))

            def fsig(name, per=1):
                return Count(front.enter_context(nc.semaphore(name)), per)

            mats = fb("mats_sb", [P, len(MATS), KC, D])
            cols = fb("cols_sb", [P, len(COLS), KC])
            rows = fb("rows_sb", [P, sum(ROWS.values())])
            wr = fb("wr_sb", [P, KC, E])
            ident = fb("ident_sb", [P, P])
            identb = fb("identb", [P, P], BF16)
            tri = fb("tri_sb", [P, 3, P])
            mask = fb("mask_sb", [P, 2, S], BF16)
            eb2 = fb("expert_b2", [E, D])
            ones = fb("ones", [P, P])
            qscale = fb("qscale", [P, 2, KC])
            qbias = fb("qbias", [P, 2, KC])

            W = {n: mats[:, i] for i, n in enumerate(MATS)}
            col = {n: (lambda kc, i=i: cols[:, i, kc:kc + 1]) for i, n in enumerate(COLS)}
            row, at = {}, 0
            for n, w in ROWS.items():
                row[n] = rows[:, at:at + w]
                at += w

            def over_tiles(r, n=TB):
                w = r.shape[1]
                return r.rearrange("p (o d) -> p o d", o=1).to_broadcast([P, n, w])

            room4 = fb("room4", [P, 4, TB * D])
            xt, lg, pt = (room4[:, i, :].rearrange("p (t d) -> p t d", t=TB) for i in range(3))
            x1T = room4[:, 3, :].rearrange("p (k n) -> p k n", k=KC)
            p8 = room4[:, :, :].rearrange("p (a b) (h k) -> p a (b h) k", a=2, k=S)
            room2 = fb("room2", [P, 2, TB * D])
            Wx = room2[:, 0, :].rearrange("p (b k d) -> p b k d", b=SB, k=KC)
            x1 = room2[:, 1, :].rearrange("p (t d) -> p t d", t=TB)
            qz = room2[:, :, :].rearrange("p e (k n) -> p e k n", k=KC)
            ctx = fb("ctx_tok", [C, SB, D])
            hn = fb("hn_tok", [P, TB, D])
            hT = fb("hT", [P, KC, BLK])
            qT = fb("qT", [P, KC, BLK])
            kT = fb("kT", [P, KC, BLK])
            vt = fb("v_tok", [P, TB, D])
            wt = fb("w_tok", [P, TB, D])
            x2 = fb("x2_tok", [P, TB, D])
            AT = fb("AT", [C, BLK])
            cT = fb("cT", [P, KC, SB * C])
            PT = fb("PT", [P, 3, 512])
            st = fb("bn_parts", [P, TB, 6])
            mv = fb("mean_var", [P, TB, 2])
            ve = fb("var_eps", [P, TB])
            rstd = fb("rstd", [P, TB])
            mx = fb("max4", [P, TB])
            nm = fb("negmax4", [P, TB])
            sm = fb("sum4", [P, TB])
            rs = fb("rsum4", [P, TB])
            bm = fb("b_rowmax", [P, TB])
            bg = fb("b_seqmax", [1, SB])
            bd = fb("b_diff", [P, TB])
            be = fb("b_exp", [P, TB])
            hcr = fb("hc_recip", [P, SB])
            hc = fb("hc", [P, SB, KC])
            mx8 = fb("max8", [P, 8])
            nm8 = fb("negmax8", [P, 2, 8])
            sm16 = fb("sum16", [P, TB, H])
            rs16 = fb("rsum16", [P, H])
            rl = fb("router_logits", [P, TB, E])
            rt8 = fb("router_sorted", [P, TB, 8])
            rex = fb("router_exp", [P, TB, E])
            rw = fb("router_w", [P, TB, E])
            wT = fb("router_wT", [E, BLK])

            consts = fsig("front_consts")
            pool_consts = fsig("pool_consts")
            x_in = fsig("x_in", 16)
            ctx_in_ = fsig("ctx_in", 16)
            ln_stat = fsig("ln_stat", 4 * TB)
            ln_mv = fsig("ln_mv", 4 * TB)
            ln_ve = fsig("ln_ve", 5)
            ln_rstd = fsig("ln_rstd", 5)
            ln_out = fsig("ln_out", 5 * TB)
            hT_ps = fsig("hT_ps", 3)
            hT_sb = fsig("hT_sb", 3 * KC)
            q_ps = fsig("q_ps", 2)
            k_ps = fsig("k_ps", 2)
            v_ps = fsig("v_ps", 2)
            qT_sb = fsig("qT_sb", KC)
            kT_sb = fsig("kT_sb", 2 * KC)
            v_sb = fsig("v_sb", 2)
            tok_ps = fsig("tok_ps", 2)
            lg_ps = fsig("lg_ps", 2 * TB)
            lg_sb = fsig("lg_sb", 2 * TB)
            lg_nm = fsig("lg_nm", 2)
            p_sb = fsig("p_sb", 2 * TB)
            p_rs = fsig("p_rs", 2)
            w_sb = fsig("w_sb", 2 * TB)
            pool_ps = fsig("pool_ps", KC)
            mT_sb = fsig("mT_sb", KC)
            pk_ps = fsig("pk_ps")
            a_mul = fsig("a_mul")
            a_sum = fsig("a_sum")
            x1T_ps = fsig("x1T_ps")
            cT_ps = fsig("cT_ps")
            x1T_sb = fsig("x1T_sb")
            cT_sb = fsig("cT_sb")
            xwT_sb = fsig("xwT_sb", KC)
            sim_ps = fsig("sim_ps")
            sim_mx = fsig("sim_mx")
            sim_nm = fsig("sim_nm", 2)
            bp_sb = fsig("bp_sb", TB)
            bp_rs = fsig("bp_rs")
            A_sb = fsig("A_sb", TB)
            AT_ps = fsig("AT_ps")
            mrow_ps = fsig("mrow_ps")
            AT_sb = fsig("AT_sb")
            g_sb = fsig("g_sb")
            g_ps = fsig("g_ps")
            bd_sb = fsig("bd_sb", SB)
            be_sb = fsig("be_sb")
            hq_ps = fsig("hq_ps")
            hqT_sb = fsig("hqT_sb")
            xhT_sb = fsig("xhT_sb")
            hc_ps = fsig("hc_ps")
            hc_rs = fsig("hc_rs")
            hc_sb = fsig("hc_sb", SB)
            Wx_sb = fsig("Wx_sb", SB * KC)
            hcq_ps = fsig("hcq_ps")
            b_bias = fsig("b_bias")
            b_sum = fsig("b_sum")
            qz_sb = fsig("qz_sb", 2 * KC)
            s_ps = fsig("s_ps", 2 * TB)
            s_mx = fsig("s_mx", 2 * TB)
            s_nm = fsig("s_nm", 2 * TB)
            s_p = fsig("s_p", 2 * TB)
            NCH = 2 * SB * (2 + 4)
            pT_ps = fsig("pT_ps", NCH)
            pT_sb = fsig("pT_sb", NCH)
            pT_used = fsig("pT_used", NCH)
            o_rs = fsig("o_rs", TB)
            o_sb = fsig("o_sb", TB)
            oT_ps = fsig("oT_ps")
            oT_sb = fsig("oT_sb")
            ao_ps = fsig("ao_ps")
            c_bias = fsig("c_bias")
            c_sum = fsig("c_sum")
            h2_split = fsig("h2_split", 2)
            rl_ps = fsig("rl_ps")
            rl_sb = fsig("rl_sb")
            rl_max = fsig("rl_max", TB)
            rl_nm = fsig("rl_nm")
            rl_exp = fsig("rl_exp", TB)
            rl_w = fsig("rl_w", TB)
            rl_rs = fsig("rl_rs")
            rl_out = fsig("rl_out")
            wT_ps = fsig("wT_ps")
            wT_sb = fsig("wT_sb")
            mb_ps = fsig("mb_ps")
            acc_xa = fsig("acc_xa")

            block = front.enter_context(nc.Block())

            def stats(eng, it, n, src):
                for t in range(TB):
                    eng.bn_stats(st[:, t, :], src[:, t, :]).then_inc(ln_stat.sem, 1)
                for t in range(TB):
                    wait_apart(eng, ln_stat.sem, it * 5 * TB + n * TB + t + 1)
                    eng.bn_aggr(mv[:, t, :], st[:, t, :]).then_inc(ln_mv.sem, 1)
                eng.wait_ge(ln_mv.sem, it * 5 * TB + n * TB + TB)
                eng.tensor_scalar(ve[:, :], mv[:, :, 1], EPS, None, ALU.add).then_inc(ln_ve.sem, 1)

            def normalize(eng, it, n, src, dst):
                eng.wait_ge(ln_rstd.sem, ln_rstd.at(it, n + 1))
                for t in range(TB):
                    eng.tensor_scalar(dst[:, t, :], src[:, t, :], mv[:, t, 0:1], rstd[:, t:t + 1],
                                      ALU.subtract, ALU.mult).then_inc(ln_out.sem, 1)

            def chunks_before(s):
                return sum(4 if (i // 2) % 2 else 2 for i in range(s))

            @block.sync
            def _(sp):
                sp.dma_start(cols[:, :, :], cols_in).then_inc(c_loaded.sem, 16)
                sp.dma_start(rows[:, :], rows_in).then_inc(c_loaded.sem, 16)
                sp.dma_start(ident[:, :], ident_in).then_inc(c_loaded.sem, 16)
                sp.dma_start(tri[:, :, :], tri_in).then_inc(c_loaded.sem, 16)
                sp.dma_start(mask[:, :, :], mask_in).then_inc(c_loaded.sem, 16)
                for i in range(len(MATS)):
                    sp.dma_start(mats[:, i], mats_in[i].rearrange("(k p) n -> p k n", p=P)).then_inc(c_loaded.sem, 16)
                sp.dma_start(wr[:, :, :], wr_in.rearrange("(k p) n -> p k n", p=P)).then_inc(c_loaded.sem, 16)
                sp.dma_start(eb1[:, :, :], eb1_in).then_inc(c_loaded.sem, 16)
                sp.dma_start(eb2[:, :], eb2_in).then_inc(c_loaded.sem, 16)
                with sp.Fori(0, NBLK) as it:
                    sp.wait_ge(block_done.sem, it + 1)
                    sp.dma_start(xt[:, :, :], x[bass.ds(it * TB, TB)].rearrange("t p d -> p t d")).then_inc(x_in.sem, 16)
                    sp.dma_start(ctx[:, :, :], ctx_in[bass.ds(it * SB, SB)].rearrange("b c d -> c b d")).then_inc(ctx_in_.sem, 16)

            NLOAD = 5 + len(MATS) + 3

            @block.gpsimd
            def _(pool):
                pool.memset(ones[:, :], 1.0).then_inc(pool_consts.sem, 1)
                pool.memset(eps_t[:, :], -0.5).then_inc(pool_consts.sem, 1)
                pool.wait_ge(pool_consts.sem, 2)
                with pool.Fori(0, NBLK) as it:
                    for n in range(5):
                        pool.wait_ge(ln_ve.sem, ln_ve.at(it, n + 1))
                        pool.tensor_tensor(rstd[:, :], ve[:, :], eps_t[:, :], ALU.pow).then_inc(ln_rstd.sem, 1)

            @block.scalar
            def _(act):
                act.wait_ge(c_loaded.sem, 16 * NLOAD)
                act.wait_ge(consts.sem, 7)
                with act.Fori(0, NBLK) as it:
                    def to_hT(n, scale, shift, bank):
                        act.wait_ge(hT_ps.sem, hT_ps.at(it, n + 1))
                        for kc in range(KC):
                            act.activation(hT[:, kc, :], ps[:, bank + kc, :], ACT.Identity, bias=col[shift](kc),
                                           scale=col[scale](kc)).then_inc(hT_sb.sem, 1)

                    def feature_softmax(n):
                        act.wait_ge(lg_nm.sem, lg_nm.at(it, n + 1))
                        for t in range(TB):
                            act.activation(pt[:, t, :], lg[:, t, :], ACT.Exp, bias=nm[:, t:t + 1], scale=D ** -0.5,
                                           accum_out=sm[:, t:t + 1]).then_inc(p_sb.sem, 1)

                    to_hT(0, "gamma", "beta", 0)
                    for mc in range(KC):
                        act.wait_ge(q_ps.sem, (it * 2) * KC + mc + 1)
                        act.activation(qT[:, mc, :], ps[:, 2 + mc, :], ACT.Identity, bias=col["bq"](mc)).then_inc(qT_sb.sem, 1)
                    feature_softmax(0)
                    feature_softmax(1)
                    act.wait_ge(cT_ps.sem, cT_ps.at(it))
                    act.activation(cT[:, :, :], ps[:, 4, 0:KC * SB * C].rearrange("p (k c) -> p k c", k=KC), ACT.Copy).then_inc(cT_sb.sem, 1)
                    act.wait_ge(x1T_ps.sem, x1T_ps.at(it))
                    act.activation(x1T[:, :, :], ps[:, 2:4, :], ACT.Copy).then_inc(x1T_sb.sem, 1)
                    act.wait_ge(sim_nm.sem, sim_nm.at(it))
                    for t in range(TB):
                        act.activation(pt[:, t, 0:C], ps[:, 5, t * P:t * P + C], ACT.Exp, bias=nm[:, t:t + 1],
                                       accum_out=sm[:, t:t + 1]).then_inc(bp_sb.sem, 1)
                    act.wait_ge(AT_ps.sem, AT_ps.at(it))
                    act.activation(AT[:, :], ps[0:C, 6, :], ACT.Copy).then_inc(AT_sb.sem, 1)
                    act.wait_ge(bd_sb.sem, bd_sb.at(it))
                    act.activation(be[:, :], bd[:, :], ACT.Exp).then_inc(be_sb.sem, 1)
                    act.wait_ge(hq_ps.sem, hq_ps.at(it))
                    act.activation(qT[:, :, :], ps[:, 0:2, :], ACT.Copy).then_inc(hqT_sb.sem, 1)
                    to_hT(1, "g1", "b1", 0)
                    for mc in range(KC):
                        act.wait_ge(q_ps.sem, (it * 2 + 1) * KC + mc + 1)
                        for eo in range(2):
                            act.activation(qz[:, eo, mc, :], ps[:, 2 + mc, :], ACT.Identity, bias=qbias[:, eo, mc:mc + 1],
                                           scale=qscale[:, eo, mc:mc + 1]).then_inc(qz_sb.sem, 1)
                    for s in range(2 * TB):
                        t, kc = s // 2, s % 2
                        L = P * (t % 2 + 1)
                        act.wait_ge(s_nm.sem, s_nm.at(it, s + 1))
                        if s >= 2:
                            act.wait_ge(pT_ps.sem, pT_ps.at(it, chunks_before(s - 1)))
                        for h in range(8):
                            ins = act.activation(p8[:, s % 2, h, 0:L], ps[:, h // 2, (h % 2) * L:(h % 2 + 1) * L], ACT.Exp,
                                                 bias=nm8[:, s % 2, h:h + 1], accum_out=sm16[:, t, kc * 8 + h:kc * 8 + h + 1])
                        ins.then_inc(s_p.sem, 1)
                    act.wait_ge(oT_ps.sem, oT_ps.at(it))
                    act.activation(qT[:, :, :], ps[:, 0:2, :], ACT.Copy).then_inc(oT_sb.sem, 1)
                    to_hT(2, "g2", "b2", 4)
                    act.wait_ge(rl_nm.sem, rl_nm.at(it))
                    for t in range(TB):
                        act.activation(rex[:, t, :], rl[:, t, :], ACT.Exp, bias=nm[:, t:t + 1]).then_inc(rl_exp.sem, 1)
                    act.wait_ge(wT_ps.sem, wT_ps.at(it))
                    act.activation(wT[:, :], ps[0:E, 7, :], ACT.Copy).then_inc(wT_sb.sem, 1)

            @block.vector
            def _(dve):
                dve.memset(sm[:, :], 0.0).then_inc(block_done.sem, 1)
                dve.wait_ge(c_loaded.sem, 16 * NLOAD)
                dve.tensor_copy(identb[:, :], ident[:, :]).then_inc(consts.sem, 1)
                for eo, n in enumerate(("even", "odd")):
                    i = COLS.index(n)
                    dve.tensor_scalar(qscale[:, eo, :], cols[:, i, :], HD ** -0.5, None, ALU.mult).then_inc(consts.sem, 1)
                dve.wait_ge(consts.sem, 3)
                for eo in range(2):
                    for kc in range(KC):
                        dve.tensor_tensor(qbias[:, eo, kc:kc + 1], qscale[:, eo, kc:kc + 1], col["fbq"](kc), ALU.mult).then_inc(consts.sem, 1)
                with dve.Fori(0, NBLK) as it:
                    def feature_logits(n, bias):
                        for t in range(TB):
                            if t % 2 == 0:
                                wait_apart(dve, lg_ps.sem, lg_ps.at(it, n * TB + t + 2))
                            dve.tensor_tensor_reduce(lg[:, t, :], tile_of(2, t), row[bias], 1.0, -3.0e38, ALU.add, ALU.max,
                                                     mx[:, t:t + 1]).then_inc(lg_sb.sem, 1)
                        dve.wait_ge(lg_sb.sem, lg_sb.at(it, n * TB + TB))
                        dve.tensor_scalar(nm[:, :], mx[:, :], -(D ** -0.5), None, ALU.mult).then_inc(lg_nm.sem, 1)

                    def feature_weight(n, bank):
                        dve.wait_ge(p_sb.sem, p_sb.at(it, n * TB + TB))
                        dve.reciprocal(rs[:, :], sm[:, :]).then_inc(p_rs.sem, 1)
                        dve.wait_ge(p_rs.sem, p_rs.at(it, n + 1))
                        for t in range(TB):
                            dve.scalar_tensor_tensor(wt[:, t, :], pt[:, t, :], rs[:, t:t + 1], tile_of(bank, t),
                                                     ALU.mult, ALU.mult).then_inc(w_sb.sem, 1)

                    dve.wait_ge(x_in.sem, x_in.at(it))
                    stats(dve, it, 0, xt)
                    normalize(dve, it, 0, xt, hn)
                    for mc in range(KC):
                        dve.wait_ge(k_ps.sem, it * 2 * KC + mc + 1)
                        dve.tensor_scalar(kT[:, mc, :], ps[:, 4 + mc, :], col["bk"](mc), None, ALU.add).then_inc(kT_sb.sem, 1)
                    dve.wait_ge(v_ps.sem, v_ps.at(it, 1))
                    dve.tensor_tensor(vt[:, :, :], pair(6), over_tiles(row["bv"]), ALU.add).then_inc(v_sb.sem, 1)
                    feature_logits(0, "bqa")
                    dve.wait_ge(tok_ps.sem, tok_ps.at(it, 1))
                    feature_weight(0, 0)
                    for mc in range(KC):
                        dve.wait_ge(pool_ps.sem, pool_ps.at(it, mc + 1))
                        dve.tensor_tensor(hT[:, mc, :], ps[:, 4 + mc, :], kT[:, mc, :], ALU.mult).then_inc(mT_sb.sem, 1)
                    feature_logits(1, "bka")
                    dve.wait_ge(tok_ps.sem, tok_ps.at(it, 2))
                    feature_weight(1, 6)
                    dve.wait_ge(pk_ps.sem, pk_ps.at(it))
                    dve.tensor_tensor(lg[:, :, :], pair(0), vt[:, :, :], ALU.mult).then_inc(a_mul.sem, 1)
                    dve.wait_ge(a_mul.sem, a_mul.at(it))
                    dve.tensor_tensor(hn[:, :, :], lg[:, :, :], xt[:, :, :], ALU.add).then_inc(a_sum.sem, 1)
                    dve.wait_ge(a_sum.sem, a_sum.at(it))
                    stats(dve, it, 1, hn)
                    normalize(dve, it, 1, hn, x1)
                    dve.wait_ge(x1T_sb.sem, x1T_sb.at(it))
                    for kc in range(KC):
                        dve.tensor_scalar(hT[:, kc, :], x1T[:, kc, :], col["w3"](kc), col["w2"](kc), ALU.mult, ALU.add).then_inc(xwT_sb.sem, 1)
                    dve.wait_ge(sim_ps.sem, sim_ps.at(it))
                    sim = ps[:, 5, :].rearrange("p (t c) -> p t c", t=TB)
                    dve.tensor_reduce(mx[:, :], sim[:, :, 0:C], AX.X, ALU.max).then_inc(sim_mx.sem, 1)
                    dve.wait_ge(sim_mx.sem, sim_mx.at(it))
                    dve.tensor_scalar(nm[:, :], mx[:, :], -1.0, None, ALU.mult).then_inc(sim_nm.sem, 1)
                    dve.scalar_tensor_tensor(bm[:, :], mx[:, :], row["bs"], sim[:, :, C], ALU.add, ALU.add).then_inc(sim_nm.sem, 1)
                    dve.wait_ge(bp_sb.sem, bp_sb.at(it))
                    dve.reciprocal(rs[:, :], sm[:, :]).then_inc(bp_rs.sem, 1)
                    dve.wait_ge(bp_rs.sem, bp_rs.at(it))
                    for t in range(TB):
                        dve.tensor_scalar(wt[:, t, 0:C], pt[:, t, 0:C], rs[:, t:t + 1], None, ALU.mult).then_inc(A_sb.sem, 1)
                    dve.wait_ge(mrow_ps.sem, mrow_ps.at(it))
                    dve.tensor_reduce(bg[:, :], ps[0:1, 7, :].rearrange("p (b s) -> p b s", b=SB), AX.X, ALU.max).then_inc(g_sb.sem, 1)
                    dve.wait_ge(g_ps.sem, g_ps.at(it))
                    for b in range(SB):
                        dve.tensor_scalar(bd[:, 2 * b:2 * b + 2], bm[:, 2 * b:2 * b + 2], ps[:, 4, b:b + 1], None,
                                          ALU.subtract).then_inc(bd_sb.sem, 1)
                    dve.wait_ge(hqT_sb.sem, hqT_sb.at(it))
                    dve.tensor_tensor(kT[:, :, :], qT[:, :, :], x1T[:, :, :], ALU.mult).then_inc(xhT_sb.sem, 1)
                    dve.wait_ge(hc_ps.sem, hc_ps.at(it))
                    dve.reciprocal(hcr[:, :], ps[:, 7, 0:3 * SB].rearrange("p (b j) -> p b j", j=3)[:, :, 2]).then_inc(hc_rs.sem, 1)
                    dve.wait_ge(hc_rs.sem, hc_rs.at(it))
                    for b in range(SB):
                        dve.tensor_scalar(hc[:, b, :], ps[:, 7, 3 * b:3 * b + KC], hcr[:, b:b + 1], None, ALU.mult).then_inc(hc_sb.sem, 1)
                    dve.wait_ge(hc_sb.sem, hc_sb.at(it))
                    for b in range(SB):
                        for kc in range(KC):
                            dve.scalar_tensor_tensor(Wx[:, b, kc, :], W["Wf3"][:, kc, :], hc[:, b, kc:kc + 1], W["Wf0"][:, kc, :],
                                                     ALU.mult, ALU.add).then_inc(Wx_sb.sem, 1)
                    dve.wait_ge(hcq_ps.sem, hcq_ps.at(it))
                    dve.tensor_tensor(hn[:, :, :], pair(2), over_tiles(row["bqv"]), ALU.add).then_inc(b_bias.sem, 1)
                    dve.wait_ge(b_bias.sem, b_bias.at(it))
                    dve.tensor_tensor(hn[:, :, :], hn[:, :, :], x1[:, :, :], ALU.add).then_inc(b_sum.sem, 1)
                    dve.wait_ge(b_sum.sem, b_sum.at(it))
                    stats(dve, it, 2, hn)
                    normalize(dve, it, 2, hn, x2)
                    dve.wait_ge(ln_out.sem, it * 5 * TB + 3 * TB)
                    stats(dve, it, 3, x2)
                    normalize(dve, it, 3, x2, hn)
                    for mc in range(KC):
                        dve.wait_ge(k_ps.sem, (it * 2 + 1) * KC + mc + 1)
                        dve.tensor_scalar(kT[:, mc, :], ps[:, 4 + mc, :], col["fbk"](mc), None, ALU.add).then_inc(kT_sb.sem, 1)
                    dve.wait_ge(v_ps.sem, v_ps.at(it, 2))
                    dve.tensor_tensor(vt[:, :, :], pair(6), over_tiles(row["fbv"]), ALU.add).then_inc(v_sb.sem, 1)

                    def evacuate(s):
                        for n in range(chunks_before(s), chunks_before(s + 1)):
                            dve.wait_ge(pT_ps.sem, pT_ps.at(it, n + 1))
                            if n >= 3:
                                dve.wait_ge(pT_used.sem, pT_used.at(it, n - 2))
                            dve.tensor_copy(PT[:, n % 3, :], ps[:, 4 + n % 2, :]).then_inc(pT_sb.sem, 1)

                    def head_out(t):
                        dve.wait_ge(pT_used.sem, pT_used.at(it, chunks_before(2 * t + 2)))
                        dve.reciprocal(rs16[:, :], sm16[:, t, :]).then_inc(o_rs.sem, 1)
                        dve.wait_ge(o_rs.sem, o_rs.at(it, t + 1))
                        o = ps[:, 6 + t % 2, 0:D].rearrange("p (h d) -> p h d", h=H)
                        dve.tensor_tensor(wt[:, t, :].rearrange("p (h d) -> p h d", h=H), o,
                                          rs16[:, :].rearrange("p (h o) -> p h o", o=1).to_broadcast([P, H, HD]),
                                          ALU.mult).then_inc(o_sb.sem, 1)

                    for s in range(2 * TB):
                        L = P * ((s // 2) % 2 + 1)
                        dve.wait_ge(s_ps.sem, s_ps.at(it, s + 1))
                        dve.tensor_reduce(mx8[:, :], ps[:, 0:4, 0:2 * L].rearrange("p r (e k) -> p r e k", e=2), AX.X, ALU.max).then_inc(s_mx.sem, 1)
                        dve.wait_ge(s_mx.sem, s_mx.at(it, s + 1))
                        dve.tensor_scalar(nm8[:, s % 2, :], mx8[:, :], -1.0, None, ALU.mult).then_inc(s_nm.sem, 1)
                        if s >= 1:
                            evacuate(s - 1)
                        if s >= 3 and s % 2:
                            head_out(s // 2 - 1)
                    evacuate(2 * TB - 1)
                    head_out(TB - 1)
                    dve.wait_ge(ao_ps.sem, ao_ps.at(it))
                    dve.tensor_tensor(x1[:, :, :], pair(2), over_tiles(row["bo"]), ALU.add).then_inc(c_bias.sem, 1)
                    dve.wait_ge(c_bias.sem, c_bias.at(it))
                    dve.tensor_tensor(x1[:, :, :], x1[:, :, :], x2[:, :, :], ALU.add).then_inc(c_sum.sem, 1)
                    dve.wait_ge(c_sum.sem, c_sum.at(it))
                    stats(dve, it, 4, x1)
                    normalize(dve, it, 4, x1, hn)
                    dve.tensor_tensor(x2[:, :, :], x1[:, :, :], x2[:, :, :], ALU.add).then_inc(acc_xa.sem, 1)
                    dve.wait_ge(hT_sb.sem, hT_sb.at(it))
                    tokens = bass.ds(it * BLK, BLK)
                    dve.tensor_copy(h2hi[:, :, tokens], hT[:, :, :]).then_inc(h2_split.sem, 1)
                    dve.wait_ge(h2_split.sem, h2_split.at(it, 1))
                    dve.tensor_tensor(h2lo[:, :, tokens], hT[:, :, :], h2hi[:, :, tokens].bitcast(F32), ALU.subtract).then_inc(h2_split.sem, 1)
                    dve.wait_ge(rl_ps.sem, rl_ps.at(it))
                    dve.tensor_tensor(rl[:, :, :], ps[:, 6, 0:TB * E].rearrange("p (t e) -> p t e", t=TB), over_tiles(row["br"]), ALU.add).then_inc(rl_sb.sem, 1)
                    wait_apart(dve, rl_sb.sem, rl_sb.at(it))
                    for t in range(TB):
                        dve.max(rt8[:, t, :], rl[:, t, :]).then_inc(rl_max.sem, 1)
                    dve.wait_ge(rl_max.sem, rl_max.at(it))
                    dve.tensor_scalar(nm[:, :], rt8[:, :, 0], -1.0, None, ALU.mult).then_inc(rl_nm.sem, 1)
                    dve.wait_ge(rl_exp.sem, rl_exp.at(it))
                    for t in range(TB):
                        dve.scalar_tensor_tensor(rw[:, t, :], rl[:, t, :], rt8[:, t, 1:2], rex[:, t, :], ALU.is_ge, ALU.mult,
                                                 accum_out=sm[:, t:t + 1]).then_inc(rl_w.sem, 1)
                    dve.wait_ge(rl_w.sem, rl_w.at(it))
                    dve.reciprocal(rs[:, :], sm[:, :]).then_inc(rl_rs.sem, 1)
                    dve.wait_ge(rl_rs.sem, rl_rs.at(it))
                    dve.tensor_tensor(rw[:, :, :], rw[:, :, :], rs[:, :].rearrange("p (t o) -> p t o", o=1).to_broadcast([P, TB, E]),
                                      ALU.mult).then_inc(rl_out.sem, 1)
                    dve.wait_ge(rl_out.sem, rl_out.at(it))
                    dve.tensor_copy(wts[:, bass.ds(it * TB, TB), :], rw[:, :, :])
                    dve.wait_ge(acc_xa.sem, acc_xa.at(it))
                    dve.wait_ge(mb_ps.sem, mb_ps.at(it))
                    dve.tensor_tensor(acc[:, bass.ds(it * TB, TB), :], pair(2), x2[:, :, :], ALU.add).then_inc(block_done.sem, 1)

            @block.tensor
            def _(pe):
                pe.wait_ge(c_loaded.sem, 16 * NLOAD)
                pe.wait_ge(consts.sem, 7)
                pe.wait_ge(pool_consts.sem, 2)
                with pe.Fori(0, NBLK) as it:
                    def to_features(src, bank, last):
                        for t in range(TB):
                            for kc in range(KC):
                                ins = pe.transpose(ps[:, bank + kc, t * P:(t + 1) * P], src[:, t, kc * P:(kc + 1) * P], ident[:, :])
                        ins.then_inc(last.sem, 1)

                    def to_tokens(src, bank, last):
                        for t in range(TB):
                            for kc in range(KC):
                                ins = pe.transpose(tile_of(bank, t)[:, kc * P:(kc + 1) * P], src[:, kc, t * P:(t + 1) * P], ident[:, :])
                        ins.then_inc(last.sem, 1)

                    def weight_rows(w, src, bank, done):
                        for mc in range(KC):
                            for kc in range(KC):
                                ins = pe.matmul(ps[:, bank + mc, :], w[:, kc, mc * P:(mc + 1) * P], src[:, kc, :],
                                                start=(kc == 0), stop=(kc == KC - 1))
                            ins.then_inc(done.sem, 1)

                    def token_rows(terms, bank, t):
                        n = len(terms) * KC
                        for i, (src, w) in enumerate(terms):
                            for kc in range(KC):
                                j = i * KC + kc
                                ins = pe.matmul(tile_of(bank, t), src[:, kc, t * P:(t + 1) * P], w[:, kc, :],
                                                start=(j == 0), stop=(j == n - 1))
                        return ins

                    pe.wait_ge(ln_out.sem, it * 5 * TB + TB)
                    pe.wait_ge(block_done.sem, it + 1)
                    to_features(hn, 0, hT_ps)
                    pe.wait_ge(hT_sb.sem, hT_sb.at(it, KC))
                    weight_rows(W["Wq"], hT, 2, q_ps)
                    weight_rows(W["Wk"], hT, 4, k_ps)
                    for t in range(TB):
                        ins = token_rows([(hT, W["Wv"])], 6, t)
                    ins.then_inc(v_ps.sem, 1)
                    pe.wait_ge(qT_sb.sem, qT_sb.at(it))
                    to_tokens(qT, 0, tok_ps)
                    for t in range(TB):
                        token_rows([(qT, W["Wqa"])], 2, t).then_inc(lg_ps.sem, 1)
                    pe.wait_ge(w_sb.sem, w_sb.at(it, TB))
                    pe.wait_ge(kT_sb.sem, kT_sb.at(it, KC))
                    for mc in range(KC):
                        for b in range(SB):
                            o = ps[:, 4 + mc, b * S:(b + 1) * S]
                            pe.matmul(o, wt[:, 2 * b, mc * P:(mc + 1) * P], tri[:, 0:2, :].rearrange("p a q -> p (a q)"),
                                      start=True, stop=False, skip_group_check=True)
                            ins = pe.matmul(o[:, P:S], wt[:, 2 * b + 1, mc * P:(mc + 1) * P], tri[:, 2, :],
                                            start=False, stop=True, skip_group_check=True)
                        ins.then_inc(pool_ps.sem, 1)
                    pe.wait_ge(mT_sb.sem, mT_sb.at(it))
                    pe.wait_ge(v_sb.sem, v_sb.at(it, 1))
                    to_tokens(hT, 6, tok_ps)
                    for t in range(TB):
                        token_rows([(hT, W["Wka"])], 2, t).then_inc(lg_ps.sem, 1)
                    pe.wait_ge(w_sb.sem, w_sb.at(it))
                    for t in range(TB):
                        o = tile_of(0, t)
                        if t % 2 == 0:
                            ins = pe.matmul(o, tri[:, 0, :], wt[:, t, :], start=True, stop=True)
                        else:
                            pe.matmul(o, tri[:, 1, :], wt[:, t - 1, :], start=True, stop=False)
                            ins = pe.matmul(o, tri[:, 2, :], wt[:, t, :], start=False, stop=True)
                    ins.then_inc(pk_ps.sem, 1)
                    pe.wait_ge(ctx_in_.sem, ctx_in_.at(it))
                    for b in range(SB):
                        for kc in range(KC):
                            o = ps[:, 4, kc * SB * C + b * C:kc * SB * C + (b + 1) * C]
                            ins = pe.transpose(o, ctx[:, b, kc * P:(kc + 1) * P], ident[0:C, 0:C])
                    ins.then_inc(cT_ps.sem, 1)
                    pe.wait_ge(ln_out.sem, it * 5 * TB + 2 * TB)
                    to_features(x1, 2, x1T_ps)
                    pe.wait_ge(xwT_sb.sem, xwT_sb.at(it))
                    pe.wait_ge(cT_sb.sem, cT_sb.at(it))
                    pe.wait_ge(x1T_sb.sem, x1T_sb.at(it))
                    for t in range(TB):
                        tok = slice(t * P, (t + 1) * P)
                        for kc in range(KC):
                            pe.matmul(ps[:, 5, t * P:t * P + C], hT[:, kc, tok], cT[:, kc, (t // 2) * C:(t // 2 + 1) * C],
                                      start=(kc == 0), stop=(kc == KC - 1))
                        for kc in range(KC):
                            ins = pe.matmul(ps[:, 5, t * P + C:t * P + C + 1], x1T[:, kc, tok], col["w1"](kc),
                                            start=(kc == 0), stop=(kc == KC - 1))
                    ins.then_inc(sim_ps.sem, 1)
                    pe.wait_ge(sim_nm.sem, sim_nm.at(it))
                    for t in range(TB):
                        ins = pe.matmul(ps[0:1, 7, t * P:(t + 1) * P], bm[:, t:t + 1], ident[:, :], start=True, stop=True)
                    ins.then_inc(mrow_ps.sem, 1)
                    pe.wait_ge(A_sb.sem, A_sb.at(it))
                    for t in range(TB):
                        ins = pe.transpose(ps[0:C, 6, t * P:(t + 1) * P], wt[:, t, 0:C], ident[:, :])
                    ins.then_inc(AT_ps.sem, 1)
                    pe.wait_ge(g_sb.sem, g_sb.at(it))
                    pe.matmul(ps[:, 4, 0:SB], ones[0:1, :], bg[:, :], start=True, stop=True).then_inc(g_ps.sem, 1)
                    pe.wait_ge(AT_sb.sem, AT_sb.at(it))
                    for mc in range(KC):
                        for b in range(SB):
                            ins = pe.matmul(ps[:, mc, b * S:(b + 1) * S], ctx[:, b, mc * P:(mc + 1) * P], AT[:, b * S:(b + 1) * S],
                                            start=True, stop=True)
                    ins.then_inc(hq_ps.sem, 1)
                    pe.wait_ge(be_sb.sem, be_sb.at(it))
                    for b in range(SB):
                        for j in range(KC + 1):
                            for i in range(2):
                                t = 2 * b + i
                                lhs = x1[:, t, j * P:(j + 1) * P] if j < KC else ones[:, :]
                                ins = pe.matmul(ps[:, 7, 3 * b + j:3 * b + j + 1], lhs, be[:, t:t + 1], start=(i == 0), stop=(i == 1))
                    ins.then_inc(hc_ps.sem, 1)
                    pe.wait_ge(hqT_sb.sem, hqT_sb.at(it))
                    pe.wait_ge(xhT_sb.sem, xhT_sb.at(it))
                    pe.wait_ge(Wx_sb.sem, Wx_sb.at(it))
                    for t in range(TB):
                        ins = token_rows([(x1T, Wx[:, t // 2]), (qT, W["Wf1"]), (kT, W["Wf2"])], 2, t)
                    ins.then_inc(hcq_ps.sem, 1)
                    pe.wait_ge(ln_out.sem, it * 5 * TB + 4 * TB)
                    to_features(hn, 0, hT_ps)
                    pe.wait_ge(hT_sb.sem, hT_sb.at(it, 2 * KC))
                    weight_rows(W["fWq"], hT, 2, q_ps)
                    weight_rows(W["fWk"], hT, 4, k_ps)
                    for t in range(TB):
                        ins = token_rows([(hT, W["fWv"])], 6, t)
                    ins.then_inc(v_ps.sem, 1)
                    pe.wait_ge(qz_sb.sem, qz_sb.at(it))
                    pe.wait_ge(kT_sb.sem, kT_sb.at(it))
                    pe.wait_ge(v_sb.sem, v_sb.at(it))

                    def scores(s):
                        t, kc = s // 2, s % 2
                        b, L = t // 2, P * (t % 2 + 1)
                        if s:
                            pe.wait_ge(s_p.sem, s_p.at(it, s))
                        for r in range(4):
                            m = mask[:, :, S - L:S]
                            pe.matmul(ps[:, r, 0:2 * L].rearrange("p (e k) -> p e k", e=2), identb[:, :], m,
                                      start=True, stop=False, skip_group_check=True)
                        for eo in range(2):
                            for r in range(4):
                                g = slice(32 * r, 32 * r + 32)
                                ins = pe.matmul(ps[:, r, eo * L:(eo + 1) * L], qz[g, eo, kc, t * P:(t + 1) * P],
                                                kT[g, kc, b * S:b * S + L], start=False, stop=True, skip_group_check=True)
                        ins.then_inc(s_ps.sem, 1)

                    def turn(s, n):
                        t = s // 2
                        nb = t % 2 + 1
                        c = n - chunks_before(s)
                        if n >= 2:
                            pe.wait_ge(pT_sb.sem, pT_sb.at(it, n - 1))
                        for i in range(4):
                            h, kb = c * 4 // nb + i // nb, i % nb
                            ins = pe.transpose(ps[:, 4 + n % 2, i * P:(i + 1) * P], p8[:, s % 2, h, kb * P:(kb + 1) * P], ident[:, :])
                        ins.then_inc(pT_ps.sem, 1)

                    def weigh(s, n):
                        t, kc = s // 2, s % 2
                        nb = t % 2 + 1
                        c = n - chunks_before(s)
                        pe.wait_ge(pT_sb.sem, pT_sb.at(it, n + 1))
                        for i in range(4):
                            h, kb = kc * 8 + c * 4 // nb + i // nb, i % nb
                            ins = pe.matmul(ps[:, 6 + t % 2, h * HD:(h + 1) * HD], PT[:, n % 3, i * P:(i + 1) * P],
                                            vt[:, 2 * (t // 2) + kb, h * HD:(h + 1) * HD], start=(kb == 0), stop=(kb == nb - 1))
                        ins.then_inc(pT_used.sem, 1)

                    def attend(s):
                        if s % 2 == 0 and s >= 4:
                            pe.wait_ge(o_sb.sem, o_sb.at(it, s // 2 - 1))
                        a, z = chunks_before(s), chunks_before(s + 1)
                        for n in range(a, z):
                            turn(s, n)
                            if n > a:
                                weigh(s, n - 1)
                        weigh(s, z - 1)

                    for s in range(2 * TB):
                        scores(s)
                        if s:
                            attend(s - 1)
                    pe.wait_ge(s_p.sem, s_p.at(it))
                    attend(2 * TB - 1)
                    pe.wait_ge(o_sb.sem, o_sb.at(it))
                    to_features(wt, 0, oT_ps)
                    pe.wait_ge(oT_sb.sem, oT_sb.at(it))
                    for t in range(TB):
                        ins = token_rows([(qT, W["fWo"])], 2, t)
                    ins.then_inc(ao_ps.sem, 1)
                    pe.wait_ge(ln_out.sem, ln_out.at(it))
                    to_features(hn, 4, hT_ps)
                    pe.wait_ge(hT_sb.sem, hT_sb.at(it))
                    for t in range(TB):
                        for kc in range(KC):
                            ins = pe.matmul(ps[:, 6, t * E:(t + 1) * E], hT[:, kc, t * P:(t + 1) * P], wr[:, kc, :], start=(kc == 0), stop=(kc == KC - 1))
                    ins.then_inc(rl_ps.sem, 1)
                    pe.wait_ge(rl_out.sem, rl_out.at(it))
                    for t in range(TB):
                        ins = pe.matmul(ps[0:E, 7, t * P:(t + 1) * P], rw[:, t, :], ident[:, :], start=True, stop=True)
                    ins.then_inc(wT_ps.sem, 1)
                    pe.wait_ge(wT_sb.sem, wT_sb.at(it))
                    for t in range(TB):
                        ins = pe.matmul(tile_of(2, t), wT[:, t * P:(t + 1) * P], eb2[:, :], start=True, stop=True)
                    ins.then_inc(mb_ps.sem, 1)

        with ExitStack() as back:
            def bb(name, shape, dt=F32):
                return back.enter_context(nc.sbuf_tensor(name, shape, dt))

            def bsig(name, per=1):
                return Count(back.enter_context(nc.semaphore(name)), per)

            RING = 4
            raw1 = bb("raw_w1", [P, KC, F])
            raw2 = bb("raw_w2", [P, FT, D])
            w1h = bb("w1_hi", [P, KC, F], F32R)
            w1l = bb("w1_lo", [P, KC, F], F32R)
            w2h = bb("w2_hi", [P, FT, D], F32R)
            w2l = bb("w2_lo", [P, FT, D], F32R)
            mid = bb("mid", [P, RING, BLK])
            midh = bb("mid_hi", [P, RING, BLK], F32R)
            midl = bb("mid_lo", [P, RING, BLK], F32R)
            b1e = bb("b1_of_expert", [P, FT])
            ost = bb("out_st", [P, TB, 6])
            omv = bb("out_mv", [P, TB, 2])
            ove = bb("out_ve", [P, TB])
            ors = bb("out_rstd", [P, TB])
            ob = bb("out_buf", [P, 2, TB, D])

            w_in = bsig("w_in", 32)
            w_hi = bsig("w_hi", 2)
            w_lo = bsig("w_lo", 2)
            b1_set = bsig("b1_set")
            mid_ps = bsig("mid_ps", FT)
            mid_sb = bsig("mid_sb", FT)
            mid_hi = bsig("mid_hi", FT)
            mid_lo = bsig("mid_lo", FT)
            mid_used = bsig("mid_used", FT)
            eo_acc = bsig("eo_acc", TB)
            o_st = bsig("o_st", TB)
            o_mv = bsig("o_mv", TB)
            o_ve = bsig("o_ve")
            o_rstd = bsig("o_rstd")
            o_out = bsig("o_out", TB)
            stored = [bsig(f"stored_{j}", 16) for j in range(2)]
            block = back.enter_context(nc.Block())

            @block.sync
            def _(sp):
                for j in range(2):
                    sp.nop().then_inc(stored[j].sem, 16)
                with sp.Fori(0, E) as e:
                    sp.wait_ge(w_lo.sem, w_lo.at(e, 1))
                    sp.dma_start(raw1[:, :, :], w1_in[bass.ds(e, 1)].rearrange("o (k p) f -> p (o k) f", p=P)).then_inc(w_in.sem, 16)
                    sp.dma_start(raw2[:, :, :], w2_in[bass.ds(e, 1)].rearrange("o (f p) d -> p (o f) d", p=P)).then_inc(w_in.sem, 16)
                with sp.Fori(0, NBLK // 2) as i:
                    for j in range(2):
                        sp.wait_ge(o_out.sem, i * 2 * TB + (j + 1) * TB)
                        sp.dma_start(out[bass.ds(i * 2 * TB + j * TB, TB)].rearrange("t p d -> p t d"), ob[:, j]).then_inc(stored[j].sem, 16)
                for j in range(2):
                    sp.wait_ge(stored[j].sem, 16 * NBLK // 2 + 16)

            @block.gpsimd
            def _(pool):
                with pool.Fori(0, NBLK) as i:
                    pool.wait_ge(o_ve.sem, o_ve.at(i))
                    pool.tensor_tensor(ors[:, :], ove[:, :], eps_t[:, :], ALU.pow).then_inc(o_rstd.sem, 1)

            @block.scalar
            def _(act):
                with act.Fori(0, E) as e:
                    act.wait_ge(b1_set.sem, b1_set.at(e))
                    with act.Fori(0, NBLK) as it:
                        n = e * NBLK + it
                        for f in range(FT):
                            act.wait_ge(mid_ps.sem, mid_ps.at(n, f + 1))
                            act.wait_ge(mid_lo.sem, mid_lo.at(n, f + 1))
                            act.activation(mid[:, f % RING, :], ps[:, f % 2, :], ACT.Gelu, bias=b1e[:, f:f + 1]).then_inc(mid_sb.sem, 1)

            @block.vector
            def _(dve):
                dve.memset(ost[:, 0, :], 0.0).then_inc(w_lo.sem, 1)
                dve.memset(ost[:, 1, :], 0.0).then_inc(mid_lo.sem, RING)
                dve.memset(ost[:, 2, :], 0.0).then_inc(eo_acc.sem, TB)
                with dve.Fori(0, E) as e:
                    dve.wait_ge(w_in.sem, w_in.at(e))
                    dve.wait_ge(mid_used.sem, e * NBLK * FT + RING)
                    dve.tensor_copy(b1e[:, :], eb1[:, bass.ds(e, 1), :].rearrange("p o f -> p (o f)")).then_inc(b1_set.sem, 1)
                    dve.tensor_copy(w1h[:, :, :], raw1[:, :, :]).then_inc(w_hi.sem, 1)
                    dve.tensor_copy(w2h[:, :, :], raw2[:, :, :]).then_inc(w_hi.sem, 1)
                    dve.wait_ge(w_hi.sem, w_hi.at(e, 1))
                    dve.tensor_tensor(w1l[:, :, :], raw1[:, :, :], w1h[:, :, :].bitcast(F32), ALU.subtract).then_inc(w_lo.sem, 1)
                    dve.wait_ge(w_hi.sem, w_hi.at(e))
                    dve.tensor_tensor(w2l[:, :, :], raw2[:, :, :], w2h[:, :, :].bitcast(F32), ALU.subtract).then_inc(w_lo.sem, 1)
                    with dve.Fori(0, NBLK) as it:
                        n = e * NBLK + it
                        for f in range(FT):
                            dve.wait_ge(mid_sb.sem, mid_sb.at(n, f + 1))
                            dve.wait_ge(mid_used.sem, mid_used.at(n, f + 1))
                            dve.tensor_copy(midh[:, f % RING, :], mid[:, f % RING, :]).then_inc(mid_hi.sem, 1)
                            dve.wait_ge(mid_hi.sem, mid_hi.at(n, f + 1))
                            dve.tensor_tensor(midl[:, f % RING, :], mid[:, f % RING, :], midh[:, f % RING, :].bitcast(F32),
                                              ALU.subtract).then_inc(mid_lo.sem, 1)
                        dve.wait_ge(mid_used.sem, mid_used.at(n) + RING)
                        for t in range(TB):
                            a = acc[:, bass.ds(it * TB + t, 1), :].rearrange("p o d -> p (o d)")
                            w = wts[:, bass.ds(it * TB + t, 1), bass.ds(e, 1)].rearrange("p o d -> p (o d)")
                            dve.scalar_tensor_tensor(a, tile_of(2, t), w, a, ALU.mult, ALU.add).then_inc(eo_acc.sem, 1)
                dve.wait_ge(eo_acc.sem, TB * E * NBLK + TB)
                with dve.Fori(0, NBLK // 2) as i:
                    for j in range(2):
                        k = i * 2 + j
                        for t in range(TB):
                            a = acc[:, bass.ds(i * 2 * TB + j * TB + t, 1), :].rearrange("p o d -> p (o d)")
                            dve.bn_stats(ost[:, t, :], a).then_inc(o_st.sem, 1)
                        for t in range(TB):
                            wait_apart(dve, o_st.sem, o_st.at(k, t + 1))
                            dve.bn_aggr(omv[:, t, :], ost[:, t, :]).then_inc(o_mv.sem, 1)
                        dve.wait_ge(o_mv.sem, o_mv.at(k))
                        dve.tensor_scalar(ove[:, :], omv[:, :, 1], EPS, None, ALU.add).then_inc(o_ve.sem, 1)
                        dve.wait_ge(o_rstd.sem, o_rstd.at(k))
                        dve.wait_ge(stored[j].sem, stored[j].at(i))
                        for t in range(TB):
                            a = acc[:, bass.ds(i * 2 * TB + j * TB + t, 1), :].rearrange("p o d -> p (o d)")
                            dve.tensor_scalar(ob[:, j, t, :], a, omv[:, t, 0:1], ors[:, t:t + 1], ALU.subtract, ALU.mult).then_inc(o_out.sem, 1)

            @block.tensor
            def _(pe):
                pe.nop().then_inc(mid_used.sem, RING)
                with pe.Fori(0, E) as e:
                    wait_apart(pe, w_lo.sem, w_lo.at(e) + 1)
                    with pe.Fori(0, NBLK) as it:
                        n = e * NBLK + it
                        tokens = bass.ds(it * BLK, BLK)

                        def up(f):
                            if f >= 2:
                                pe.wait_ge(mid_sb.sem, mid_sb.at(n, f - 1))
                            fs = slice(f * P, (f + 1) * P)
                            terms = [(w, h) for w, h in ((w1h, h2hi), (w1l, h2hi), (w1h, h2lo))]
                            for i, (w, h) in enumerate(terms):
                                for kc in range(KC):
                                    ins = pe.matmul(ps[:, f % 2, :], w[:, kc, fs], h[:, kc, tokens],
                                                    start=(i == 0 and kc == 0), stop=(i == 2 and kc == KC - 1))
                            ins.then_inc(mid_ps.sem, 1)

                        def down(f):
                            pe.wait_ge(mid_lo.sem, mid_lo.at(n, f + 1) + RING)
                            if f == 0:
                                pe.wait_ge(eo_acc.sem, eo_acc.at(n))
                            for t in range(TB):
                                ts = slice(t * P, (t + 1) * P)
                                for i, (m, w) in enumerate(((midh, w2h), (midh, w2l), (midl, w2h))):
                                    ins = pe.matmul(tile_of(2, t), m[:, f % RING, ts], w[:, f, :],
                                                    start=(f == 0 and i == 0 and t % 2 == 0), stop=(f == FT - 1 and i == 2),
                                                    skip_group_check=True)
                            ins.then_inc(mid_used.sem, 1)

                        up(0)
                        up(1)
                        for f in range(FT):
                            if f + 2 < FT:
                                up(f + 2)
                            down(f)


def kernel(**inputs):
    import numpy as np
    import concourse.bacc as bacc
    from concourse import mybir as mb
    from concourse.bass_utils import run_bass_kernel_spmd as run

    g = {k: np.asarray(v) for k, v in inputs.items()}
    f32 = np.float32
    a, xa, ff = "L0_attn_", "L0_xattn_", "L0_ffn_"
    halves = np.arange(D) // HD % 2
    w_sim = g[xa + "w_sim"]
    vec = {
        "bq": g[a + "bq"], "bk": g[a + "bk"], "gamma": g[a + "gamma"], "beta": g[a + "beta"],
        "w1": w_sim[:D], "w2": w_sim[D:2 * D], "w3": w_sim[2 * D:],
        "g1": g[ff + "ln1_g"], "b1": g[ff + "ln1_b"], "g2": g[ff + "ln2_g"], "b2": g[ff + "ln2_b"],
        "fbq": g[ff + "bq"], "fbk": g[ff + "bk"],
        "even": (halves == 0).astype(f32), "odd": (halves == 1).astype(f32),
    }
    cols = np.stack([vec[n].reshape(KC, P) for n in COLS]).transpose(2, 0, 1)
    rvec = {"bv": g[a + "bv"], "bqa": g[a + "bqa"], "bka": g[a + "bka"], "bqv": g[xa + "b_qv"],
            "fbv": g[ff + "bv"], "bo": g[ff + "bo"], "br": g[ff + "br"], "bs": g[xa + "b_sim"]}
    rows = np.broadcast_to(np.concatenate([rvec[n] for n in ROWS]), (P, sum(ROWS.values())))
    Wf = g[xa + "W_qv"]
    mat = {"Wq": g[a + "Wq"], "Wqa": g[a + "Wqa"], "Wk": g[a + "Wk"], "Wka": g[a + "Wka"], "Wv": g[a + "Wv"],
           "fWq": g[ff + "Wq"], "fWk": g[ff + "Wk"], "fWv": g[ff + "Wv"], "fWo": g[ff + "Wo"]}
    for i in range(4):
        mat[f"Wf{i}"] = Wf[i * D:(i + 1) * D]
    mats = np.stack([mat[n] for n in MATS])
    ident = np.eye(P, dtype=f32)
    t = np.arange(P)
    le = t[:, None] <= t[None, :]
    tri = np.stack([le / (t + 1.0), np.ones((P, P)) / (t + P + 1.0), le / (t + P + 1.0)], 1).astype(f32)
    mask = np.zeros((P, 2, S), np.dtype(mb.dt.np(mb.dt.bfloat16)))
    mask[:, :, P:] = np.where(t[None, :] > t[:, None], -1e30, 0.0)[:, None, :]
    arrays = {
        "x": g["x"].reshape(NT, P, D), "ctx": g["ctx_1024"], "mats": mats, "cols": cols, "rows": rows,
        "wr": g[ff + "Wr"], "ident": ident, "tri": tri, "mask": mask,
        "w1": g[ff + "e_w1"], "w2": g[ff + "e_w2"],
        "eb1": g[ff + "e_b1"].reshape(E, FT, P).transpose(2, 0, 1), "eb2": g[ff + "e_b2"],
    }
    arrays = {k: np.ascontiguousarray(v) for k, v in arrays.items()}
    nc = bacc.Bacc("TRN2", target_bir_lowering=False, num_devices=1)
    args = [nc.dram_tensor(k, v.shape, mb.dt.from_np(v.dtype), kind="ExternalInput").ap() for k, v in arrays.items()]
    args.append(nc.dram_tensor("out", (NT, P, D), F32, kind="ExternalOutput").ap())
    decoder_kernel(nc, *args)
    r = run(nc, [arrays], core_ids=[0])
    return r.results[0]["out"].reshape(B, S, D)
```

```python
from contextlib import ExitStack

import concourse.bass as bass
from concourse import mybir

F32 = mybir.dt.float32
F32R = mybir.dt.float32r
I32 = mybir.dt.int32
BF16 = mybir.dt.bfloat16
ALU = mybir.AluOpType
ACT = mybir.ActivationFunctionType
AX = mybir.AxisListType

P = 128
B, S, D = 16, 256, 256
T = B * S
NT = T // P
TB = 4
BLK = TB * P
NBLK = T // BLK
SB = BLK // S
KC = D // P
C = 120
H, HD = 16, 16
E, F = 8, 1024
FT = F // P
EPS = 1e-5
TE = 256
PAD = TE
CAP = T
SPARE = TB * E * P

COLS = ["bq", "bk", "gamma", "beta", "w1", "w2", "w3", "g1", "b1", "g2", "b2", "fbq", "fbk", "even", "odd"]
ROWS = {"bv": D, "bqa": D, "bka": D, "bqv": D, "fbv": D, "bo": D, "br": E, "bs": 1}
MATS = ["Wq", "Wqa", "Wk", "Wka", "Wv", "Wf0", "Wf1", "Wf2", "Wf3", "fWq", "fWk", "fWv", "fWo"]


class Count:

    def __init__(self, sem, per):
        self.sem, self.per = sem, per

    def at(self, it, k=None):
        return it * self.per + (self.per if k is None else k)


class Woven:

    def __init__(self, *parts):
        self.steps = (step for part in parts for step in part)
        self.next = next(self.steps, None)

    def through(self, step):
        while self.next is not None and self.next <= step:
            self.next = next(self.steps, None)


def decoder_kernel(nc, x, ctx_in, mats_in, cols_in, rows_in, wr_in, ident_in, tri_in, mask_in, lower_in,
                   slots_in, ids_in, unused_in, zeros_in, w1_in, w2_in, eb1_in, eb2_in, out):
    with ExitStack() as stack:
        def sb(name, shape, dt=F32):
            return stack.enter_context(nc.sbuf_tensor(name, shape, dt))

        def signal(name, per=1):
            return Count(stack.enter_context(nc.semaphore(name)), per)

        ps = stack.enter_context(nc.psum_tensor("ps", [P, 8, 512], F32))

        def pair(bank):
            return ps[:, bank:bank + 2, :].rearrange("p b (t d) -> p (b t) d", t=2)

        def wait_apart(eng, *waits):
            waits = [(sem, value if isinstance(value, int) else eng.to_reg(value)) for sem, value in waits]
            eng.wait_ge(c_loaded.sem, 16)
            for sem, value in waits:
                eng.wait_ge(sem, value)

        def tile_of(bank, t):
            return ps[:, bank + t // 2, (t % 2) * D:(t % 2 + 1) * D]

        h_rows = nc.dram_tensor("h_rows", (T + PAD, D), F32, kind="Internal").ap()
        r_rows = nc.dram_tensor("r_rows", (T + PAD, D), F32, kind="Internal").ap()
        lists = nc.dram_tensor("lists", (E * CAP + SPARE, 2), I32, kind="Internal").ap()

        cols = sb("cols_sb", [P, len(COLS), KC])
        ident = sb("ident_sb", [P, P])
        raw = sb("raw_weights", [P, KC * F + FT * D])
        tiles = sb("tiles", [1, 2, E], I32)
        w_in = signal("w_in", 32)
        eb1 = sb("expert_b1", [P, E, FT])

        c_loaded = signal("consts_loaded", 16)
        eps_t = sb("eps_half", [P, TB])

        def load_expert(sp, e):
            sp.dma_start(raw[:, 0:KC * F].rearrange("p (k f) -> p k f", k=KC),
                         w1_in[bass.ds(e, 1)].rearrange("o (k p) f -> p (o k) f", p=P)).then_inc(w_in.sem, 16)
            sp.dma_start(raw[:, KC * F:].rearrange("p (f d) -> p f d", f=FT),
                         w2_in[bass.ds(e, 1)].rearrange("o (f p) d -> p (o f) d", p=P)).then_inc(w_in.sem, 16)

        with ExitStack() as front:
            def fb(name, shape, dt=F32):
                return front.enter_context(nc.sbuf_tensor(name, shape, dt))

            def fsig(name, per=1):
                return Count(front.enter_context(nc.semaphore(name)), per)

            mats = fb("mats_sb", [P, len(MATS), KC, D])
            rows = fb("rows_sb", [P, sum(ROWS.values())])
            wr = fb("wr_sb", [P, KC, E])
            identb = fb("identb", [P, P], BF16)
            tri = fb("tri_sb", [P, 3, P])
            mask = fb("mask_sb", [P, 2, S], BF16)
            eb2 = fb("expert_b2", [E, D])
            ones = fb("ones", [P, P])
            qscale = fb("qscale", [P, 2, KC])
            qbias = fb("qbias", [P, 2, KC])

            W = {n: mats[:, i] for i, n in enumerate(MATS)}
            col = {n: (lambda kc, i=i: cols[:, i, kc:kc + 1]) for i, n in enumerate(COLS)}
            row, at = {}, 0
            for n, w in ROWS.items():
                row[n] = rows[:, at:at + w]
                at += w

            def over_tiles(r, n=TB):
                w = r.shape[1]
                return r.rearrange("p (o d) -> p o d", o=1).to_broadcast([P, n, w])

            xt = fb("x_tok", [P, TB, D])
            lg = fb("logits", [P, TB, D])
            pt = fb("exp_logits", [P, TB, D])
            x1T = fb("x1T", [P, KC, BLK])
            Wx = fb("Wx", [P, SB, KC, D])
            x1 = fb("x1_tok", [P, TB, D])
            x1b = fb("x1_bias", [P, TB, D])
            ctx = fb("ctx_tok", [C, SB, D])
            hn = fb("hn_tok", [P, TB, D])
            hT = fb("hT", [P, KC, BLK])
            qT = fb("qT", [P, KC, BLK])
            kT = fb("kT", [P, KC, BLK])
            vt = fb("v_tok", [P, TB, D])
            wt = fb("w_tok", [P, TB, D])
            x2 = fb("x2_tok", [P, TB, D])
            AT = fb("AT", [C, BLK])
            cT = fb("cT", [P, KC, SB * C])
            mx = fb("max4", [P, TB])
            nm = fb("negmax4", [P, TB])
            sm = fb("sum4", [P, TB])
            rs = fb("rsum4", [P, TB])
            bm = fb("b_rowmax", [P, TB])
            bg = fb("b_seqmax", [1, SB])
            bd = fb("b_diff", [P, TB])
            be = fb("b_exp", [P, TB])
            hcr = fb("hc_recip", [P, SB])
            hc = fb("hc", [P, SB, KC])
            qz = fb("q_even_odd", [P, 2, KC, BLK])
            skT = fb("self_kT", [P, KC, BLK])
            sv = fb("self_v", [P, TB, D])
            p4 = fb("exp_scores", [P, 2, 4, S])
            PT = fb("PT", [P, 3, 512])
            ot = fb("o_tok", [P, TB, D])
            nm4 = fb("negmax_heads", [P, 2, 4])
            mx4 = fb("max_heads", [P, 2, 4])
            sm16 = fb("sum16", [P, TB, H])
            rs16 = fb("rsum16", [P, H])
            xb = fb("x2_bias", [P, TB, D])
            xr = fb("x2_kept", [P, TB, D])
            oT = fb("oT", [P, KC, BLK])
            at_ = fb("a_tok", [P, TB, D])
            h2n = fb("h2n_tok", [P, TB, D])
            h2T = fb("h2T", [P, KC, BLK])
            xa = fb("x2_plus_a", [P, TB, D])
            rt_ = fb("r_tok_f", [P, TB, D])
            rl = fb("router_logits", [P, TB, E])
            rt8 = fb("router_sorted", [P, TB, 8])
            rnm = fb("router_negmax", [P, TB])
            rsm = fb("router_sum", [P, TB])
            rrs = fb("router_rsum", [P, TB])
            rex = fb("router_exp", [P, TB, E])
            rw = fb("router_w", [P, TB, E])
            wT = fb("router_wT", [E, BLK])
            lower = fb("lower_sb", [P, P], BF16)
            onesb = fb("ones_bf16", [P, P], BF16)
            slots = fb("slots_sb", [P, 2, TB * E])
            ids = fb("ids_sb", [P, TB])
            rm = fb("router_mask", [P, TB, E], BF16)
            taken = fb("taken", [P, E])
            d1 = fb("slot_1", [P, TB * E])
            d2 = fb("slot_2", [P, TB * E])
            d3 = fb("slot_3", [P, TB * E])
            dst = fb("slot", [P, TB * E], I32)
            pairs = fb("pairs", [P, TB * E, 2], I32)
            cf = fb("counts", [1, 3, E])
            ci = fb("counts_int", [1, 2, E], I32)

            class Norm:

                def __init__(self, name, n):
                    self.parts = fb(name + "_parts", [P, TB, 6])
                    self.mv = fb(name + "_mean_var", [P, TB, 2])
                    self.ve = fb(name + "_var_eps", [P, TB])
                    self.rstd = fb(name + "_rstd", [P, TB])
                    self.stat_done = fsig(name + "_stat_done", n * TB)
                    self.mv_done = fsig(name + "_mv_done", n * TB)
                    self.ve_done = fsig(name + "_ve_done", n)
                    self.rstd_done = fsig(name + "_rstd_done", n)
                    self.out = fsig(name + "_out", n * TB)

            ln = Norm("ln", 4)
            ln2 = Norm("ln2", 1)

            consts = fsig("front_consts")
            pool_consts = fsig("pool_consts")
            x_in = fsig("x_in", 16)
            ctx_in_ = fsig("ctx_in", 16)
            hT_ps = fsig("hT_ps", 2)
            hT_sb = fsig("hT_sb", 2 * KC)
            q_ps = fsig("q_ps", 2 * KC)
            k_ps = fsig("k_ps", 2 * KC)
            v_ps = fsig("v_ps", 2)
            qT_sb = fsig("qT_sb", KC)
            kT_sb = fsig("kT_sb", 2 * KC)
            v_sb = fsig("v_sb", 2)
            tok_ps = fsig("tok_ps", 2)
            lg_ps = fsig("lg_ps", 2 * TB)
            lg_sb = fsig("lg_sb", 2 * TB)
            lg_nm = fsig("lg_nm", 2)
            p_sb = fsig("p_sb", 2 * TB)
            p_rs = fsig("p_rs", 2)
            w_sb = fsig("w_sb", 2 * TB)
            pool_ps = fsig("pool_ps", KC)
            mT_sb = fsig("mT_sb", KC)
            pk_ps = fsig("pk_ps")
            a_mul = fsig("a_mul")
            a_sum = fsig("a_sum")
            x1b_sb = fsig("x1b_sb")
            x1T_ps = fsig("x1T_ps")
            cT_ps = fsig("cT_ps")
            x1T_sb = fsig("x1T_sb")
            cT_sb = fsig("cT_sb")
            xwT_sb = fsig("xwT_sb", KC)
            sim_ps = fsig("sim_ps")
            sim_mx = fsig("sim_mx")
            sim_nm = fsig("sim_nm", 2)
            bp_sb = fsig("bp_sb", TB)
            bp_rs = fsig("bp_rs")
            A_sb = fsig("A_sb", TB)
            AT_ps = fsig("AT_ps")
            mrow_ps = fsig("mrow_ps")
            AT_sb = fsig("AT_sb")
            g_sb = fsig("g_sb")
            g_ps = fsig("g_ps")
            bd_sb = fsig("bd_sb", SB)
            be_sb = fsig("be_sb")
            hq_ps = fsig("hq_ps")
            hqT_sb = fsig("hqT_sb")
            xhT_sb = fsig("xhT_sb")
            hc_ps = fsig("hc_ps")
            hc_rs = fsig("hc_rs")
            hc_sb = fsig("hc_sb", SB)
            Wx_sb = fsig("Wx_sb", SB * KC)
            hcq_ps = fsig("hcq_ps")
            b_sum = fsig("b_sum")
            qz_sb = fsig("qz_sb", 2 * KC)
            NS = 4 * TB
            NCH = sum(t % 2 + 1 for t in range(TB)) * 4
            s_ps = fsig("s_ps", NS)
            s_mx = fsig("s_mx", NS)
            s_nm = fsig("s_nm", NS)
            s_p = fsig("s_p", NS)
            pT_ps = fsig("pT_ps", NCH)
            pT0_sb = fsig("pT0_sb", NS)
            pT1_sb = fsig("pT1_sb", NCH - NS)
            pT_used = fsig("pT_used", NCH)
            o_rs = fsig("o_rs", TB)
            o_sb = fsig("o_sb", TB)
            kept = fsig("kept", 2)
            oT_ps = fsig("oT_ps")
            oT_sb = fsig("oT_sb")
            ao_ps = fsig("ao_ps")
            c_sum = fsig("c_sum")
            h2T_ps = fsig("h2T_ps")
            h2T_sb = fsig("h2T_sb", KC)
            rl_ps = fsig("rl_ps")
            rl_sb = fsig("rl_sb")
            rl_max = fsig("rl_max", TB)
            rl_nm = fsig("rl_nm")
            rl_exp = fsig("rl_exp", TB)
            rl_w = fsig("rl_w", TB)
            rl_rs = fsig("rl_rs")
            rl_out = fsig("rl_out")
            wT_ps = fsig("wT_ps")
            wT_sb = fsig("wT_sb")
            mb_ps = fsig("mb_ps")
            acc_xa = fsig("acc_xa")
            h_out = fsig("h_out", 16)
            r_sb = fsig("r_sb")
            r_out = fsig("r_out", 16)
            rm_sb = fsig("rm_sb", TB)
            pos_ps = fsig("pos_ps")
            pos_sb = fsig("pos_sb", 2)
            slot_a = fsig("slot_a")
            slot_b = fsig("slot_b")
            listed = fsig("listed", 4)
            lists_set = fsig("lists_set", 48)
            scattered = fsig("scattered", 16 * TB * E)
            lists_free = fsig("lists_free")
            counted = fsig("counted")

            block = front.enter_context(nc.Block())

            SIDE = 6
            BEFORE = 14
            STEPS = 65
            SLOTS = 3 * (NS + 2)

            def blocks(eng, attention, behind, before):
                def one_pass(it, has_behind, has_before):
                    parts = ([behind(it - 1)] if has_behind else []) + ([before(it + 1, has_behind)] if has_before else [])
                    side = Woven(*parts)
                    a, z = 0 if has_behind else BEFORE, STEPS if has_before else BEFORE + 1
                    for slot, _ in enumerate(attention(it)):
                        side.through(a + (z - a) * (slot + 1) // SLOTS - 1)
                    side.through(STEPS)

                Woven(before(0, False)).through(STEPS)
                one_pass(0, False, True)
                with eng.Fori(1, NBLK - 1) as it:
                    one_pass(it, True, True)
                one_pass(NBLK - 1, True, False)
                Woven(behind(NBLK - 1)).through(STEPS)

            def no_attention(it):
                for _ in range(SLOTS):
                    yield

            def stats(eng, norm, b, n, src):
                per = norm.out.per
                for t in range(TB):
                    eng.bn_stats(norm.parts[:, t, :], src[:, t, :]).then_inc(norm.stat_done.sem, 1)
                for t in range(TB):
                    wait_apart(eng, (norm.stat_done.sem, b * per + n * TB + t + 1))
                    eng.bn_aggr(norm.mv[:, t, :], norm.parts[:, t, :]).then_inc(norm.mv_done.sem, 1)
                eng.wait_ge(norm.mv_done.sem, b * per + n * TB + TB)
                eng.tensor_scalar(norm.ve[:, :], norm.mv[:, :, 1], EPS, None, ALU.add).then_inc(norm.ve_done.sem, 1)

            def normalize(eng, norm, b, n, src, dst):
                eng.wait_ge(norm.rstd_done.sem, norm.rstd_done.at(b, n + 1))
                for t in range(TB):
                    eng.tensor_scalar(dst[:, t, :], src[:, t, :], norm.mv[:, t, 0:1], norm.rstd[:, t:t + 1],
                                      ALU.subtract, ALU.mult).then_inc(norm.out.sem, 1)

            def tile_of_step(s):
                t = s // 4
                return t, t % 2 + 1

            def chunks_before(s):
                return sum(tile_of_step(i)[1] for i in range(s))

            def seconds_before(s):
                return chunks_before(s) - s

            def free_of_chunk(eng, it, s, c):
                if c == 0:
                    eng.wait_ge(pT0_sb.sem, pT0_sb.at(it, s + 1))
                else:
                    eng.wait_ge(pT1_sb.sem, pT1_sb.at(it, seconds_before(s) + 1))

            @block.sync
            def _(sp):
                sp.dma_start(cols[:, :, :], cols_in).then_inc(c_loaded.sem, 16)
                sp.dma_start(xt[:, :, :], x[0:TB].rearrange("t p d -> p t d")).then_inc(x_in.sem, 16)
                sp.dma_start(rows[:, :], rows_in).then_inc(c_loaded.sem, 16)
                sp.dma_start(ident[:, :], ident_in).then_inc(c_loaded.sem, 16)
                sp.dma_start(tri[:, :, :], tri_in).then_inc(c_loaded.sem, 16)
                sp.dma_start(mask[:, :, :], mask_in).then_inc(c_loaded.sem, 16)
                for i in range(len(MATS)):
                    sp.dma_start(mats[:, i], mats_in[i].rearrange("(k p) n -> p k n", p=P)).then_inc(c_loaded.sem, 16)
                sp.dma_start(wr[:, :, :], wr_in.rearrange("(k p) n -> p k n", p=P)).then_inc(c_loaded.sem, 16)
                sp.dma_start(eb1[:, :, :], eb1_in).then_inc(c_loaded.sem, 16)
                sp.dma_start(eb2[:, :], eb2_in).then_inc(c_loaded.sem, 16)
                sp.dma_start(lower[:, :], lower_in).then_inc(c_loaded.sem, 16)
                sp.dma_start(slots[:, :, :], slots_in).then_inc(c_loaded.sem, 16)
                sp.dma_start(ids[:, :], ids_in).then_inc(c_loaded.sem, 16)
                sp.dma_start(lists[0:E * CAP, :], unused_in).then_inc(lists_set.sem, 16)
                sp.dma_start(h_rows[T:T + PAD, :], zeros_in).then_inc(lists_set.sem, 16)
                sp.dma_start(r_rows[T:T + PAD, :], zeros_in).then_inc(lists_set.sem, 16)
                sp.dma_start(ctx[:, :, :], ctx_in[0:SB].rearrange("b c d -> c b d")).then_inc(ctx_in_.sem, 16)

                def load_block(b):
                    sp.wait_ge(a_sum.sem, a_sum.at(b - 1))
                    sp.dma_start(xt[:, :, :], x[bass.ds(b * TB, TB)].rearrange("t p d -> p t d")).then_inc(x_in.sem, 16)
                    sp.wait_ge(hq_ps.sem, hq_ps.at(b - 1))
                    sp.dma_start(ctx[:, :, :], ctx_in[bass.ds(b * SB, SB)].rearrange("b c d -> c b d")).then_inc(ctx_in_.sem, 16)

                def store_block(b):
                    rows_of = bass.ds(b * BLK, BLK)
                    sp.wait_ge(ln2.out.sem, ln2.out.at(b))
                    sp.dma_start(h_rows[rows_of, :].rearrange("(t p) d -> p t d", p=P), h2n[:, :, :]).then_inc(h_out.sem, 16)
                    sp.wait_ge(r_sb.sem, r_sb.at(b))
                    sp.dma_start(r_rows[rows_of, :].rearrange("(t p) d -> p t d", p=P), rt_[:, :, :]).then_inc(r_out.sem, 16)

                load_block(1)
                load_expert(sp, 0)
                load_block(2)
                with sp.Fori(1, NBLK - 2) as it:
                    store_block(it - 1)
                    load_block(it + 2)
                for b in range(NBLK - 3, NBLK):
                    store_block(b)
                sp.wait_ge(lists_set.sem, 48)
                sp.wait_ge(h_out.sem, 16 * NBLK)
                sp.wait_ge(r_out.sem, 16 * NBLK)

            NLOAD = 5 + len(MATS) + 3 + 3

            @block.gpsimd
            def _(pool):
                pool.memset(onesb[:, :], 1.0).then_inc(pool_consts.sem, 1)
                pool.memset(ones[:, :], 1.0).then_inc(pool_consts.sem, 1)
                pool.memset(eps_t[:, :], -0.5).then_inc(pool_consts.sem, 1)
                pool.wait_ge(pool_consts.sem, 3)
                pool.wait_ge(lists_set.sem, 48)
                pool.wait_ge(c_loaded.sem, 16 * NLOAD)

                def root(norm, b, n):
                    pool.wait_ge(norm.ve_done.sem, norm.ve_done.at(b, n + 1))
                    pool.tensor_tensor(norm.rstd[:, :], norm.ve[:, :], eps_t[:, :], ALU.pow).then_inc(norm.rstd_done.sem, 1)

                def scatter(b, a, z):
                    for j in range(a, z):
                        pool.indirect_dma_start(lists, bass.IndirectOffsetOnAxis(dst[:, j:j + 1], 0), pairs[:, j, :], None)\
                            .then_inc(scattered.sem, 16)

                def keep(b):
                    pool.wait_ge(ln.out.sem, ln.out.at(b, 3 * TB))
                    if not (isinstance(b, int) and b == 0):
                        pool.wait_ge(acc_xa.sem, acc_xa.at(b - 1))
                    pool.tensor_tensor(xb[:, :, :], x2[:, :, :], over_tiles(row["bo"]), ALU.add).then_inc(kept.sem, 1)
                    pool.tensor_copy(xr[:, :, :], x2[:, :, :]).then_inc(kept.sem, 1)

                def behind(b):
                    yield 3
                    root(ln2, b, 0)
                    yield 4
                    pool.wait_ge(kept.sem, kept.at(b))
                    pool.tensor_tensor(xa[:, :, :], at_[:, :, :], xr[:, :, :], ALU.add).then_inc(acc_xa.sem, 1)
                    yield 11
                    wait_apart(pool, (listed.sem, listed.at(b, 3)))
                    scatter(b, 0, 2)
                    if isinstance(b, int) and b == NBLK - 2:
                        keep(b + 1)
                    if isinstance(b, int) and b >= NBLK - 2:
                        scatter(b, 2, TB * E)
                        pool.wait_ge(scattered.sem, scattered.at(b))
                        pool.nop().then_inc(lists_free.sem, 1)

                def before(b, has_behind):
                    if has_behind or b == 1:
                        keep(b - 1)
                    yield 14
                    root(ln, b, 0)
                    for i in range(10):
                        yield 16 + i
                        if has_behind:
                            scatter(b - 2, 2 + 3 * i, 5 + 3 * i)
                    yield 36
                    pool.wait_ge(a_mul.sem, a_mul.at(b))
                    pool.tensor_tensor(hn[:, :, :], lg[:, :, :], xt[:, :, :], ALU.add).then_inc(a_sum.sem, 1)
                    yield 37
                    root(ln, b, 1)
                    yield 39
                    pool.wait_ge(ln.out.sem, ln.out.at(b, 2 * TB))
                    pool.tensor_tensor(x1b[:, :, :], x1[:, :, :], over_tiles(row["bqv"]), ALU.add).then_inc(x1b_sb.sem, 1)
                    yield 53
                    root(ln, b, 2)
                    yield 55
                    root(ln, b, 3)
                    if has_behind:
                        pool.wait_ge(scattered.sem, scattered.at(b - 2))
                        pool.nop().then_inc(lists_free.sem, 1)

                def attention(it):
                    return no_attention(it)

                blocks(pool, attention, behind, before)

            @block.scalar
            def _(act):
                act.wait_ge(c_loaded.sem, 16 * NLOAD)
                act.wait_ge(consts.sem, 8)

                def to_hT(b, n, scale, shift):
                    act.wait_ge(hT_ps.sem, hT_ps.at(b, n + 1))
                    for kc in range(KC):
                        act.activation(hT[:, kc, :], ps[:, SIDE + kc, :], ACT.Identity, bias=col[shift](kc),
                                       scale=col[scale](kc)).then_inc(hT_sb.sem, 1)

                def feature_exp(b, n):
                    act.wait_ge(lg_nm.sem, lg_nm.at(b, n + 1))
                    for t in range(TB):
                        act.activation(pt[:, t, :], lg[:, t, :], ACT.Exp, bias=nm[:, t:t + 1], scale=D ** -0.5,
                                       accum_out=sm[:, t:t + 1]).then_inc(p_sb.sem, 1)

                def keys(b, n, dst, bias):
                    for mc in range(KC):
                        act.wait_ge(k_ps.sem, k_ps.at(b, n * KC + mc + 1))
                        act.activation(dst[:, mc, :], ps[:, SIDE + mc, :], ACT.Identity, bias=col[bias](mc)).then_inc(kT_sb.sem, 1)

                def before(b, has_behind):
                    yield 17
                    to_hT(b, 0, "gamma", "beta")
                    yield 19
                    for mc in range(KC):
                        act.wait_ge(q_ps.sem, q_ps.at(b, mc + 1))
                        act.activation(qT[:, mc, :], ps[:, SIDE + mc, :], ACT.Identity, bias=col["bq"](mc)).then_inc(qT_sb.sem, 1)
                    yield 21
                    keys(b, 0, kT, "bk")
                    yield 26
                    feature_exp(b, 0)
                    yield 32
                    feature_exp(b, 1)
                    yield 37
                    act.wait_ge(cT_ps.sem, cT_ps.at(b))
                    act.activation(cT[:, :, :], ps[:, SIDE, 0:KC * SB * C].rearrange("p (k c) -> p k c", k=KC), ACT.Copy).then_inc(cT_sb.sem, 1)
                    yield 40
                    act.wait_ge(x1T_ps.sem, x1T_ps.at(b))
                    act.activation(x1T[:, :, :], ps[:, SIDE:SIDE + 2, :], ACT.Copy).then_inc(x1T_sb.sem, 1)
                    yield 44
                    act.wait_ge(sim_nm.sem, sim_nm.at(b))
                    for t in range(TB):
                        act.activation(pt[:, t, 0:C], ps[:, SIDE, t * P:t * P + C], ACT.Exp, bias=nm[:, t:t + 1],
                                       accum_out=sm[:, t:t + 1]).then_inc(bp_sb.sem, 1)
                    yield 47
                    act.wait_ge(AT_ps.sem, AT_ps.at(b))
                    act.activation(AT[:, :], ps[0:C, SIDE, :], ACT.Copy).then_inc(AT_sb.sem, 1)
                    yield 48
                    act.wait_ge(bd_sb.sem, bd_sb.at(b))
                    act.activation(be[:, :], bd[:, :], ACT.Exp).then_inc(be_sb.sem, 1)
                    yield 49
                    act.wait_ge(hq_ps.sem, hq_ps.at(b))
                    act.activation(qT[:, :, :], ps[:, SIDE:SIDE + 2, :], ACT.Copy).then_inc(hqT_sb.sem, 1)
                    yield 58
                    to_hT(b, 1, "g1", "b1")
                    yield 60
                    for mc in range(KC):
                        act.wait_ge(q_ps.sem, q_ps.at(b, KC + mc + 1))
                        for eo in range(2):
                            act.activation(qz[:, eo, mc, :], ps[:, SIDE + mc, :], ACT.Identity, bias=qbias[:, eo, mc:mc + 1],
                                           scale=qscale[:, eo, mc:mc + 1]).then_inc(qz_sb.sem, 1)
                    yield 62
                    keys(b, 1, skT, "fbk")

                def attention(it):
                    for s in range(NS + 2):
                        yield
                        yield
                        if s < NS:
                            t, nb = tile_of_step(s)
                            L = P * nb
                            act.wait_ge(s_nm.sem, s_nm.at(it, s + 1))
                            if s >= 2:
                                act.wait_ge(pT_ps.sem, pT_ps.at(it, chunks_before(s - 1)))
                            for h in range(4):
                                ins = act.activation(p4[:, s % 2, h, 0:L], ps[:, 2 * (s % 2) + h // 2, (h % 2) * L:(h % 2 + 1) * L],
                                                     ACT.Exp, bias=nm4[:, s % 2, h:h + 1],
                                                     accum_out=sm16[:, t, s % 4 * 4 + h:s % 4 * 4 + h + 1])
                            ins.then_inc(s_p.sem, 1)
                        if 1 <= s <= NS and tile_of_step(s - 1)[1] == 2:
                            n = chunks_before(s - 1) + 1
                            act.wait_ge(pT_ps.sem, pT_ps.at(it, n + 1))
                            if n >= 3:
                                act.wait_ge(pT_used.sem, pT_used.at(it, n - 2))
                            act.activation(PT[:, n % 3, :], ps[:, 4, :], ACT.Copy).then_inc(pT1_sb.sem, 1)
                        yield

                def behind(b):
                    yield 1
                    act.wait_ge(oT_ps.sem, oT_ps.at(b))
                    act.activation(oT[:, :, :], ps[:, SIDE:SIDE + 2, :], ACT.Copy).then_inc(oT_sb.sem, 1)
                    yield 6
                    act.wait_ge(h2T_ps.sem, h2T_ps.at(b))
                    for kc in range(KC):
                        act.activation(h2T[:, kc, :], ps[:, SIDE + kc, :], ACT.Identity, bias=col["b2"](kc),
                                       scale=col["g2"](kc)).then_inc(h2T_sb.sem, 1)
                    yield 9
                    act.wait_ge(rl_nm.sem, rl_nm.at(b))
                    for t in range(TB):
                        act.activation(rex[:, t, :], rl[:, t, :], ACT.Exp, bias=rnm[:, t:t + 1]).then_inc(rl_exp.sem, 1)
                    yield 12
                    act.wait_ge(wT_ps.sem, wT_ps.at(b))
                    act.activation(wT[:, :], ps[0:E, SIDE + 1, :], ACT.Copy).then_inc(wT_sb.sem, 1)

                blocks(act, attention, behind, before)

            @block.vector
            def _(dve):
                dve.wait_ge(c_loaded.sem, 16 * NLOAD)
                dve.memset(taken[:, :], 0.0).then_inc(consts.sem, 1)
                dve.tensor_copy(identb[:, :], ident[:, :]).then_inc(consts.sem, 1)
                for eo, n in enumerate(("even", "odd")):
                    i = COLS.index(n)
                    dve.tensor_scalar(qscale[:, eo, :], cols[:, i, :], HD ** -0.5, None, ALU.mult).then_inc(consts.sem, 1)
                dve.wait_ge(consts.sem, 4)
                for eo in range(2):
                    for kc in range(KC):
                        dve.tensor_tensor(qbias[:, eo, kc:kc + 1], qscale[:, eo, kc:kc + 1], col["fbq"](kc), ALU.mult).then_inc(consts.sem, 1)

                def feature_logits(b, n, bias):
                    for t in range(TB):
                        if t % 2 == 0:
                            wait_apart(dve, (lg_ps.sem, lg_ps.at(b, n * TB + t + 2)))
                        dve.tensor_tensor_reduce(lg[:, t, :], tile_of(SIDE, t), row[bias], 1.0, -3.0e38, ALU.add, ALU.max,
                                                 mx[:, t:t + 1]).then_inc(lg_sb.sem, 1)
                    dve.wait_ge(lg_sb.sem, lg_sb.at(b, n * TB + TB))
                    dve.tensor_scalar(nm[:, :], mx[:, :], -(D ** -0.5), None, ALU.mult).then_inc(lg_nm.sem, 1)

                def feature_weight(b, n):
                    dve.wait_ge(p_sb.sem, p_sb.at(b, n * TB + TB))
                    dve.reciprocal(rs[:, :], sm[:, :]).then_inc(p_rs.sem, 1)
                    dve.wait_ge(tok_ps.sem, tok_ps.at(b, n + 1))
                    dve.wait_ge(p_rs.sem, p_rs.at(b, n + 1))
                    for t in range(TB):
                        dve.scalar_tensor_tensor(wt[:, t, :], pt[:, t, :], rs[:, t:t + 1], tile_of(SIDE, t),
                                                 ALU.mult, ALU.mult).then_inc(w_sb.sem, 1)

                def values(b, n, dst, bias):
                    dve.wait_ge(v_ps.sem, v_ps.at(b, n + 1))
                    dve.tensor_tensor(dst[:, :, :], pair(SIDE), over_tiles(row[bias]), ALU.add).then_inc(v_sb.sem, 1)

                def before(b, has_behind):
                    yield 14
                    dve.wait_ge(x_in.sem, x_in.at(b))
                    stats(dve, ln, b, 0, xt)
                    yield 15
                    normalize(dve, ln, b, 0, xt, hn)
                    yield 23
                    values(b, 0, vt, "bv")
                    yield 25
                    feature_logits(b, 0, "bqa")
                    yield 27
                    feature_weight(b, 0)
                    yield 29
                    for mc in range(KC):
                        dve.wait_ge(pool_ps.sem, pool_ps.at(b, mc + 1))
                        dve.wait_ge(kT_sb.sem, kT_sb.at(b, mc + 1))
                        dve.tensor_tensor(hT[:, mc, :], ps[:, SIDE + mc, :], kT[:, mc, :], ALU.mult).then_inc(mT_sb.sem, 1)
                    yield 31
                    feature_logits(b, 1, "bka")
                    yield 33
                    feature_weight(b, 1)
                    yield 35
                    dve.wait_ge(pk_ps.sem, pk_ps.at(b))
                    dve.tensor_tensor(lg[:, :, :], pair(SIDE), vt[:, :, :], ALU.mult).then_inc(a_mul.sem, 1)
                    yield 37
                    wait_apart(dve, (a_sum.sem, a_sum.at(b)))
                    stats(dve, ln, b, 1, hn)
                    yield 38
                    normalize(dve, ln, b, 1, hn, x1)
                    yield 41
                    dve.wait_ge(x1T_sb.sem, x1T_sb.at(b))
                    for kc in range(KC):
                        dve.tensor_scalar(hT[:, kc, :], x1T[:, kc, :], col["w3"](kc), col["w2"](kc), ALU.mult, ALU.add).then_inc(xwT_sb.sem, 1)
                    yield 43
                    dve.wait_ge(sim_ps.sem, sim_ps.at(b))
                    sim = ps[:, SIDE, :].rearrange("p (t c) -> p t c", t=TB)
                    dve.tensor_reduce(mx[:, :], sim[:, :, 0:C], AX.X, ALU.max).then_inc(sim_mx.sem, 1)
                    dve.wait_ge(sim_mx.sem, sim_mx.at(b))
                    dve.tensor_scalar(nm[:, :], mx[:, :], -1.0, None, ALU.mult).then_inc(sim_nm.sem, 1)
                    dve.scalar_tensor_tensor(bm[:, :], mx[:, :], row["bs"], sim[:, :, C], ALU.add, ALU.add).then_inc(sim_nm.sem, 1)
                    yield 45
                    dve.wait_ge(bp_sb.sem, bp_sb.at(b))
                    dve.reciprocal(rs[:, :], sm[:, :]).then_inc(bp_rs.sem, 1)
                    dve.wait_ge(bp_rs.sem, bp_rs.at(b))
                    for t in range(TB):
                        dve.tensor_scalar(wt[:, t, 0:C], pt[:, t, 0:C], rs[:, t:t + 1], None, ALU.mult).then_inc(A_sb.sem, 1)
                    dve.wait_ge(mrow_ps.sem, mrow_ps.at(b))
                    dve.tensor_reduce(bg[:, :], ps[0:1, SIDE + 1, :].rearrange("p (b s) -> p b s", b=SB), AX.X, ALU.max).then_inc(g_sb.sem, 1)
                    yield 47
                    dve.wait_ge(g_ps.sem, g_ps.at(b))
                    for i in range(SB):
                        dve.tensor_scalar(bd[:, 2 * i:2 * i + 2], bm[:, 2 * i:2 * i + 2], ps[:, SIDE + 1, i:i + 1], None,
                                          ALU.subtract).then_inc(bd_sb.sem, 1)
                    yield 50
                    dve.wait_ge(hqT_sb.sem, hqT_sb.at(b))
                    dve.tensor_tensor(kT[:, :, :], qT[:, :, :], x1T[:, :, :], ALU.mult).then_inc(xhT_sb.sem, 1)
                    yield 51
                    dve.wait_ge(hc_ps.sem, hc_ps.at(b))
                    dve.reciprocal(hcr[:, :], ps[:, SIDE + 1, 0:3 * SB].rearrange("p (b j) -> p b j", j=3)[:, :, 2]).then_inc(hc_rs.sem, 1)
                    dve.wait_ge(hc_rs.sem, hc_rs.at(b))
                    for i in range(SB):
                        dve.tensor_scalar(hc[:, i, :], ps[:, SIDE + 1, 3 * i:3 * i + KC], hcr[:, i:i + 1], None, ALU.mult).then_inc(hc_sb.sem, 1)
                    dve.wait_ge(hc_sb.sem, hc_sb.at(b))
                    for i in range(SB):
                        for kc in range(KC):
                            dve.scalar_tensor_tensor(Wx[:, i, kc, :], W["Wf3"][:, kc, :], hc[:, i, kc:kc + 1], W["Wf0"][:, kc, :],
                                                     ALU.mult, ALU.add).then_inc(Wx_sb.sem, 1)
                    yield 53
                    dve.wait_ge(hcq_ps.sem, hcq_ps.at(b))
                    dve.wait_ge(x1b_sb.sem, x1b_sb.at(b))
                    dve.tensor_tensor(hn[:, :, :], pair(SIDE), x1b[:, :, :], ALU.add).then_inc(b_sum.sem, 1)
                    wait_apart(dve, (b_sum.sem, b_sum.at(b)))
                    stats(dve, ln, b, 2, hn)
                    yield 54
                    if has_behind or b == 1:
                        dve.wait_ge(kept.sem, kept.at(b - 1))
                    normalize(dve, ln, b, 2, hn, x2)
                    yield 55
                    wait_apart(dve, (ln.out.sem, ln.out.at(b, 3 * TB)))
                    stats(dve, ln, b, 3, x2)
                    yield 56
                    normalize(dve, ln, b, 3, x2, hn)
                    yield 64
                    values(b, 1, sv, "fbv")

                def attention(it):
                    for s in range(NS + 2):
                        yield
                        if s >= 5 and s % 4 == 1:
                            t = (s - 5) // 4
                            if t == 0 and not (isinstance(it, int) and it == 0):
                                dve.wait_ge(oT_ps.sem, oT_ps.at(it - 1))
                            dve.wait_ge(pT_used.sem, pT_used.at(it, chunks_before(4 * t + 4)))
                            dve.reciprocal(rs16[:, :], sm16[:, t, :]).then_inc(o_rs.sem, 1)
                            dve.wait_ge(o_rs.sem, o_rs.at(it, t + 1))
                            o = ps[:, 5, (t % 2) * D:(t % 2 + 1) * D].rearrange("p (h d) -> p h d", h=H)
                            dve.tensor_tensor(ot[:, t, :].rearrange("p (h d) -> p h d", h=H), o,
                                              rs16[:, :].rearrange("p (h o) -> p h o", o=1).to_broadcast([P, H, HD]),
                                              ALU.mult).then_inc(o_sb.sem, 1)
                        if s < NS:
                            L = P * tile_of_step(s)[1]
                            dve.wait_ge(s_ps.sem, s_ps.at(it, s + 1))
                            dve.tensor_reduce(mx4[:, s % 2, :], ps[:, 2 * (s % 2):2 * (s % 2) + 2, 0:2 * L].rearrange("p r (e k) -> p r e k", e=2),
                                              AX.X, ALU.max).then_inc(s_mx.sem, 1)
                            dve.wait_ge(s_mx.sem, s_mx.at(it, s + 1))
                            dve.tensor_scalar(nm4[:, s % 2, :], mx4[:, s % 2, :], -1.0, None, ALU.mult).then_inc(s_nm.sem, 1)
                        if 1 <= s <= NS:
                            n = chunks_before(s - 1)
                            dve.wait_ge(pT_ps.sem, pT_ps.at(it, n + 1))
                            if n >= 3:
                                dve.wait_ge(pT_used.sem, pT_used.at(it, n - 2))
                            dve.tensor_copy(PT[:, n % 3, :], ps[:, 4, :]).then_inc(pT0_sb.sem, 1)
                        yield
                        yield

                def behind(b):
                    yield 3
                    dve.wait_ge(ao_ps.sem, ao_ps.at(b))
                    dve.wait_ge(kept.sem, kept.at(b))
                    dve.tensor_tensor(at_[:, :, :], pair(SIDE), xb[:, :, :], ALU.add).then_inc(c_sum.sem, 1)
                    wait_apart(dve, (c_sum.sem, c_sum.at(b)))
                    stats(dve, ln2, b, 0, at_)
                    yield 4
                    if not (isinstance(b, int) and b == 0):
                        dve.wait_ge(h_out.sem, h_out.at(b - 1))
                    normalize(dve, ln2, b, 0, at_, h2n)
                    yield 8
                    dve.wait_ge(rl_ps.sem, rl_ps.at(b))
                    dve.tensor_tensor(rl[:, :, :], ps[:, SIDE, 0:TB * E].rearrange("p (t e) -> p t e", t=TB), over_tiles(row["br"]), ALU.add).then_inc(rl_sb.sem, 1)
                    wait_apart(dve, (rl_sb.sem, rl_sb.at(b)))
                    for t in range(TB):
                        dve.max(rt8[:, t, :], rl[:, t, :]).then_inc(rl_max.sem, 1)
                    dve.wait_ge(rl_max.sem, rl_max.at(b))
                    dve.tensor_scalar(rnm[:, :], rt8[:, :, 0], -1.0, None, ALU.mult).then_inc(rl_nm.sem, 1)
                    for t in range(TB):
                        dve.tensor_scalar(rm[:, t, :], rl[:, t, :], rt8[:, t, 1:2], None, ALU.is_ge).then_inc(rm_sb.sem, 1)
                    yield 10
                    dve.wait_ge(rl_exp.sem, rl_exp.at(b))
                    for t in range(TB):
                        dve.scalar_tensor_tensor(rw[:, t, :], rl[:, t, :], rt8[:, t, 1:2], rex[:, t, :], ALU.is_ge, ALU.mult,
                                                 accum_out=rsm[:, t:t + 1]).then_inc(rl_w.sem, 1)
                    dve.wait_ge(rl_w.sem, rl_w.at(b))
                    dve.reciprocal(rrs[:, :], rsm[:, :]).then_inc(rl_rs.sem, 1)
                    dve.wait_ge(rl_rs.sem, rl_rs.at(b))
                    dve.tensor_tensor(rw[:, :, :], rw[:, :, :], rrs[:, :].rearrange("p (t o) -> p t o", o=1).to_broadcast([P, TB, E]),
                                      ALU.mult).then_inc(rl_out.sem, 1)
                    yield 11
                    dve.wait_ge(pos_ps.sem, pos_ps.at(b))
                    pos = ps[:, SIDE, 0:TB * E]
                    dve.tensor_tensor(d1[:, :].rearrange("p (t e) -> p t e", t=TB), pos.rearrange("p (t e) -> p t e", t=TB),
                                      over_tiles(taken[:, :]), ALU.add).then_inc(pos_sb.sem, 1)
                    dve.wait_ge(pos_sb.sem, pos_sb.at(b, 1))
                    dve.tensor_tensor(taken[:, :], ps[:, SIDE, TB * E:TB * E + E], taken[:, :], ALU.add).then_inc(pos_sb.sem, 1)
                    dve.tensor_tensor(d2[:, :], d1[:, :], slots[:, 1, :], ALU.add).then_inc(slot_a.sem, 1)
                    dve.wait_ge(slot_a.sem, slot_a.at(b))
                    dve.tensor_tensor(d3[:, :], d2[:, :], rm[:, :, :].rearrange("p t e -> p (t e)"), ALU.mult).then_inc(slot_b.sem, 1)
                    dve.wait_ge(slot_b.sem, slot_b.at(b))
                    if not (isinstance(b, int) and b == 0):
                        dve.wait_ge(lists_free.sem, lists_free.at(b - 1))
                    dve.tensor_tensor(dst[:, :], d3[:, :], slots[:, 0, :], ALU.add).then_inc(listed.sem, 1)
                    dve.tensor_copy(pairs[:, :, 1].bitcast(F32), rw[:, :, :].rearrange("p t e -> p (t e)")).then_inc(listed.sem, 1)
                    dve.tensor_copy(pairs[:, :, 0].rearrange("p (t e) -> p t e", t=TB),
                                    ids[:, :].rearrange("p (t o) -> p t o", o=1).to_broadcast([P, TB, E])).then_inc(listed.sem, 1)
                    dve.wait_ge(listed.sem, listed.at(b, 3))
                    dve.tensor_scalar(ids[:, :], ids[:, :], float(BLK), None, ALU.add).then_inc(listed.sem, 1)
                    yield 14
                    dve.wait_ge(mb_ps.sem, mb_ps.at(b))
                    dve.wait_ge(acc_xa.sem, acc_xa.at(b))
                    if not (isinstance(b, int) and b == 0):
                        dve.wait_ge(r_out.sem, r_out.at(b - 1))
                    dve.tensor_tensor(rt_[:, :, :], pair(SIDE), xa[:, :, :], ALU.add).then_inc(r_sb.sem, 1)

                blocks(dve, attention, behind, before)
                dve.wait_ge(pos_sb.sem, pos_sb.at(NBLK - 1))
                dve.tensor_scalar(ci[:, 0, :], taken[0:1, :], float(TE - 1), None, ALU.add).then_inc(counted.sem, 1)
                dve.wait_ge(counted.sem, 1)
                dve.tensor_scalar(ci[:, 1, :], ci[:, 0, :], TE.bit_length() - 1, None, ALU.logical_shift_right).then_inc(counted.sem, 1)
                dve.wait_ge(counted.sem, 2)
                dve.tensor_scalar(cf[:, 0, :], ci[:, 1, :], 2.0, None, ALU.max).then_inc(counted.sem, 1)
                dve.memset(cf[:, 1, 0:1], 0.0).then_inc(counted.sem, 1)
                for e in range(1, E):
                    dve.wait_ge(counted.sem, 3 + e)
                    dve.tensor_tensor(cf[:, 1, e:e + 1], cf[:, 1, e - 1:e], cf[:, 0, e - 1:e], ALU.add).then_inc(counted.sem, 1)
                dve.wait_ge(counted.sem, 3 + E)
                dve.tensor_copy(tiles[:, :, :], cf[:, 0:2, :]).then_inc(counted.sem, 1)

            @block.tensor
            def _(pe):
                pe.wait_ge(c_loaded.sem, 16 * NLOAD)
                pe.wait_ge(consts.sem, 8)
                pe.wait_ge(pool_consts.sem, 3)

                def to_features(src, last):
                    for t in range(TB):
                        for kc in range(KC):
                            ins = pe.transpose(ps[:, SIDE + kc, t * P:(t + 1) * P], src[:, t, kc * P:(kc + 1) * P], ident[:, :])
                    ins.then_inc(last.sem, 1)

                def to_tokens(src, last):
                    for t in range(TB):
                        for kc in range(KC):
                            ins = pe.transpose(tile_of(SIDE, t)[:, kc * P:(kc + 1) * P], src[:, kc, t * P:(t + 1) * P], ident[:, :])
                    ins.then_inc(last.sem, 1)

                def weight_rows(w, src, done):
                    for mc in range(KC):
                        for kc in range(KC):
                            ins = pe.matmul(ps[:, SIDE + mc, :], w[:, kc, mc * P:(mc + 1) * P], src[:, kc, :],
                                            start=(kc == 0), stop=(kc == KC - 1))
                        ins.then_inc(done.sem, 1)

                def token_rows(terms, t):
                    n = len(terms) * KC
                    for i, (src, w) in enumerate(terms):
                        for kc in range(KC):
                            j = i * KC + kc
                            ins = pe.matmul(tile_of(SIDE, t), src[:, kc, t * P:(t + 1) * P], w[:, kc, :],
                                            start=(j == 0), stop=(j == n - 1))
                    return ins

                def before(b, has_behind):
                    yield 16
                    pe.wait_ge(ln.out.sem, ln.out.at(b, TB))
                    if has_behind:
                        pe.wait_ge(r_sb.sem, r_sb.at(b - 2))
                    elif b == 1:
                        pe.wait_ge(v_sb.sem, v_sb.at(0))
                    to_features(hn, hT_ps)
                    yield 18
                    pe.wait_ge(hT_sb.sem, hT_sb.at(b, KC))
                    weight_rows(W["Wq"], hT, q_ps)
                    yield 20
                    pe.wait_ge(qT_sb.sem, qT_sb.at(b))
                    weight_rows(W["Wk"], hT, k_ps)
                    yield 22
                    pe.wait_ge(kT_sb.sem, kT_sb.at(b, KC))
                    for t in range(TB):
                        ins = token_rows([(hT, W["Wv"])], t)
                    ins.then_inc(v_ps.sem, 1)
                    yield 24
                    pe.wait_ge(v_sb.sem, v_sb.at(b, 1))
                    for t in range(TB):
                        token_rows([(qT, W["Wqa"])], t).then_inc(lg_ps.sem, 1)
                    yield 26
                    pe.wait_ge(lg_sb.sem, lg_sb.at(b, TB))
                    to_tokens(qT, tok_ps)
                    yield 28
                    pe.wait_ge(w_sb.sem, w_sb.at(b, TB))
                    for mc in range(KC):
                        for i in range(SB):
                            o = ps[:, SIDE + mc, i * S:(i + 1) * S]
                            pe.matmul(o, wt[:, 2 * i, mc * P:(mc + 1) * P], tri[:, 0:2, :].rearrange("p a q -> p (a q)"),
                                      start=True, stop=False, skip_group_check=True)
                            ins = pe.matmul(o[:, P:S], wt[:, 2 * i + 1, mc * P:(mc + 1) * P], tri[:, 2, :],
                                            start=False, stop=True, skip_group_check=True)
                        ins.then_inc(pool_ps.sem, 1)
                    yield 30
                    pe.wait_ge(mT_sb.sem, mT_sb.at(b))
                    for t in range(TB):
                        token_rows([(hT, W["Wka"])], t).then_inc(lg_ps.sem, 1)
                    yield 32
                    pe.wait_ge(lg_sb.sem, lg_sb.at(b))
                    to_tokens(hT, tok_ps)
                    yield 34
                    pe.wait_ge(w_sb.sem, w_sb.at(b))
                    for t in range(TB):
                        o = tile_of(SIDE, t)
                        if t % 2 == 0:
                            ins = pe.matmul(o, tri[:, 0, :], wt[:, t, :], start=True, stop=True)
                        else:
                            pe.matmul(o, tri[:, 1, :], wt[:, t - 1, :], start=True, stop=False)
                            ins = pe.matmul(o, tri[:, 2, :], wt[:, t, :], start=False, stop=True)
                    ins.then_inc(pk_ps.sem, 1)
                    yield 36
                    pe.wait_ge(ctx_in_.sem, ctx_in_.at(b))
                    pe.wait_ge(a_mul.sem, a_mul.at(b))
                    for i in range(SB):
                        for kc in range(KC):
                            o = ps[:, SIDE, kc * SB * C + i * C:kc * SB * C + (i + 1) * C]
                            ins = pe.transpose(o, ctx[:, i, kc * P:(kc + 1) * P], ident[0:C, 0:C])
                    ins.then_inc(cT_ps.sem, 1)
                    yield 39
                    pe.wait_ge(ln.out.sem, ln.out.at(b, 2 * TB))
                    pe.wait_ge(cT_sb.sem, cT_sb.at(b))
                    to_features(x1, x1T_ps)
                    yield 42
                    pe.wait_ge(xwT_sb.sem, xwT_sb.at(b))
                    for t in range(TB):
                        tok = slice(t * P, (t + 1) * P)
                        for kc in range(KC):
                            pe.matmul(ps[:, SIDE, t * P:t * P + C], hT[:, kc, tok], cT[:, kc, (t // 2) * C:(t // 2 + 1) * C],
                                      start=(kc == 0), stop=(kc == KC - 1))
                        for kc in range(KC):
                            ins = pe.matmul(ps[:, SIDE, t * P + C:t * P + C + 1], x1T[:, kc, tok], col["w1"](kc),
                                            start=(kc == 0), stop=(kc == KC - 1))
                    ins.then_inc(sim_ps.sem, 1)
                    yield 44
                    pe.wait_ge(sim_nm.sem, sim_nm.at(b))
                    for t in range(TB):
                        ins = pe.matmul(ps[0:1, SIDE + 1, t * P:(t + 1) * P], bm[:, t:t + 1], ident[:, :], start=True, stop=True)
                    ins.then_inc(mrow_ps.sem, 1)
                    yield 46
                    pe.wait_ge(A_sb.sem, A_sb.at(b))
                    for t in range(TB):
                        ins = pe.transpose(ps[0:C, SIDE, t * P:(t + 1) * P], wt[:, t, 0:C], ident[:, :])
                    ins.then_inc(AT_ps.sem, 1)
                    pe.wait_ge(g_sb.sem, g_sb.at(b))
                    pe.matmul(ps[:, SIDE + 1, 0:SB], ones[0:1, :], bg[:, :], start=True, stop=True).then_inc(g_ps.sem, 1)
                    yield 48
                    pe.wait_ge(AT_sb.sem, AT_sb.at(b))
                    pe.wait_ge(bd_sb.sem, bd_sb.at(b))
                    for mc in range(KC):
                        for i in range(SB):
                            ins = pe.matmul(ps[:, SIDE + mc, i * S:(i + 1) * S], ctx[:, i, mc * P:(mc + 1) * P], AT[:, i * S:(i + 1) * S],
                                            start=True, stop=True)
                    ins.then_inc(hq_ps.sem, 1)
                    yield 50
                    pe.wait_ge(be_sb.sem, be_sb.at(b))
                    pe.wait_ge(hqT_sb.sem, hqT_sb.at(b))
                    for i in range(SB):
                        for j in range(KC + 1):
                            for k in range(2):
                                t = 2 * i + k
                                lhs = x1[:, t, j * P:(j + 1) * P] if j < KC else ones[:, :]
                                ins = pe.matmul(ps[:, SIDE + 1, 3 * i + j:3 * i + j + 1], lhs, be[:, t:t + 1], start=(k == 0), stop=(k == 1))
                    ins.then_inc(hc_ps.sem, 1)
                    yield 52
                    pe.wait_ge(xhT_sb.sem, xhT_sb.at(b))
                    pe.wait_ge(Wx_sb.sem, Wx_sb.at(b))
                    for t in range(TB):
                        ins = token_rows([(x1T, Wx[:, t // 2]), (qT, W["Wf1"]), (kT, W["Wf2"])], t)
                    ins.then_inc(hcq_ps.sem, 1)
                    yield 57
                    pe.wait_ge(ln.out.sem, ln.out.at(b))
                    to_features(hn, hT_ps)
                    yield 59
                    pe.wait_ge(hT_sb.sem, hT_sb.at(b))
                    weight_rows(W["fWq"], hT, q_ps)
                    yield 61
                    pe.wait_ge(qz_sb.sem, qz_sb.at(b))
                    weight_rows(W["fWk"], hT, k_ps)
                    yield 63
                    pe.wait_ge(kT_sb.sem, kT_sb.at(b))
                    for t in range(TB):
                        ins = token_rows([(hT, W["fWv"])], t)
                    ins.then_inc(v_ps.sem, 1)

                def attention(it):
                    def scores(s):
                        t, nb = tile_of_step(s)
                        b, L, kc = t // 2, P * nb, s % 4 // 2
                        if s == 0:
                            pe.wait_ge(qz_sb.sem, qz_sb.at(it))
                            pe.wait_ge(kT_sb.sem, kT_sb.at(it))
                        if s >= 2:
                            pe.wait_ge(s_p.sem, s_p.at(it, s - 1))
                        m = mask[:, :, S - L:S]
                        for r in range(2):
                            pe.matmul(ps[:, 2 * (s % 2) + r, 0:2 * L].rearrange("p (e k) -> p e k", e=2), identb[:, :], m,
                                      start=True, stop=False, skip_group_check=True)
                        for eo in range(2):
                            for r in range(2):
                                row0 = 64 * (s % 2) + 32 * r
                                g = slice(row0, row0 + 32)
                                ins = pe.matmul(ps[:, 2 * (s % 2) + r, eo * L:(eo + 1) * L], qz[g, eo, kc, t * P:(t + 1) * P],
                                                skT[g, kc, b * S:b * S + L], start=False, stop=True, skip_group_check=True)
                        ins.then_inc(s_ps.sem, 1)

                    def turn(s, c):
                        t, nb = tile_of_step(s)
                        if c:
                            free_of_chunk(pe, it, s, 0)
                        elif s:
                            free_of_chunk(pe, it, s - 1, tile_of_step(s - 1)[1] - 1)
                        pe.wait_ge(s_p.sem, s_p.at(it, s + 1))
                        for i in range(4):
                            h, kb = c * 4 // nb + i // nb, i % nb
                            ins = pe.transpose(ps[:, 4, i * P:(i + 1) * P], p4[:, s % 2, h, kb * P:(kb + 1) * P], ident[:, :])
                        ins.then_inc(pT_ps.sem, 1)

                    def weigh(s, c):
                        t, nb = tile_of_step(s)
                        n = chunks_before(s) + c
                        free_of_chunk(pe, it, s, c)
                        if s == 0:
                            pe.wait_ge(v_sb.sem, v_sb.at(it))
                        if c == 0 and s % 4 == 0 and s:
                            pe.wait_ge(o_sb.sem, o_sb.at(it, t))
                        for i in range(4):
                            h, kb = s % 4 * 4 + c * 4 // nb + i // nb, i % nb
                            o = (t % 2) * D + h * HD
                            ins = pe.matmul(ps[:, 5, o:o + HD], PT[:, n % 3, i * P:(i + 1) * P],
                                            sv[:, 2 * (t // 2) + kb, h * HD:(h + 1) * HD], start=(kb == 0), stop=(kb == nb - 1))
                        ins.then_inc(pT_used.sem, 1)

                    for s in range(NS + 2):
                        if s >= 2 and tile_of_step(s - 2)[1] == 2:
                            weigh(s - 2, 1)
                        if s < NS:
                            scores(s)
                        yield
                        if 1 <= s <= NS:
                            turn(s - 1, 0)
                        yield
                        if 1 <= s <= NS:
                            weigh(s - 1, 0)
                            if tile_of_step(s - 1)[1] == 2:
                                turn(s - 1, 1)
                        yield

                def behind(b):
                    yield 0
                    pe.wait_ge(o_sb.sem, o_sb.at(b))
                    if isinstance(b, int) and b == NBLK - 1:
                        pe.wait_ge(r_sb.sem, r_sb.at(b - 1))
                    elif isinstance(b, int):
                        pe.wait_ge(v_sb.sem, v_sb.at(b + 1))
                    else:
                        pe.wait_ge(v_sb.sem, v_sb.at(b + 1))
                    to_features(ot, oT_ps)
                    yield 2
                    pe.wait_ge(oT_sb.sem, oT_sb.at(b))
                    for t in range(TB):
                        ins = token_rows([(oT, W["fWo"])], t)
                    ins.then_inc(ao_ps.sem, 1)
                    yield 5
                    pe.wait_ge(ln2.out.sem, ln2.out.at(b))
                    to_features(h2n, h2T_ps)
                    yield 7
                    pe.wait_ge(h2T_sb.sem, h2T_sb.at(b))
                    for t in range(TB):
                        for kc in range(KC):
                            ins = pe.matmul(ps[:, SIDE, t * E:(t + 1) * E], h2T[:, kc, t * P:(t + 1) * P], wr[:, kc, :], start=(kc == 0), stop=(kc == KC - 1))
                    ins.then_inc(rl_ps.sem, 1)
                    yield 9
                    pe.wait_ge(rm_sb.sem, rm_sb.at(b))
                    for t in range(TB):
                        o = ps[:, SIDE, t * E:(t + 1) * E]
                        for u in range(t):
                            pe.matmul(o, onesb[:, :], rm[:, u, :], start=(u == 0), stop=False)
                        pe.matmul(o, lower[:, :], rm[:, t, :], start=(t == 0), stop=True)
                    for t in range(TB):
                        ins = pe.matmul(ps[:, SIDE, TB * E:TB * E + E], onesb[:, :], rm[:, t, :], start=(t == 0), stop=(t == TB - 1))
                    ins.then_inc(pos_ps.sem, 1)
                    yield 11
                    pe.wait_ge(rl_out.sem, rl_out.at(b))
                    for t in range(TB):
                        ins = pe.matmul(ps[0:E, SIDE + 1, t * P:(t + 1) * P], rw[:, t, :], ident[:, :], start=True, stop=True)
                    ins.then_inc(wT_ps.sem, 1)
                    yield 13
                    pe.wait_ge(wT_sb.sem, wT_sb.at(b))
                    pe.wait_ge(pos_sb.sem, pos_sb.at(b))
                    for t in range(TB):
                        ins = pe.matmul(tile_of(SIDE, t), wT[:, t * P:(t + 1) * P], eb2[:, :], start=True, stop=True)
                    ins.then_inc(mb_ps.sem, 1)

                blocks(pe, attention, behind, before)

        with ExitStack() as back:
            def bb(name, shape, dt=F32):
                return back.enter_context(nc.sbuf_tensor(name, shape, dt))

            def bsig(name, per=1):
                return Count(back.enter_context(nc.semaphore(name)), per)

            RING = 4
            NW = 8
            WC = (KC * F + FT * D) // NW
            whi = bb("w_hi", [P, 2, KC * F + FT * D], F32R)
            wlo = bb("w_lo", [P, 2, KC * F + FT * D], F32R)
            b1e = bb("b1_of_expert", [P, 2, FT])
            li = bb("list_in", [P, 2, 2], I32)
            lis = bb("list_out", [P, 2, 2], I32)
            hg = bb("h_gathered", [P, 2, D])
            hT = bb("h_T", [P, KC, TE])
            hh = bb("h_hi", [P, KC, TE], F32R)
            hl = bb("h_lo", [P, KC, TE], F32R)
            mid = bb("mid", [P, RING, TE])
            midh = bb("mid_hi", [P, RING, TE], F32R)
            midl = bb("mid_lo", [P, RING, TE], F32R)
            y = bb("y", [P, 2, D])
            rt = bb("r_tok", [P, 2, TB, D])
            ost = bb("out_st", [P, TB, 6])
            omv = bb("out_mv", [P, TB, 2])
            ove = bb("out_ve", [P, TB])
            ors = bb("out_rstd", [P, TB])
            ob = bb("out_buf", [P, 2, TB, D])

            w_split_hi = bsig("w_split_hi", NW)
            w_split_lo = bsig("w_split_lo", NW)
            b1_set = bsig("b1_set")
            li_in = bsig("li_in", 16)
            hg_in = bsig("hg_in", 32)
            T_ps = bsig("T_ps")
            hT_sb = bsig("hT_sb_e", KC)
            h_hi = bsig("h_hi_set")
            h_lo = bsig("h_lo_set")
            up_ps = bsig("up_ps", FT)
            mid_sb = bsig("mid_sb", FT)
            mid_hi = bsig("mid_hi_set", FT)
            mid_lo = bsig("mid_lo_set", FT)
            mid_used = bsig("mid_used", FT)
            y_sb = bsig("y_sb", 2)
            lis_in = bsig("lis_in", 16)
            sc_done = bsig("sc_done", 32)
            r_in = [bsig(f"r_in_{j}", 16) for j in range(2)]
            o_st = bsig("o_st", TB)
            o_mv = bsig("o_mv", TB)
            o_ve = bsig("o_ve")
            o_rstd = bsig("o_rstd")
            o_out = bsig("o_out", TB)
            stored = [bsig(f"stored_{j}", 16) for j in range(2)]
            all_scattered = bsig("all_scattered")
            block = back.enter_context(nc.Block())

            def w1_of(w, j):
                return w[:, j, 0:KC * F].rearrange("p (k f) -> p k f", k=KC)

            def w2_of(w, j):
                return w[:, j, KC * F:].rearrange("p (f d) -> p f d", f=FT)

            def experts(eng, run):
                with eng.Fori(0, E // 2 - 1) as half:
                    for j in range(2):
                        run(half * 2 + j, j, False)
                for j in range(2):
                    run(E - 2 + j, j, j == 1)

            def tiles_of(eng, e):
                mine = eng.value_load(tiles[0:1, 0, bass.ds(e, 1)], min_val=2, max_val=CAP // TE)
                before = eng.value_load(tiles[0:1, 1, bass.ds(e, 1)], min_val=0, max_val=E * CAP // TE)
                return mine, before

            def list_part(e, k):
                return lists[bass.ds(e * CAP + k * TE, TE), :].rearrange("(h p) c -> p h c", p=P)

            @block.sync
            def _(sp):
                sp.dma_start(lis[:, :, :], unused_in[0:TE, :].rearrange("(h p) c -> p h c", p=P)).then_inc(lis_in.sem, 16)
                sp.wait_ge(w_split_lo.sem, w_split_lo.at(0))
                load_expert(sp, 1)

                def expert(e, j, last):
                    mine, before = tiles_of(sp, e)
                    if not (last or isinstance(e, int)):
                        sp.wait_ge(w_split_lo.sem, w_split_lo.at(e + 1))
                        load_expert(sp, e + 2)
                    with sp.Fori(0, mine) as k:
                        sp.wait_ge(sc_done.sem, sc_done.at(before + k + 1))
                        sp.dma_start(lis[:, :, :], list_part(e, k)).then_inc(lis_in.sem, 16)

                experts(sp, expert)
                sp.wait_ge(all_scattered.sem, 1)
                for j in range(2):
                    sp.nop().then_inc(stored[j].sem, 16)
                with sp.Fori(0, NBLK // 2) as i:
                    for j in range(2):
                        sp.wait_ge(stored[j].sem, stored[j].at(i))
                        sp.dma_start(rt[:, j], r_rows[bass.ds(i * 2 * BLK + j * BLK, BLK), :].rearrange("(t p) d -> p t d", p=P)).then_inc(r_in[j].sem, 16)
                for j in range(2):
                    sp.wait_ge(stored[j].sem, 16 * NBLK // 2 + 16)

            @block.gpsimd
            def _(pool):
                pool.memset(y[:, :, :], 0.0).then_inc(y_sb.sem, 2)
                pool.nop().then_inc(T_ps.sem, 1)
                pool.wait_ge(y_sb.sem, 2)
                pool.wait_ge(lis_in.sem, 16)
                for h in range(2):
                    pool.indirect_dma_start(r_rows, bass.IndirectOffsetOnAxis(lis[:, h, 0:1], 0), y[:, h, :], None,
                                            compute_op=ALU.add).then_inc(sc_done.sem, 16)

                def load_rows(e, k, n):
                    wait_apart(pool, (T_ps.sem, T_ps.at(n)))
                    pool.dma_start(li[:, :, :], list_part(e, k)).then_inc(li_in.sem, 16)
                    wait_apart(pool, (li_in.sem, li_in.at(n)))
                    for h in range(2):
                        pool.indirect_dma_start(hg[:, h, :], None, h_rows, bass.IndirectOffsetOnAxis(li[:, h, 0:1], 0)).then_inc(hg_in.sem, 16)

                def add_rows(n):
                    wait_apart(pool, (y_sb.sem, y_sb.at(n)), (lis_in.sem, lis_in.at(n)), (sc_done.sem, sc_done.at(n)))
                    for h in range(2):
                        pool.indirect_dma_start(r_rows, bass.IndirectOffsetOnAxis(lis[:, h, 0:1], 0), y[:, h, :], None,
                                                compute_op=ALU.add).then_inc(sc_done.sem, 16)

                def expert(e, j, last):
                    mine, before = tiles_of(pool, e)
                    with pool.Fori(0, mine) as k:
                        load_rows(e, k, before + k)
                        add_rows(before + k)
                    if last:
                        load_rows(0, 0, before + mine)
                        add_rows(before + mine)
                        wait_apart(pool, (sc_done.sem, sc_done.at(before + mine + 1)), (hg_in.sem, hg_in.at(before + mine)))
                        pool.memset(ors[:, :], 0.0).then_inc(all_scattered.sem, 1)

                experts(pool, expert)
                pool.wait_ge(all_scattered.sem, 1)
                with pool.Fori(0, NBLK) as i:
                    pool.wait_ge(o_ve.sem, o_ve.at(i))
                    pool.tensor_tensor(ors[:, :], ove[:, :], eps_t[:, :], ALU.pow).then_inc(o_rstd.sem, 1)

            @block.scalar
            def _(act):
                act.nop().then_inc(mid_sb.sem, RING)

                def split_hi(e, j, c):
                    act.activation(whi[:, j, c * WC:(c + 1) * WC], raw[:, c * WC:(c + 1) * WC], ACT.Copy).then_inc(w_split_hi.sem, 1)

                def h_out_of_psum(n):
                    act.wait_ge(T_ps.sem, T_ps.at(n) + 1)
                    for kc in range(KC):
                        act.activation(hT[:, kc, :], ps[:, 4, kc * TE:(kc + 1) * TE], ACT.Identity, bias=cols[:, COLS.index("b2"), kc:kc + 1],
                                       scale=cols[:, COLS.index("g2"), kc:kc + 1]).then_inc(hT_sb.sem, 1)

                act.wait_ge(w_in.sem, w_in.at(0))
                for c in range(NW):
                    split_hi(0, 0, c)
                h_out_of_psum(0)

                def tile(n, j, split=None):
                    for f in range(FT):
                        act.wait_ge(up_ps.sem, up_ps.at(n, f + 1))
                        act.wait_ge(mid_lo.sem, mid_lo.at(n, f + 1))
                        act.activation(mid[:, f % RING, :], ps[:, f % RING, 0:TE], ACT.Gelu, bias=b1e[:, j, f:f + 1]).then_inc(mid_sb.sem, 1)
                        if split:
                            split(f)
                    h_out_of_psum(n + 1)

                def expert(e, j, last):
                    mine, before = tiles_of(act, e)
                    act.activation(b1e[:, j, :], eb1[:, bass.ds(e, 1), :].rearrange("p o f -> p (o f)"), ACT.Copy).then_inc(b1_set.sem, 1)
                    act.wait_ge(b1_set.sem, b1_set.at(e))
                    if last:
                        tile(before, j)
                    else:
                        act.wait_ge(w_in.sem, w_in.at(e + 1))
                        act.wait_ge(mid_used.sem, before * FT + RING)
                        tile(before, j, lambda c: split_hi(e + 1, 1 - j, c))
                    with act.Fori(1, mine) as k:
                        tile(before + k, j)

                experts(act, expert)
                with act.Fori(0, NBLK // 2) as i:
                    for j in range(2):
                        act.wait_ge(o_out.sem, i * 2 * TB + (j + 1) * TB)
                        act.dma_start(out[bass.ds(i * 2 * TB + j * TB, TB)].rearrange("t p d -> p t d"), ob[:, j]).then_inc(stored[j].sem, 16)

            @block.vector
            def _(dve):
                dve.nop().then_inc(mid_lo.sem, RING)

                def split_lo(e, j, c):
                    dve.wait_ge(w_split_hi.sem, w_split_hi.at(e, c + 1))
                    w = slice(c * WC, (c + 1) * WC)
                    dve.tensor_tensor(wlo[:, j, w], raw[:, w], whi[:, j, w].bitcast(F32), ALU.subtract).then_inc(w_split_lo.sem, 1)

                def split_h(n):
                    dve.wait_ge(hT_sb.sem, hT_sb.at(n))
                    dve.tensor_copy(hh[:, :, :], hT[:, :, :]).then_inc(h_hi.sem, 1)
                    dve.wait_ge(h_hi.sem, h_hi.at(n))
                    dve.tensor_tensor(hl[:, :, :], hT[:, :, :], hh[:, :, :].bitcast(F32), ALU.subtract).then_inc(h_lo.sem, 1)

                for c in range(NW):
                    split_lo(0, 0, c)
                split_h(0)

                def tile(n, split=None):
                    for f in range(FT):
                        dve.wait_ge(mid_sb.sem, mid_sb.at(n, f + 1) + RING)
                        dve.wait_ge(mid_used.sem, mid_used.at(n, f + 1))
                        dve.tensor_copy(midh[:, f % RING, :], mid[:, f % RING, :]).then_inc(mid_hi.sem, 1)
                        dve.wait_ge(mid_hi.sem, mid_hi.at(n, f + 1))
                        dve.tensor_tensor(midl[:, f % RING, :], mid[:, f % RING, :], midh[:, f % RING, :].bitcast(F32),
                                          ALU.subtract).then_inc(mid_lo.sem, 1)
                        if split and f:
                            split(f - 1)
                    split_h(n + 1)
                    if split:
                        split(FT - 1)
                    dve.wait_ge(mid_used.sem, mid_used.at(n) + RING)
                    dve.wait_ge(lis_in.sem, lis_in.at(n + 1))
                    for h in range(2):
                        dve.tensor_scalar(y[:, h, :], ps[:, 5, h * D:(h + 1) * D], lis[:, h, 1:2].bitcast(F32), None,
                                          ALU.mult).then_inc(y_sb.sem, 1)

                def expert(e, j, last):
                    mine, before = tiles_of(dve, e)
                    tile(before, None if last else lambda c: split_lo(e + 1, 1 - j, c))
                    with dve.Fori(1, mine) as k:
                        tile(before + k)

                experts(dve, expert)
                with dve.Fori(0, NBLK // 2) as i:
                    for j in range(2):
                        k = i * 2 + j
                        dve.wait_ge(r_in[j].sem, r_in[j].at(i))
                        for t in range(TB):
                            dve.bn_stats(ost[:, t, :], rt[:, j, t, :]).then_inc(o_st.sem, 1)
                        for t in range(TB):
                            wait_apart(dve, (o_st.sem, o_st.at(k, t + 1)))
                            dve.bn_aggr(omv[:, t, :], ost[:, t, :]).then_inc(o_mv.sem, 1)
                        dve.wait_ge(o_mv.sem, o_mv.at(k))
                        dve.tensor_scalar(ove[:, :], omv[:, :, 1], EPS, None, ALU.add).then_inc(o_ve.sem, 1)
                        dve.wait_ge(o_rstd.sem, o_rstd.at(k))
                        dve.wait_ge(stored[j].sem, stored[j].at(i))
                        for t in range(TB):
                            dve.tensor_scalar(ob[:, j, t, :], rt[:, j, t, :], omv[:, t, 0:1], ors[:, t:t + 1], ALU.subtract, ALU.mult).then_inc(o_out.sem, 1)

            @block.tensor
            def _(pe):
                pe.nop().then_inc(mid_used.sem, RING)

                def turn(n):
                    pe.wait_ge(hg_in.sem, hg_in.at(n))
                    for h in range(2):
                        for kc in range(KC):
                            ins = pe.transpose(ps[:, 4, kc * TE + h * P:kc * TE + (h + 1) * P], hg[:, h, kc * P:(kc + 1) * P], ident[:, :])
                    ins.then_inc(T_ps.sem, 1)

                turn(0)

                def tile(n, j):
                    def up(f):
                        pe.wait_ge(mid_sb.sem, mid_sb.at(n, f + 1))
                        fs = slice(f * P, (f + 1) * P)
                        terms = ((w1_of(whi, j), hh), (w1_of(wlo, j), hh), (w1_of(whi, j), hl))
                        for i, (w, h) in enumerate(terms):
                            for kc in range(KC):
                                ins = pe.matmul(ps[:, f % RING, 0:TE], w[:, kc, fs], h[:, kc, :],
                                                start=(i == 0 and kc == 0), stop=(i == 2 and kc == KC - 1))
                        ins.then_inc(up_ps.sem, 1)

                    def down(f):
                        pe.wait_ge(mid_lo.sem, mid_lo.at(n, f + 1) + RING)
                        if f == 0:
                            pe.wait_ge(y_sb.sem, y_sb.at(n))
                        for h in range(2):
                            hs = slice(h * P, (h + 1) * P)
                            terms = ((midh, w2_of(whi, j)), (midh, w2_of(wlo, j)), (midl, w2_of(whi, j)))
                            for i, (m, w) in enumerate(terms):
                                ins = pe.matmul(ps[:, 5, h * D:(h + 1) * D], m[:, f % RING, hs], w[:, f, :],
                                                start=(f == 0 and i == 0 and h == 0), stop=(f == FT - 1 and i == 2),
                                                skip_group_check=True)
                        ins.then_inc(mid_used.sem, 1)

                    pe.wait_ge(h_lo.sem, h_lo.at(n))
                    LEAD = 3
                    for f in range(LEAD):
                        up(f)
                    for f in range(FT):
                        if f + LEAD < FT:
                            up(f + LEAD)
                        if f + LEAD == FT:
                            turn(n + 1)
                        down(f)

                def expert(e, j, last):
                    mine, before = tiles_of(pe, e)
                    wait_apart(pe, (w_split_lo.sem, w_split_lo.at(e)))
                    with pe.Fori(0, mine) as k:
                        tile(before + k, j)

                experts(pe, expert)


def kernel(**inputs):
    import numpy as np
    import concourse.bacc as bacc
    from concourse import mybir as mb
    from concourse.bass_utils import run_bass_kernel_spmd as run

    g = {k: np.asarray(v) for k, v in inputs.items()}
    f32 = np.float32
    a, xa, ff = "L0_attn_", "L0_xattn_", "L0_ffn_"
    halves = np.arange(D) // HD % 2
    w_sim = g[xa + "w_sim"]
    vec = {
        "bq": g[a + "bq"], "bk": g[a + "bk"], "gamma": g[a + "gamma"], "beta": g[a + "beta"],
        "w1": w_sim[:D], "w2": w_sim[D:2 * D], "w3": w_sim[2 * D:],
        "g1": g[ff + "ln1_g"], "b1": g[ff + "ln1_b"], "g2": g[ff + "ln2_g"], "b2": g[ff + "ln2_b"],
        "fbq": g[ff + "bq"], "fbk": g[ff + "bk"],
        "even": (halves == 0).astype(f32), "odd": (halves == 1).astype(f32),
    }
    cols = np.stack([vec[n].reshape(KC, P) for n in COLS]).transpose(2, 0, 1)
    rvec = {"bv": g[a + "bv"], "bqa": g[a + "bqa"], "bka": g[a + "bka"], "bqv": g[xa + "b_qv"],
            "fbv": g[ff + "bv"], "bo": g[ff + "bo"], "br": g[ff + "br"], "bs": g[xa + "b_sim"]}
    rows = np.broadcast_to(np.concatenate([rvec[n] for n in ROWS]), (P, sum(ROWS.values())))
    Wf = g[xa + "W_qv"]
    mat = {"Wq": g[a + "Wq"], "Wqa": g[a + "Wqa"], "Wk": g[a + "Wk"], "Wka": g[a + "Wka"], "Wv": g[a + "Wv"],
           "fWq": g[ff + "Wq"], "fWk": g[ff + "Wk"], "fWv": g[ff + "Wv"], "fWo": g[ff + "Wo"]}
    for i in range(4):
        mat[f"Wf{i}"] = Wf[i * D:(i + 1) * D]
    mats = np.stack([mat[n] for n in MATS])
    ident = np.eye(P, dtype=f32)
    t = np.arange(P)
    le = t[:, None] <= t[None, :]
    tri = np.stack([le / (t + 1.0), np.ones((P, P)) / (t + P + 1.0), le / (t + P + 1.0)], 1).astype(f32)
    mask = np.zeros((P, 2, S), np.dtype(mb.dt.np(mb.dt.bfloat16)))
    mask[:, :, P:] = np.where(t[None, :] > t[:, None], -1e30, 0.0)[:, None, :]
    spare = E * CAP + (np.arange(TB * E)[None, :] * P + t[:, None]).astype(f32)
    start = np.tile(np.arange(E) * CAP, TB)[None, :].astype(f32)
    unused = np.zeros((E * CAP, 2), np.int32)
    unused[:, 0] = T + np.arange(E * CAP) % PAD
    arrays = {
        "x": g["x"].reshape(NT, P, D), "ctx": g["ctx_1024"], "mats": mats, "cols": cols, "rows": rows,
        "wr": g[ff + "Wr"], "ident": ident, "tri": tri, "mask": mask,
        "lower": (t[:, None] < t[None, :]).astype(mask.dtype), "slots": np.stack([spare, start - spare], 1),
        "ids": (t[:, None] + P * np.arange(TB)[None, :]).astype(f32), "unused": unused, "zeros": np.zeros((PAD, D), f32),
        "w1": g[ff + "e_w1"], "w2": g[ff + "e_w2"],
        "eb1": g[ff + "e_b1"].reshape(E, FT, P).transpose(2, 0, 1), "eb2": g[ff + "e_b2"],
    }
    arrays = {k: np.ascontiguousarray(v) for k, v in arrays.items()}
    nc = bacc.Bacc("TRN2", target_bir_lowering=False, num_devices=1)
    args = [nc.dram_tensor(k, v.shape, mb.dt.from_np(v.dtype), kind="ExternalInput").ap() for k, v in arrays.items()]
    args.append(nc.dram_tensor("out", (NT, P, D), F32, kind="ExternalOutput").ap())
    decoder_kernel(nc, *args)
    r = run(nc, [arrays], core_ids=[0])
    return r.results[0]["out"].reshape(B, S, D)
```

```python
from contextlib import ExitStack

import concourse.bass as bass
from concourse import mybir

F32 = mybir.dt.float32
F32R = mybir.dt.float32r
I32 = mybir.dt.int32
BF16 = mybir.dt.bfloat16
ALU = mybir.AluOpType
ACT = mybir.ActivationFunctionType
AX = mybir.AxisListType

P = 128
B, S, D = 16, 256, 256
T = B * S
NT = T // P
TB = 4
BLK = TB * P
NBLK = T // BLK
SB = BLK // S
KC = D // P
C = 120
H, HD = 16, 16
E, F = 8, 1024
FT = F // P
EPS = 1e-5
TE = 256
PAD = TE
CAP = T
SPARE = TB * E * P

COLS = ["bq", "bk", "gamma", "beta", "w2", "w3", "g1", "b1", "g2", "b2", "fbq", "fbk", "even", "odd"]
ROWS = {"bv": D, "bqa": D, "bka": D, "bqv": D, "fbv": D, "bo": D, "br": E, "bs": 1, "w1": D}
MATS = ["Wq", "Wk", "Wv", "Wqa", "Wka", "Wf0", "Wf1", "Wf2", "Wf3", "fWq", "fWk", "fWv", "fWo"]
N_GATED = 5


class Count:

    def __init__(self, sem, per):
        self.sem, self.per = sem, per

    def at(self, it, k=None):
        return it * self.per + (self.per if k is None else k)


class Woven:

    def __init__(self, *parts):
        self.steps = (step for part in parts for step in part)
        self.next = next(self.steps, None)

    def through(self, step):
        while self.next is not None and self.next <= step:
            self.next = next(self.steps, None)


def decoder_kernel(nc, x, ctx_in, mats_in, cols_in, rows_in, wr_in, ident_in, tri_in, mask_in, lower_in,
                   slots_in, ids_in, unused_in, zeros_in, w1_in, w2_in, eb1_in, eb2_in, out):
    with ExitStack() as stack:
        def sb(name, shape, dt=F32):
            return stack.enter_context(nc.sbuf_tensor(name, shape, dt))

        def signal(name, per=1):
            return Count(stack.enter_context(nc.semaphore(name)), per)

        ps = stack.enter_context(nc.psum_tensor("ps", [P, 8, 512], F32))

        def wait_apart(eng, *waits):
            waits = [(sem, value if isinstance(value, int) else eng.to_reg(value)) for sem, value in waits]
            eng.wait_ge(c_loaded.sem, 16)
            for sem, value in waits:
                eng.wait_ge(sem, value)

        def scatter(pool, js, sem):
            for j in js:
                pool.indirect_dma_start(lists, bass.IndirectOffsetOnAxis(dst[:, j:j + 1], 0), pairs[:, j, :], None).then_inc(sem, 16)

        def tile_of(bank, t):
            return ps[:, bank + t // 2, (t % 2) * D:(t % 2 + 1) * D]

        h_rows = nc.dram_tensor("h_rows", (T + PAD, D), F32, kind="Internal").ap()
        r_rows = nc.dram_tensor("r_rows", (T + PAD, D), F32, kind="Internal").ap()
        lists = nc.dram_tensor("lists", (E * CAP + SPARE, 2), I32, kind="Internal").ap()

        cols = sb("cols_sb", [P, len(COLS), KC])
        ident = sb("ident_sb", [P, P])
        raw = sb("raw_weights", [P, KC * F + FT * D])
        tiles = sb("tiles", [1, 2, E], I32)
        dst = sb("slot", [P, TB * E], I32)
        pairs = sb("pairs", [P, TB * E, 2], I32)
        raw_b2 = sb("raw_b2", [P, D])
        w_in = signal("w_in", 48)
        eb1 = sb("expert_b1", [P, E, FT])

        c_loaded = signal("consts_loaded", 16)
        rest_loaded = signal("rest_loaded", 16)
        eps_t = sb("eps_half", [P, TB])

        def load_expert(sp, e):
            sp.dma_start(raw[:, 0:KC * F].rearrange("p (k f) -> p k f", k=KC),
                         w1_in[bass.ds(e, 1)].rearrange("o (k p) f -> p (o k) f", p=P)).then_inc(w_in.sem, 16)
            sp.dma_start(raw[:, KC * F:].rearrange("p (f d) -> p f d", f=FT),
                         w2_in[bass.ds(e, 1)].rearrange("o (f p) d -> p (o f) d", p=P)).then_inc(w_in.sem, 16)
            sp.dma_start(raw_b2[:, :], eb2_in[bass.ds(e, 1)].rearrange("o p d -> p (o d)")).then_inc(w_in.sem, 16)

        with ExitStack() as front:
            def fb(name, shape, dt=F32):
                return front.enter_context(nc.sbuf_tensor(name, shape, dt))

            def fsig(name, per=1):
                return Count(front.enter_context(nc.semaphore(name)), per)

            mats = fb("mats_sb", [P, len(MATS), KC, D])
            rows = fb("rows_sb", [P, sum(ROWS.values())])
            wr = fb("wr_sb", [P, KC, E])
            identb = fb("identb", [P, P], BF16)
            tri = fb("tri_sb", [P, 3, P])
            mask = fb("mask_sb", [P, 1, P], BF16)
            ones = fb("ones", [P, P])
            qscale = fb("qscale", [P, 2, KC])
            qbias = fb("qbias", [P, 2, KC])

            W = {n: mats[:, i] for i, n in enumerate(MATS)}
            col = {n: (lambda kc, i=i: cols[:, i, kc:kc + 1]) for i, n in enumerate(COLS)}
            row, at = {}, 0
            for n, w in ROWS.items():
                row[n] = rows[:, at:at + w]
                at += w

            def over_tiles(r, n=TB):
                w = r.shape[1]
                return r.rearrange("p (o d) -> p o d", o=1).to_broadcast([P, n, w])

            xt = fb("x_tok", [P, TB, D])
            lg = fb("logits", [P, TB, D])
            pt = fb("exp_logits", [P, TB, D])
            hn = fb("hn_tok", [P, TB, D])
            hT = fb("hT", [P, KC, BLK])
            qT = fb("qT", [P, KC, BLK])
            kT = fb("kT", [P, KC, BLK])
            vt = fb("v_tok", [P, TB, D])
            wt = fb("w_tok", [P, TB, D])
            x1 = fb("x1_tok", [P, TB, D])
            mx = fb("max4", [P, TB])
            nm = fb("negmax4", [P, TB])
            sm = fb("sum4", [P, TB])
            rs = fb("rsum4", [P, TB])
            x1T = fb("x1T", [P, KC, BLK])
            Wx = fb("Wx", [P, SB, KC, D])
            x1b = fb("x1_bias", [P, TB, D])
            ctx = fb("ctx_tok", [C, SB, D])
            chn = fb("cross_hn", [P, TB, D])
            chT = fb("cross_hT", [P, KC, BLK])
            hqT = fb("hqT", [P, KC, BLK])
            xhT = fb("x1_hqT", [P, KC, BLK])
            cp = fb("cross_exp", [P, TB, C])
            cw = fb("cross_weights", [P, TB, C])
            x2 = fb("x2_tok", [P, TB, D])
            AT = fb("AT", [C, BLK])
            cT = fb("cT", [P, KC, SB * C])
            cmx = fb("cross_max", [P, TB])
            xw1 = fb("x1_times_w1", [P, TB, D])
            c1 = fb("x1_dot_w1", [P, TB])
            cnm = fb("cross_negmax", [P, TB])
            csm = fb("cross_sum", [P, TB])
            crs = fb("cross_rsum", [P, TB])
            bm = fb("b_rowmax", [P, TB])
            bg = fb("b_seqmax", [1, SB])
            bd = fb("b_diff", [P, TB])
            be = fb("b_exp", [P, TB])
            hcr = fb("hc_recip", [P, SB])
            hc = fb("hc", [P, SB, KC])
            qz = fb("q_even_odd", [P, 2, KC, BLK])
            skT = fb("self_kT", [P, KC, BLK])
            sv = fb("self_v", [P, TB, D])
            p2 = fb("exp_scores", [P, 2, 512])
            PT = fb("PT", [P, 3, 512])
            ot = fb("o_tok", [P, TB, D])
            nm4 = fb("negmax_heads", [P, 2, 4])
            mx4 = fb("max_heads", [P, 2, 4])
            sm16 = fb("sum16", [P, TB, H])
            rs16 = fb("rsum16", [P, H])
            xb = fb("x2_bias", [P, TB, D])
            xr = fb("x2_kept", [P, TB, D])
            oT = fb("oT", [P, KC, BLK])
            at_ = fb("a_tok", [P, TB, D])
            h2n = fb("h2n_tok", [P, TB, D])
            h2T = fb("h2T", [P, KC, BLK])
            xa = fb("x2_plus_a", [P, TB, D])
            rl = fb("router_logits", [P, TB, E])
            rt8 = fb("router_sorted", [P, TB, 8])
            rnm = fb("router_negmax", [P, TB])
            rsm = fb("router_sum", [P, TB])
            rrs = fb("router_rsum", [P, TB])
            rex = fb("router_exp", [P, TB, E])
            rw = fb("router_w", [P, TB, E])
            lower = fb("lower_sb", [P, P], BF16)
            onesb = fb("ones_bf16", [P, P], BF16)
            slots = fb("slots_sb", [P, 2, TB * E])
            ids = fb("ids_sb", [P, TB])
            rm = fb("router_mask", [P, TB, E], BF16)
            taken = fb("taken", [P, E])
            d1 = fb("slot_1", [P, TB * E])
            d2 = fb("slot_2", [P, TB * E])
            d3 = fb("slot_3", [P, TB * E])
            cf = fb("counts", [1, 3, E])
            ci = fb("counts_int", [1, 2, E], I32)

            class Norm:

                def __init__(self, name, n):
                    self.parts = fb(name + "_parts", [P, TB, 6])
                    self.mv = fb(name + "_mean_var", [P, TB, 2])
                    self.ve = fb(name + "_var_eps", [P, TB])
                    self.rstd = fb(name + "_rstd", [P, TB])
                    self.stat_done = fsig(name + "_stat_done", n * TB)
                    self.mv_done = fsig(name + "_mv_done", n * TB)
                    self.ve_done = fsig(name + "_ve_done", n)
                    self.rstd_done = fsig(name + "_rstd_done", n)
                    self.out = fsig(name + "_out", n * TB)

            ln = Norm("ln", 2)
            lnc = Norm("lnc", 2)
            ln2 = Norm("ln2", 1)

            consts = fsig("front_consts")
            pool_consts = fsig("pool_consts")
            x_in = fsig("x_in", 16)
            ctx_in_ = fsig("ctx_in", 16)
            HV = 2
            hT_ps = fsig("hT_ps", KC)
            hT_sb = fsig("hT_sb", KC)
            q_ps = fsig("q_ps", KC)
            k_ps = fsig("k_ps", KC)
            v_ps = fsig("v_ps", HV)
            qT_sb = fsig("qT_sb", KC)
            kT_sb = fsig("kT_sb", KC)
            v_sb = fsig("v_sb", HV)
            tok_ps = fsig("tok_ps", 2 * HV)
            lg_ps = fsig("lg_ps", 2 * HV)
            lg_sb = fsig("lg_sb", 2 * TB)
            lg_nm = fsig("lg_nm", 2)
            p_sb = fsig("p_sb", 2 * TB)
            p_rs = fsig("p_rs", 2)
            w_sb = fsig("w_sb", 2 * TB)
            pool_ps = fsig("pool_ps", KC)
            mT_sb = fsig("mT_sb", KC)
            pk_ps = fsig("pk_ps", HV)
            a_mul = fsig("a_mul", HV)
            a_sum = fsig("a_sum")
            x1b_sb = fsig("x1b_sb")
            x1T_ps = fsig("x1T_ps", KC)
            cT_ps = fsig("cT_ps")
            x1T_sb = fsig("x1T_sb", KC)
            cT_sb = fsig("cT_sb")
            xwT_sb = fsig("xwT_sb", KC)
            c1_sb = fsig("c1_sb", TB)
            sim_ps = fsig("sim_ps")
            sim_mx = fsig("sim_mx")
            sim_nm = fsig("sim_nm", 2)
            bp_sb = fsig("bp_sb", TB)
            bp_rs = fsig("bp_rs")
            A_sb = fsig("A_sb", TB)
            AT_ps = fsig("AT_ps")
            mrow_ps = fsig("mrow_ps")
            AT_sb = fsig("AT_sb")
            g_sb = fsig("g_sb")
            g_ps = fsig("g_ps")
            bd_sb = fsig("bd_sb", SB)
            be_sb = fsig("be_sb")
            hq_ps = fsig("hq_ps", KC)
            hqT_sb = fsig("hqT_sb", KC)
            xhT_sb = fsig("xhT_sb")
            hc_ps = fsig("hc_ps")
            hc_rs = fsig("hc_rs")
            hc_sb = fsig("hc_sb", SB)
            Wx_sb = fsig("Wx_sb", SB * KC)
            hcq_ps = fsig("hcq_ps", HV)
            b_sum = fsig("b_sum", HV)
            shT_ps = fsig("self_hT_ps", KC)
            shT_sb = fsig("self_hT_sb", KC)
            sq_ps = fsig("self_q_ps", KC)
            sk_ps = fsig("self_k_ps", KC)
            sv_ps = fsig("self_v_ps", HV)
            skT_sb = fsig("self_kT_sb", KC)
            sv_sb = fsig("self_v_sb", HV)
            qz_sb = fsig("qz_sb", 2 * KC)
            G = sum(4 * (t % 2 + 1) for t in range(TB))
            BY_ACT = sum(4 for t in range(TB) if t % 2)
            s_ps = fsig("s_ps", G)
            s_mx = fsig("s_mx", G)
            s_nm = fsig("s_nm", G)
            s_p = fsig("s_p", G)
            pT_ps = fsig("pT_ps", G)
            pT0_sb = fsig("pT0_sb", G - BY_ACT)
            pT1_sb = fsig("pT1_sb", BY_ACT)
            pT_used = fsig("pT_used", G)
            o_rs = fsig("o_rs", TB)
            o_sb = fsig("o_sb", TB)
            kept = fsig("kept", 2)
            oT_ps = fsig("oT_ps", KC)
            oT_sb = fsig("oT_sb", KC)
            ao_ps = fsig("ao_ps", HV)
            c_sum = fsig("c_sum", HV)
            h2T_ps = fsig("h2T_ps", KC)
            h2T_sb = fsig("h2T_sb", KC)
            rl_ps = fsig("rl_ps")
            rl_sb = fsig("rl_sb")
            rl_max = fsig("rl_max", TB)
            rl_nm = fsig("rl_nm")
            rl_exp = fsig("rl_exp", TB)
            rl_w = fsig("rl_w", TB)
            rl_rs = fsig("rl_rs")
            rl_out = fsig("rl_out")
            acc_xa = fsig("acc_xa")
            h_out = fsig("h_out", 16)
            r_out = fsig("r_out", 16)
            rm_sb = fsig("rm_sb", TB)
            pos_ps = fsig("pos_ps")
            pos_sb = fsig("pos_sb", 2)
            slot_a = fsig("slot_a")
            slot_b = fsig("slot_b")
            listed = fsig("listed", 4)
            lists_set = fsig("lists_set", 48)
            scattered = fsig("scattered", 16 * TB * E)
            lists_free = fsig("lists_free")
            counted = fsig("counted")

            block = front.enter_context(nc.Block())

            X, Y = 4, 6
            GATED, ROUTE, X_END = 5, 30, 37
            CROSS, Y_END = 39, 67
            SLOTS = 3 * (G + 2)
            PACE = 1.2

            def cross_step(slot):
                free = SLOTS - 8
                if slot < free:
                    return CROSS + (62 - CROSS) * (slot + 1) // free - 1
                return Y_END - 1 if slot == SLOTS - 1 else min(62 + slot - free, Y_END - 2)

            def blocks(eng, attention, project, route, gated, cross):
                def one_pass(it, has_attention=True, has_behind=True, has_gated=True, has_cross=True):
                    parts = ([project(it - 1)] if has_behind else []) + ([gated(it + 2, has_behind)] if has_gated else [])
                    at_x = Woven(*parts + ([route(it - 1)] if has_behind else []))
                    at_y = Woven(*[cross(it + 1)] if has_cross else [])
                    steps = [n for n in range(X_END) if (has_behind if n < GATED or n >= ROUTE else has_gated)]
                    for slot, _ in enumerate(attention(it) if has_attention else no_attention(it)):
                        at_y.through(cross_step(slot))
                        done = int(len(steps) * ((slot + 1) / SLOTS) ** PACE + 1e-9)
                        if done:
                            at_x.through(steps[done - 1])

                one_pass(-2, has_attention=False, has_behind=False, has_cross=False)
                eng.wait_ge(rest_loaded.sem, 16 * NREST)
                eng.wait_ge(lists_set.sem, 48)
                one_pass(-1, has_attention=False, has_behind=False)
                one_pass(0, has_behind=False)
                with eng.Fori(1, NBLK - 2) as it:
                    one_pass(it)
                one_pass(NBLK - 2, has_gated=False)
                one_pass(NBLK - 1, has_gated=False, has_cross=False)
                one_pass(NBLK, has_attention=False, has_gated=False, has_cross=False)

            def no_attention(it):
                for _ in range(SLOTS):
                    yield

            def stats(eng, norm, b, n, src):
                per = norm.out.per
                for t in range(TB):
                    eng.bn_stats(norm.parts[:, t, :], src[:, t, :]).then_inc(norm.stat_done.sem, 1)
                for t in range(TB):
                    wait_apart(eng, (norm.stat_done.sem, b * per + n * TB + t + 1))
                    eng.bn_aggr(norm.mv[:, t, :], norm.parts[:, t, :]).then_inc(norm.mv_done.sem, 1)
                eng.wait_ge(norm.mv_done.sem, b * per + n * TB + TB)
                eng.tensor_scalar(norm.ve[:, :], norm.mv[:, :, 1], EPS, None, ALU.add).then_inc(norm.ve_done.sem, 1)

            def normalize(eng, norm, b, n, src, dst):
                eng.wait_ge(norm.rstd_done.sem, norm.rstd_done.at(b, n + 1))
                for t in range(TB):
                    eng.tensor_scalar(dst[:, t, :], src[:, t, :], norm.mv[:, t, 0:1], norm.rstd[:, t:t + 1],
                                      ALU.subtract, ALU.mult).then_inc(norm.out.sem, 1)

            PORTIONS = [(t, (h, h + 1, h + 8, h + 9), 1) if t % 2 == 0 else (t, (h, h + 1), 2)
                        for t in range(TB) for h in range(0, H // (2 - t % 2), 2)]
            LAST = {t: max(g for g in range(G) if PORTIONS[g][0] == t) for t in range(TB)}

            def by_act(g):
                return PORTIONS[g][2] == 2 and g % 2 == 1

            def in_sbuf(eng, it, g):
                n = sum(by_act(i) for i in range(g))
                if by_act(g):
                    eng.wait_ge(pT1_sb.sem, pT1_sb.at(it, n + 1))
                else:
                    eng.wait_ge(pT0_sb.sem, pT0_sb.at(it, g - n + 1))

            def evacuate(eng, it, g):
                eng.wait_ge(pT_ps.sem, pT_ps.at(it, g + 1))
                if g >= 3:
                    eng.wait_ge(pT_used.sem, pT_used.at(it, g - 2))

            NLOAD = 5 + N_GATED
            NREST = 5 + len(MATS) - N_GATED

            @block.sync
            def _(sp):
                sp.dma_start(cols[:, :, :], cols_in).then_inc(c_loaded.sem, 16)
                sp.dma_start(xt[:, :, :], x[0:TB].rearrange("t p d -> p t d")).then_inc(x_in.sem, 16)
                sp.dma_start(ident[:, :], ident_in).then_inc(c_loaded.sem, 16)
                sp.dma_start(slots[:, :, :], slots_in).then_inc(c_loaded.sem, 16)
                for i in range(len(MATS)):
                    if i == N_GATED:
                        sp.dma_start(tri[:, :, :], tri_in).then_inc(c_loaded.sem, 16)
                        sp.dma_start(rows[:, :], rows_in).then_inc(c_loaded.sem, 16)
                    sp.dma_start(mats[:, i], mats_in[i].rearrange("(k p) n -> p k n", p=P))\
                        .then_inc((c_loaded if i < N_GATED else rest_loaded).sem, 16)
                sp.dma_start(mask[:, :, :], mask_in).then_inc(rest_loaded.sem, 16)
                sp.dma_start(wr[:, :, :], wr_in.rearrange("(k p) n -> p k n", p=P)).then_inc(rest_loaded.sem, 16)
                sp.dma_start(eb1[:, :, :], eb1_in).then_inc(rest_loaded.sem, 16)
                sp.dma_start(lower[:, :], lower_in).then_inc(rest_loaded.sem, 16)
                sp.dma_start(ids[:, :], ids_in).then_inc(rest_loaded.sem, 16)
                sp.dma_start(lists[0:E * CAP, :], unused_in).then_inc(lists_set.sem, 16)
                sp.dma_start(h_rows[T:T + PAD, :], zeros_in).then_inc(lists_set.sem, 16)
                sp.dma_start(r_rows[T:T + PAD, :], zeros_in).then_inc(lists_set.sem, 16)
                sp.dma_start(ctx[:, :, :], ctx_in[0:SB].rearrange("b c d -> c b d")).then_inc(ctx_in_.sem, 16)

                def load_x(b):
                    sp.wait_ge(a_sum.sem, a_sum.at(b - 1))
                    sp.dma_start(xt[:, :, :], x[bass.ds(b * TB, TB)].rearrange("t p d -> p t d")).then_inc(x_in.sem, 16)

                def load_context(b):
                    sp.wait_ge(hq_ps.sem, hq_ps.at(b - 1))
                    sp.dma_start(ctx[:, :, :], ctx_in[bass.ds(b * SB, SB)].rearrange("b c d -> c b d")).then_inc(ctx_in_.sem, 16)

                def store_h(b):
                    sp.wait_ge(ln2.out.sem, ln2.out.at(b))
                    sp.dma_start(h_rows[bass.ds(b * BLK, BLK), :].rearrange("(t p) d -> p t d", p=P), h2n[:, :, :]).then_inc(h_out.sem, 16)

                def store_r(b):
                    sp.wait_ge(acc_xa.sem, acc_xa.at(b))
                    sp.dma_start(r_rows[bass.ds(b * BLK, BLK), :].rearrange("(t p) d -> p t d", p=P), xa[:, :, :]).then_inc(r_out.sem, 16)

                load_x(1)
                load_expert(sp, 0)
                for b in range(1, 3):
                    load_context(b)
                    load_x(b + 1)
                with sp.Fori(1, NBLK - 3) as it:
                    store_h(it - 1)
                    store_r(it - 1)
                    load_context(it + 2)
                    load_x(it + 3)
                store_h(NBLK - 4)
                store_r(NBLK - 4)
                load_context(NBLK - 1)
                for b in range(NBLK - 3, NBLK):
                    store_h(b)
                    store_r(b)
                sp.wait_ge(lists_set.sem, 48)
                sp.wait_ge(h_out.sem, 16 * NBLK)
                sp.wait_ge(r_out.sem, 16 * NBLK)

            @block.gpsimd
            def _(pool):
                pool.memset(onesb[:, :], 1.0).then_inc(pool_consts.sem, 1)
                pool.memset(ones[:, :], 1.0).then_inc(pool_consts.sem, 1)
                pool.memset(eps_t[:, :], -0.5).then_inc(pool_consts.sem, 1)
                pool.wait_ge(pool_consts.sem, 3)
                pool.wait_ge(c_loaded.sem, 16 * NLOAD)

                def root(norm, b, n):
                    pool.wait_ge(norm.ve_done.sem, norm.ve_done.at(b, n + 1))
                    pool.tensor_tensor(norm.rstd[:, :], norm.ve[:, :], eps_t[:, :], ALU.pow).then_inc(norm.rstd_done.sem, 1)

                def enlist(b, a=0, z=TB * E):
                    if a == 0:
                        wait_apart(pool, (listed.sem, listed.at(b + 1, 3)))
                    scatter(pool, range(a, z), scattered.sem)

                def free(b):
                    pool.wait_ge(scattered.sem, scattered.at(b + 1))
                    pool.nop().then_inc(lists_free.sem, 1)

                def keep(b):
                    pool.wait_ge(lnc.out.sem, lnc.out.at(b, TB))
                    if not (isinstance(b, int) and b == 0):
                        pool.wait_ge(acc_xa.sem, acc_xa.at(b - 1))
                    pool.tensor_tensor(xb[:, :, :], x2[:, :, :], over_tiles(row["bo"]), ALU.add).then_inc(kept.sem, 1)
                    pool.tensor_copy(xr[:, :, :], x2[:, :, :]).then_inc(kept.sem, 1)

                def project(b):
                    yield 3
                    root(ln2, b, 0)
                    yield 4
                    pool.wait_ge(kept.sem, kept.at(b))
                    if not (isinstance(b, int) and b == 0):
                        pool.wait_ge(r_out.sem, r_out.at(b - 1))
                    pool.tensor_tensor(xa[:, :, :], at_[:, :, :], xr[:, :, :], ALU.add).then_inc(acc_xa.sem, 1)
                    final = isinstance(b, int) and b == NBLK - 1
                    if not final:
                        keep(b + 1)

                def route(b):
                    yield ROUTE
                    if isinstance(b, int) and b == NBLK - 3:
                        enlist(b - 1)
                        free(b - 1)
                    yield 36
                    if isinstance(b, int) and b < NBLK - 1:
                        enlist(b)
                        free(b)

                def gated(b, has_behind):
                    if isinstance(b, int) and b == 2:
                        keep(0)
                    yield 5
                    root(ln, b, 0)
                    for i in range(16):
                        yield 7 + i
                        if has_behind:
                            enlist(b - 4, 2 * i, 2 * i + 2)
                    yield 27
                    pool.wait_ge(a_mul.sem, a_mul.at(b))
                    pool.tensor_tensor(hn[:, :, :], lg[:, :, :], xt[:, :, :], ALU.add).then_inc(a_sum.sem, 1)
                    yield 28
                    root(ln, b, 1)
                    if has_behind:
                        free(b - 4)

                def cross(b):
                    yield 39
                    pool.wait_ge(ln.out.sem, ln.out.at(b))
                    if not (isinstance(b, int) and b == 0):
                        pool.wait_ge(b_sum.sem, b_sum.at(b - 1))
                    pool.tensor_tensor(x1b[:, :, :], x1[:, :, :], over_tiles(row["bqv"]), ALU.add).then_inc(x1b_sb.sem, 1)
                    yield 55
                    root(lnc, b, 0)
                    yield 57
                    root(lnc, b, 1)

                blocks(pool, no_attention, project, route, gated, cross)

            @block.scalar
            def _(act):
                act.wait_ge(c_loaded.sem, 16 * NLOAD)
                act.wait_ge(consts.sem, 8)

                def scaled(b, ready, bank, dst, scale, shift, done):
                    for kc in range(KC):
                        act.wait_ge(ready.sem, ready.at(b, kc + 1))
                        act.activation(dst[:, kc, :], ps[:, bank + kc, :], ACT.Identity, bias=col[shift](kc),
                                       scale=col[scale](kc)).then_inc(done.sem, 1)

                def shifted(b, ready, bank, dst, bias, done):
                    for mc in range(KC):
                        act.wait_ge(ready.sem, ready.at(b, mc + 1))
                        act.activation(dst[:, mc, :], ps[:, bank + mc, :], ACT.Identity, bias=col[bias](mc)).then_inc(done.sem, 1)

                def feature_exp(b, n):
                    act.wait_ge(lg_nm.sem, lg_nm.at(b, n + 1))
                    for t in range(TB):
                        act.activation(pt[:, t, :], lg[:, t, :], ACT.Exp, bias=nm[:, t:t + 1], scale=D ** -0.5,
                                       accum_out=sm[:, t:t + 1]).then_inc(p_sb.sem, 1)

                def gated(b, has_behind):
                    yield 8
                    scaled(b, hT_ps, X, hT, "gamma", "beta", hT_sb)
                    yield 10
                    shifted(b, q_ps, X, qT, "bq", qT_sb)
                    yield 12
                    shifted(b, k_ps, X, kT, "bk", kT_sb)
                    yield 17
                    feature_exp(b, 0)
                    yield 23
                    feature_exp(b, 1)

                def cross(b):
                    yield 40
                    act.wait_ge(cT_ps.sem, cT_ps.at(b))
                    act.activation(cT[:, :, :], ps[:, Y, 0:KC * SB * C].rearrange("p (k c) -> p k c", k=KC), ACT.Copy).then_inc(cT_sb.sem, 1)
                    act.wait_ge(x1T_ps.sem, x1T_ps.at(b, 1))
                    act.activation(x1T[:, 0, :], ps[:, Y + 1, :], ACT.Copy).then_inc(x1T_sb.sem, 1)
                    yield 42
                    act.wait_ge(x1T_ps.sem, x1T_ps.at(b))
                    act.activation(x1T[:, 1, :], ps[:, Y, :], ACT.Copy).then_inc(x1T_sb.sem, 1)
                    yield 46
                    act.wait_ge(sim_nm.sem, sim_nm.at(b))
                    for t in range(TB):
                        act.activation(cp[:, t, :], ps[:, Y, t * P:t * P + C], ACT.Exp, bias=cnm[:, t:t + 1],
                                       accum_out=csm[:, t:t + 1]).then_inc(bp_sb.sem, 1)
                    yield 49
                    act.wait_ge(AT_ps.sem, AT_ps.at(b))
                    act.activation(AT[:, :], ps[0:C, Y, :], ACT.Copy).then_inc(AT_sb.sem, 1)
                    yield 50
                    act.wait_ge(bd_sb.sem, bd_sb.at(b))
                    act.activation(be[:, :], bd[:, :], ACT.Exp).then_inc(be_sb.sem, 1)
                    yield 51
                    for mc in range(KC):
                        act.wait_ge(hq_ps.sem, hq_ps.at(b, mc + 1))
                        act.activation(hqT[:, mc, :], ps[:, Y + mc, :], ACT.Copy).then_inc(hqT_sb.sem, 1)
                    yield 60
                    scaled(b, shT_ps, Y, chT, "g1", "b1", shT_sb)
                    yield 62
                    for mc in range(KC):
                        act.wait_ge(sq_ps.sem, sq_ps.at(b, mc + 1))
                        for eo in range(2):
                            act.activation(qz[:, eo, mc, :], ps[:, Y + mc, :], ACT.Identity, bias=qbias[:, eo, mc:mc + 1],
                                           scale=qscale[:, eo, mc:mc + 1]).then_inc(qz_sb.sem, 1)
                    yield 64
                    shifted(b, sk_ps, Y, skT, "fbk", skT_sb)

                def attention(it):
                    for g in range(G + 2):
                        yield
                        if g < G:
                            t, heads, nb = PORTIONS[g]
                            L = P * nb
                            act.wait_ge(s_nm.sem, s_nm.at(it, g + 1))
                            if g >= 2:
                                act.wait_ge(pT_ps.sem, pT_ps.at(it, g - 1))
                            for h, head in enumerate(heads):
                                ins = act.activation(p2[:, g % 2, h * L:(h + 1) * L], ps[:, g % 2, h * L:(h + 1) * L], ACT.Exp,
                                                     bias=nm4[:, g % 2, h:h + 1], accum_out=sm16[:, t, head:head + 1])
                            ins.then_inc(s_p.sem, 1)
                        yield
                        if 1 <= g <= G and by_act(g - 1):
                            evacuate(act, it, g - 1)
                            act.activation(PT[:, (g - 1) % 3, :], ps[:, 2, :], ACT.Copy).then_inc(pT1_sb.sem, 1)
                        yield

                def project(b):
                    yield 1
                    for kc in range(KC):
                        act.wait_ge(oT_ps.sem, oT_ps.at(b, kc + 1))
                        act.activation(oT[:, kc, :], ps[:, X + kc, :], ACT.Copy).then_inc(oT_sb.sem, 1)

                def route(b):
                    yield 31
                    scaled(b, h2T_ps, X, h2T, "g2", "b2", h2T_sb)
                    yield 34
                    act.wait_ge(rl_nm.sem, rl_nm.at(b))
                    for t in range(TB):
                        act.activation(rex[:, t, :], rl[:, t, :], ACT.Exp, bias=rnm[:, t:t + 1]).then_inc(rl_exp.sem, 1)

                blocks(act, attention, project, route, gated, cross)

            @block.vector
            def _(dve):
                dve.wait_ge(c_loaded.sem, 16 * NLOAD)
                dve.memset(taken[:, :], 0.0).then_inc(consts.sem, 1)
                dve.tensor_copy(dst[:, :], slots[:, 0, :]).then_inc(listed.sem, 2)
                dve.memset(pairs[:, :, :], 0).then_inc(listed.sem, 2)
                dve.tensor_copy(identb[:, :], ident[:, :]).then_inc(consts.sem, 1)
                for eo, n in enumerate(("even", "odd")):
                    i = COLS.index(n)
                    dve.tensor_scalar(qscale[:, eo, :], cols[:, i, :], HD ** -0.5, None, ALU.mult).then_inc(consts.sem, 1)
                dve.wait_ge(consts.sem, 4)
                for eo in range(2):
                    for kc in range(KC):
                        dve.tensor_tensor(qbias[:, eo, kc:kc + 1], qscale[:, eo, kc:kc + 1], col["fbq"](kc), ALU.mult).then_inc(consts.sem, 1)

                def feature_logits(b, n, bias):
                    for t in range(TB):
                        if t % 2 == 0:
                            wait_apart(dve, (lg_ps.sem, lg_ps.at(b, n * HV + t // 2 + 1)))
                        dve.tensor_tensor_reduce(lg[:, t, :], tile_of(X, t), row[bias], 1.0, -3.0e38, ALU.add, ALU.max,
                                                 mx[:, t:t + 1]).then_inc(lg_sb.sem, 1)
                    dve.wait_ge(lg_sb.sem, lg_sb.at(b, n * TB + TB))
                    dve.tensor_scalar(nm[:, :], mx[:, :], -(D ** -0.5), None, ALU.mult).then_inc(lg_nm.sem, 1)

                def feature_weight(b, n):
                    dve.wait_ge(p_sb.sem, p_sb.at(b, n * TB + TB))
                    dve.reciprocal(rs[:, :], sm[:, :]).then_inc(p_rs.sem, 1)
                    dve.wait_ge(p_rs.sem, p_rs.at(b, n + 1))
                    for t in range(TB):
                        if t % 2 == 0:
                            dve.wait_ge(tok_ps.sem, tok_ps.at(b, n * HV + t // 2 + 1))
                        dve.scalar_tensor_tensor(wt[:, t, :], pt[:, t, :], rs[:, t:t + 1], tile_of(X, t),
                                                 ALU.mult, ALU.mult).then_inc(w_sb.sem, 1)

                def half(bank, i):
                    return ps[:, bank + i, :].rearrange("p (t d) -> p t d", t=2), slice(2 * i, 2 * i + 2)

                def values(b, ready, bank, dst, bias, done):
                    for i in range(HV):
                        dve.wait_ge(ready.sem, ready.at(b, i + 1))
                        v, ts = half(bank, i)
                        dve.tensor_tensor(dst[:, ts, :], v, over_tiles(row[bias], 2), ALU.add).then_inc(done.sem, 1)

                def gated(b, has_behind):
                    yield 5
                    dve.wait_ge(x_in.sem, x_in.at(b))
                    stats(dve, ln, b, 0, xt)
                    yield 6
                    normalize(dve, ln, b, 0, xt, hn)
                    yield 14
                    values(b, v_ps, X, vt, "bv", v_sb)
                    yield 16
                    feature_logits(b, 0, "bqa")
                    yield 18
                    feature_weight(b, 0)
                    yield 20
                    for mc in range(KC):
                        dve.wait_ge(pool_ps.sem, pool_ps.at(b, mc + 1))
                        dve.wait_ge(kT_sb.sem, kT_sb.at(b, mc + 1))
                        dve.tensor_tensor(hT[:, mc, :], ps[:, X + mc, :], kT[:, mc, :], ALU.mult).then_inc(mT_sb.sem, 1)
                    yield 22
                    feature_logits(b, 1, "bka")
                    yield 24
                    feature_weight(b, 1)
                    yield 26
                    for i in range(HV):
                        dve.wait_ge(pk_ps.sem, pk_ps.at(b, i + 1))
                        m, ts = half(X, i)
                        dve.tensor_tensor(lg[:, ts, :], m, vt[:, ts, :], ALU.mult).then_inc(a_mul.sem, 1)
                    yield 28
                    wait_apart(dve, (a_sum.sem, a_sum.at(b)))
                    stats(dve, ln, b, 1, hn)
                    yield 29
                    if not (isinstance(b, int) and b == 0):
                        dve.wait_ge(hc_ps.sem, hc_ps.at(b - 1))
                        dve.wait_ge(x1b_sb.sem, x1b_sb.at(b - 1))
                    normalize(dve, ln, b, 1, hn, x1)

                def cross(b):
                    yield 40
                    wait_apart(dve, (ln.out.sem, ln.out.at(b)))
                    for t in range(TB):
                        dve.tensor_tensor_reduce(xw1[:, t, :], x1[:, t, :], row["w1"], 1.0, 0.0, ALU.mult, ALU.add,
                                                 c1[:, t:t + 1]).then_inc(c1_sb.sem, 1)
                    yield 43
                    for kc in range(KC):
                        dve.wait_ge(x1T_sb.sem, x1T_sb.at(b, kc + 1))
                        dve.tensor_scalar(chT[:, kc, :], x1T[:, kc, :], col["w3"](kc), col["w2"](kc), ALU.mult, ALU.add).then_inc(xwT_sb.sem, 1)
                    yield 45
                    dve.wait_ge(sim_ps.sem, sim_ps.at(b))
                    sim = ps[:, Y, :].rearrange("p (t c) -> p t c", t=TB)
                    dve.tensor_reduce(cmx[:, :], sim[:, :, 0:C], AX.X, ALU.max).then_inc(sim_mx.sem, 1)
                    dve.wait_ge(sim_mx.sem, sim_mx.at(b))
                    dve.tensor_scalar(cnm[:, :], cmx[:, :], -1.0, None, ALU.mult).then_inc(sim_nm.sem, 1)
                    dve.wait_ge(c1_sb.sem, c1_sb.at(b))
                    dve.scalar_tensor_tensor(bm[:, :], cmx[:, :], row["bs"], c1[:, :], ALU.add, ALU.add).then_inc(sim_nm.sem, 1)
                    yield 47
                    dve.wait_ge(bp_sb.sem, bp_sb.at(b))
                    dve.reciprocal(crs[:, :], csm[:, :]).then_inc(bp_rs.sem, 1)
                    dve.wait_ge(bp_rs.sem, bp_rs.at(b))
                    for t in range(TB):
                        dve.tensor_scalar(cw[:, t, :], cp[:, t, :], crs[:, t:t + 1], None, ALU.mult).then_inc(A_sb.sem, 1)
                    dve.wait_ge(mrow_ps.sem, mrow_ps.at(b))
                    dve.tensor_reduce(bg[:, :], ps[0:1, Y + 1, :].rearrange("p (b s) -> p b s", b=SB), AX.X, ALU.max).then_inc(g_sb.sem, 1)
                    yield 49
                    dve.wait_ge(g_ps.sem, g_ps.at(b))
                    for i in range(SB):
                        dve.tensor_scalar(bd[:, 2 * i:2 * i + 2], bm[:, 2 * i:2 * i + 2], ps[:, Y + 1, i:i + 1], None,
                                          ALU.subtract).then_inc(bd_sb.sem, 1)
                    yield 52
                    dve.wait_ge(hqT_sb.sem, hqT_sb.at(b))
                    dve.tensor_tensor(xhT[:, :, :], hqT[:, :, :], x1T[:, :, :], ALU.mult).then_inc(xhT_sb.sem, 1)
                    yield 53
                    dve.wait_ge(hc_ps.sem, hc_ps.at(b))
                    dve.reciprocal(hcr[:, :], ps[:, Y + 1, 0:3 * SB].rearrange("p (b j) -> p b j", j=3)[:, :, 2]).then_inc(hc_rs.sem, 1)
                    dve.wait_ge(hc_rs.sem, hc_rs.at(b))
                    for i in range(SB):
                        dve.tensor_scalar(hc[:, i, :], ps[:, Y + 1, 3 * i:3 * i + KC], hcr[:, i:i + 1], None, ALU.mult).then_inc(hc_sb.sem, 1)
                    dve.wait_ge(hc_sb.sem, hc_sb.at(b))
                    for i in range(SB):
                        for kc in range(KC):
                            dve.scalar_tensor_tensor(Wx[:, i, kc, :], W["Wf3"][:, kc, :], hc[:, i, kc:kc + 1], W["Wf0"][:, kc, :],
                                                     ALU.mult, ALU.add).then_inc(Wx_sb.sem, 1)
                    yield 55
                    dve.wait_ge(x1b_sb.sem, x1b_sb.at(b))
                    for i in range(HV):
                        dve.wait_ge(hcq_ps.sem, hcq_ps.at(b, i + 1))
                        v, ts = half(Y, i)
                        dve.tensor_tensor(chn[:, ts, :], v, x1b[:, ts, :], ALU.add).then_inc(b_sum.sem, 1)
                    wait_apart(dve, (b_sum.sem, b_sum.at(b)))
                    stats(dve, lnc, b, 0, chn)
                    yield 56
                    if not (isinstance(b, int) and b == 0):
                        dve.wait_ge(kept.sem, kept.at(b - 1))
                    normalize(dve, lnc, b, 0, chn, x2)
                    yield 57
                    wait_apart(dve, (lnc.out.sem, lnc.out.at(b, TB)))
                    stats(dve, lnc, b, 1, x2)
                    yield 58
                    normalize(dve, lnc, b, 1, x2, chn)
                    yield 66
                    if not (isinstance(b, int) and b == 0):
                        dve.wait_ge(pT_used.sem, pT_used.at(b - 1))
                    values(b, sv_ps, Y, sv, "fbv", sv_sb)

                def attention(it):
                    for g in range(G + 2):
                        if g < G:
                            t, heads, nb = PORTIONS[g]
                            dve.wait_ge(s_ps.sem, s_ps.at(it, g + 1))
                            dve.tensor_reduce(mx4[:, g % 2, 0:len(heads)], ps[:, g % 2, :].rearrange("p (h k) -> p h k", h=len(heads)),
                                              AX.X, ALU.max).then_inc(s_mx.sem, 1)
                            dve.wait_ge(s_mx.sem, s_mx.at(it, g + 1))
                            dve.tensor_scalar(nm4[:, g % 2, 0:len(heads)], mx4[:, g % 2, 0:len(heads)], -1.0, None, ALU.mult).then_inc(s_nm.sem, 1)
                        yield
                        if 1 <= g <= G and not by_act(g - 1):
                            evacuate(dve, it, g - 1)
                            dve.tensor_copy(PT[:, (g - 1) % 3, :], ps[:, 2, :]).then_inc(pT0_sb.sem, 1)
                        yield
                        for t in range(TB):
                            if LAST[t] != g - 2:
                                continue
                            if t == 0 and not (isinstance(it, int) and it == 0):
                                dve.wait_ge(oT_ps.sem, oT_ps.at(it - 1))
                            dve.wait_ge(pT_used.sem, pT_used.at(it, g - 1))
                            dve.reciprocal(rs16[:, :], sm16[:, t, :]).then_inc(o_rs.sem, 1)
                            dve.wait_ge(o_rs.sem, o_rs.at(it, t + 1))
                            o = ps[:, 3, (t % 2) * D:(t % 2 + 1) * D].rearrange("p (h d) -> p h d", h=H)
                            dve.tensor_tensor(ot[:, t, :].rearrange("p (h d) -> p h d", h=H), o,
                                              rs16[:, :].rearrange("p (h o) -> p h o", o=1).to_broadcast([P, H, HD]),
                                              ALU.mult).then_inc(o_sb.sem, 1)
                        yield

                def project(b):
                    yield 3
                    dve.wait_ge(kept.sem, kept.at(b))
                    for i in range(HV):
                        dve.wait_ge(ao_ps.sem, ao_ps.at(b, i + 1))
                        v, ts = half(X, i)
                        dve.tensor_tensor(at_[:, ts, :], v, xb[:, ts, :], ALU.add).then_inc(c_sum.sem, 1)
                    wait_apart(dve, (c_sum.sem, c_sum.at(b)))
                    stats(dve, ln2, b, 0, at_)
                    yield 4
                    if not (isinstance(b, int) and b == 0):
                        dve.wait_ge(h_out.sem, h_out.at(b - 1))
                    normalize(dve, ln2, b, 0, at_, h2n)

                def route(b):
                    yield 33
                    dve.wait_ge(rl_ps.sem, rl_ps.at(b))
                    dve.tensor_tensor(rl[:, :, :], ps[:, X, 0:TB * E].rearrange("p (t e) -> p t e", t=TB), over_tiles(row["br"]), ALU.add).then_inc(rl_sb.sem, 1)
                    wait_apart(dve, (rl_sb.sem, rl_sb.at(b)))
                    for t in range(TB):
                        dve.max(rt8[:, t, :], rl[:, t, :]).then_inc(rl_max.sem, 1)
                    dve.wait_ge(rl_max.sem, rl_max.at(b))
                    dve.tensor_scalar(rnm[:, :], rt8[:, :, 0], -1.0, None, ALU.mult).then_inc(rl_nm.sem, 1)
                    for t in range(TB):
                        dve.tensor_scalar(rm[:, t, :], rl[:, t, :], rt8[:, t, 1:2], None, ALU.is_ge).then_inc(rm_sb.sem, 1)
                    yield 35
                    dve.wait_ge(rl_exp.sem, rl_exp.at(b))
                    for t in range(TB):
                        dve.scalar_tensor_tensor(rw[:, t, :], rl[:, t, :], rt8[:, t, 1:2], rex[:, t, :], ALU.is_ge, ALU.mult,
                                                 accum_out=rsm[:, t:t + 1]).then_inc(rl_w.sem, 1)
                    dve.wait_ge(rl_w.sem, rl_w.at(b))
                    dve.reciprocal(rrs[:, :], rsm[:, :]).then_inc(rl_rs.sem, 1)
                    dve.wait_ge(rl_rs.sem, rl_rs.at(b))
                    dve.tensor_tensor(rw[:, :, :], rw[:, :, :], rrs[:, :].rearrange("p (t o) -> p t o", o=1).to_broadcast([P, TB, E]),
                                      ALU.mult).then_inc(rl_out.sem, 1)
                    yield 36
                    dve.wait_ge(pos_ps.sem, pos_ps.at(b))
                    pos = ps[:, X, 0:TB * E]
                    dve.tensor_tensor(d1[:, :].rearrange("p (t e) -> p t e", t=TB), pos.rearrange("p (t e) -> p t e", t=TB),
                                      over_tiles(taken[:, :]), ALU.add).then_inc(pos_sb.sem, 1)
                    dve.wait_ge(pos_sb.sem, pos_sb.at(b, 1))
                    dve.tensor_tensor(taken[:, :], ps[:, X, TB * E:TB * E + E], taken[:, :], ALU.add).then_inc(pos_sb.sem, 1)
                    dve.tensor_tensor(d2[:, :], d1[:, :], slots[:, 1, :], ALU.add).then_inc(slot_a.sem, 1)
                    dve.wait_ge(slot_a.sem, slot_a.at(b))
                    dve.tensor_tensor(d3[:, :], d2[:, :], rm[:, :, :].rearrange("p t e -> p (t e)"), ALU.mult).then_inc(slot_b.sem, 1)
                    dve.wait_ge(slot_b.sem, slot_b.at(b))
                    dve.wait_ge(lists_free.sem, lists_free.at(b))
                    dve.tensor_tensor(dst[:, :], d3[:, :], slots[:, 0, :], ALU.add).then_inc(listed.sem, 1)
                    dve.wait_ge(rl_out.sem, rl_out.at(b))
                    dve.tensor_copy(pairs[:, :, 1].bitcast(F32), rw[:, :, :].rearrange("p t e -> p (t e)")).then_inc(listed.sem, 1)
                    dve.tensor_copy(pairs[:, :, 0].rearrange("p (t e) -> p t e", t=TB),
                                    ids[:, :].rearrange("p (t o) -> p t o", o=1).to_broadcast([P, TB, E])).then_inc(listed.sem, 1)
                    dve.wait_ge(listed.sem, listed.at(b + 1, 3))
                    dve.tensor_scalar(ids[:, :], ids[:, :], float(BLK), None, ALU.add).then_inc(listed.sem, 1)

                blocks(dve, attention, project, route, gated, cross)
                dve.wait_ge(pos_sb.sem, pos_sb.at(NBLK - 1))
                dve.tensor_scalar(ci[:, 0, :], taken[0:1, :], float(TE - 1), None, ALU.add).then_inc(counted.sem, 1)
                dve.wait_ge(counted.sem, 1)
                dve.tensor_scalar(ci[:, 1, :], ci[:, 0, :], TE.bit_length() - 1, None, ALU.logical_shift_right).then_inc(counted.sem, 1)
                dve.wait_ge(counted.sem, 2)
                dve.tensor_scalar(cf[:, 0, :], ci[:, 1, :], 2.0, None, ALU.max).then_inc(counted.sem, 1)
                dve.memset(cf[:, 1, 0:1], 0.0).then_inc(counted.sem, 1)
                for e in range(1, E):
                    dve.wait_ge(counted.sem, 3 + e)
                    dve.tensor_tensor(cf[:, 1, e:e + 1], cf[:, 1, e - 1:e], cf[:, 0, e - 1:e], ALU.add).then_inc(counted.sem, 1)
                dve.wait_ge(counted.sem, 3 + E)
                dve.tensor_copy(tiles[:, :, :], cf[:, 0:2, :]).then_inc(counted.sem, 1)

            @block.tensor
            def _(pe):
                pe.wait_ge(c_loaded.sem, 16 * NLOAD)
                pe.wait_ge(consts.sem, 8)
                pe.wait_ge(pool_consts.sem, 3)

                def to_features(src, bank, done, kcs=range(KC)):
                    for kc in kcs:
                        for t in range(TB):
                            ins = pe.transpose(ps[:, bank + kc, t * P:(t + 1) * P], src[:, t, kc * P:(kc + 1) * P], ident[:, :])
                        ins.then_inc(done.sem, 1)

                def to_tokens(b, src, done, free, n):
                    for i in range(HV):
                        pe.wait_ge(free.sem, free.at(b, n * TB + 2 * i + 2))
                        for t in (2 * i, 2 * i + 1):
                            for kc in range(KC):
                                ins = pe.transpose(tile_of(X, t)[:, kc * P:(kc + 1) * P], src[:, kc, t * P:(t + 1) * P], ident[:, :])
                        ins.then_inc(done.sem, 1)

                def weight_rows(b, w, src, bank, done, free=None):
                    for mc in range(KC):
                        if free:
                            pe.wait_ge(free.sem, free.at(b, free.per // KC * (mc + 1)))
                        for kc in range(KC):
                            ins = pe.matmul(ps[:, bank + mc, :], w[:, kc, mc * P:(mc + 1) * P], src[:, kc, :],
                                            start=(kc == 0), stop=(kc == KC - 1))
                        ins.then_inc(done.sem, 1)

                def token_rows(b, terms_of, bank, done, free=None):
                    for i in range(HV):
                        if free:
                            pe.wait_ge(free.sem, free.at(b, i + 1))
                        for t in (2 * i, 2 * i + 1):
                            terms = terms_of(t)
                            n = len(terms) * KC
                            for k, (src, w) in enumerate(terms):
                                for kc in range(KC):
                                    j = k * KC + kc
                                    ins = pe.matmul(tile_of(bank, t), src[:, kc, t * P:(t + 1) * P], w[:, kc, :],
                                                    start=(j == 0), stop=(j == n - 1))
                        ins.then_inc(done.sem, 1)

                def gated(b, has_behind):
                    yield 7
                    pe.wait_ge(ln.out.sem, ln.out.at(b, TB))
                    if has_behind:
                        pe.wait_ge(c_sum.sem, c_sum.at(b - 3))
                    elif b:
                        pe.wait_ge(a_mul.sem, a_mul.at(b - 1))
                    to_features(hn, X, hT_ps)
                    yield 9
                    pe.wait_ge(hT_sb.sem, hT_sb.at(b))
                    weight_rows(b, W["Wq"], hT, X, q_ps)
                    yield 11
                    weight_rows(b, W["Wk"], hT, X, k_ps, qT_sb)
                    yield 13
                    token_rows(b, lambda t: [(hT, W["Wv"])], X, v_ps, kT_sb)
                    yield 15
                    token_rows(b, lambda t: [(qT, W["Wqa"])], X, lg_ps, v_sb)
                    yield 17
                    to_tokens(b, qT, tok_ps, lg_sb, 0)
                    yield 19
                    pe.wait_ge(w_sb.sem, w_sb.at(b, TB))
                    for mc in range(KC):
                        for i in range(SB):
                            o = ps[:, X + mc, i * S:(i + 1) * S]
                            pe.matmul(o, wt[:, 2 * i, mc * P:(mc + 1) * P], tri[:, 0:2, :].rearrange("p a q -> p (a q)"),
                                      start=True, stop=False, skip_group_check=True)
                            ins = pe.matmul(o[:, P:S], wt[:, 2 * i + 1, mc * P:(mc + 1) * P], tri[:, 2, :],
                                            start=False, stop=True, skip_group_check=True)
                        ins.then_inc(pool_ps.sem, 1)
                    yield 21
                    pe.wait_ge(mT_sb.sem, mT_sb.at(b))
                    token_rows(b, lambda t: [(hT, W["Wka"])], X, lg_ps)
                    yield 23
                    to_tokens(b, hT, tok_ps, lg_sb, 1)
                    yield 25
                    for t in range(TB):
                        if t % 2 == 0:
                            pe.wait_ge(w_sb.sem, w_sb.at(b, TB + t + 2))
                        o = tile_of(X, t)
                        if t % 2 == 0:
                            pe.matmul(o, tri[:, 0, :], wt[:, t, :], start=True, stop=True)
                        else:
                            pe.matmul(o, tri[:, 1, :], wt[:, t - 1, :], start=True, stop=False)
                            pe.matmul(o, tri[:, 2, :], wt[:, t, :], start=False, stop=True).then_inc(pk_ps.sem, 1)

                def cross(b):
                    yield 39
                    pe.wait_ge(ctx_in_.sem, ctx_in_.at(b))
                    pe.wait_ge(ln.out.sem, ln.out.at(b))
                    if not (isinstance(b, int) and b == 0):
                        pe.wait_ge(sv_sb.sem, sv_sb.at(b - 1))
                    for i in range(SB):
                        for kc in range(KC):
                            o = ps[:, Y, kc * SB * C + i * C:kc * SB * C + (i + 1) * C]
                            ins = pe.transpose(o, ctx[:, i, kc * P:(kc + 1) * P], ident[0:C, 0:C])
                    ins.then_inc(cT_ps.sem, 1)
                    to_features(x1, Y + 1, x1T_ps, [0])
                    yield 41
                    pe.wait_ge(cT_sb.sem, cT_sb.at(b))
                    to_features(x1, Y - 1, x1T_ps, [1])
                    yield 44
                    pe.wait_ge(xwT_sb.sem, xwT_sb.at(b))
                    for t in range(TB):
                        tok = slice(t * P, (t + 1) * P)
                        for kc in range(KC):
                            ins = pe.matmul(ps[:, Y, t * P:t * P + C], chT[:, kc, tok], cT[:, kc, (t // 2) * C:(t // 2 + 1) * C],
                                      start=(kc == 0), stop=(kc == KC - 1))
                    ins.then_inc(sim_ps.sem, 1)
                    yield 46
                    pe.wait_ge(sim_nm.sem, sim_nm.at(b))
                    for t in range(TB):
                        ins = pe.transpose(ps[0:1, Y + 1, t * P:(t + 1) * P], bm[:, t:t + 1], ident[:, :])
                    ins.then_inc(mrow_ps.sem, 1)
                    yield 48
                    pe.wait_ge(A_sb.sem, A_sb.at(b))
                    for t in range(TB):
                        ins = pe.transpose(ps[0:C, Y, t * P:(t + 1) * P], cw[:, t, :], ident[:, :])
                    ins.then_inc(AT_ps.sem, 1)
                    pe.wait_ge(g_sb.sem, g_sb.at(b))
                    pe.matmul(ps[:, Y + 1, 0:SB], ones[0:1, :], bg[:, :], start=True, stop=True).then_inc(g_ps.sem, 1)
                    yield 50
                    pe.wait_ge(AT_sb.sem, AT_sb.at(b))
                    pe.wait_ge(bd_sb.sem, bd_sb.at(b))
                    for mc in range(KC):
                        for i in range(SB):
                            ins = pe.matmul(ps[:, Y + mc, i * S:(i + 1) * S], ctx[:, i, mc * P:(mc + 1) * P], AT[:, i * S:(i + 1) * S],
                                            start=True, stop=True)
                        ins.then_inc(hq_ps.sem, 1)
                    yield 52
                    pe.wait_ge(be_sb.sem, be_sb.at(b))
                    pe.wait_ge(hqT_sb.sem, hqT_sb.at(b))
                    for i in range(SB):
                        for j in range(KC + 1):
                            for k in range(2):
                                t = 2 * i + k
                                lhs = x1[:, t, j * P:(j + 1) * P] if j < KC else ones[:, :]
                                ins = pe.matmul(ps[:, Y + 1, 3 * i + j:3 * i + j + 1], lhs, be[:, t:t + 1], start=(k == 0), stop=(k == 1))
                    ins.then_inc(hc_ps.sem, 1)
                    yield 54
                    pe.wait_ge(xhT_sb.sem, xhT_sb.at(b))
                    pe.wait_ge(Wx_sb.sem, Wx_sb.at(b))
                    token_rows(b, lambda t: [(x1T, Wx[:, t // 2]), (hqT, W["Wf1"]), (xhT, W["Wf2"])], Y, hcq_ps)
                    yield 59
                    pe.wait_ge(lnc.out.sem, lnc.out.at(b))
                    to_features(chn, Y, shT_ps)
                    yield 61
                    pe.wait_ge(shT_sb.sem, shT_sb.at(b))
                    weight_rows(b, W["fWq"], chT, Y, sq_ps)
                    yield 63
                    weight_rows(b, W["fWk"], chT, Y, sk_ps, qz_sb)
                    yield 65
                    token_rows(b, lambda t: [(chT, W["fWv"])], Y, sv_ps, skT_sb)

                def attention(it):
                    def scores(g):
                        t, heads, nb = PORTIONS[g]
                        b, L = t // 2, P * nb
                        if g == 0:
                            pe.wait_ge(qz_sb.sem, qz_sb.at(it))
                            pe.wait_ge(skT_sb.sem, skT_sb.at(it))
                        if g >= 2:
                            pe.wait_ge(s_p.sem, s_p.at(it, g - 1))
                        pe.matmul(ps[:, g % 2, :].rearrange("p (e k) -> p e k", k=L)[:, :, L - P:L], identb[:, :],
                                  mask[:, 0:1, :].to_broadcast([P, len(heads), P]), start=True, stop=False, skip_group_check=True)
                        for h, head in enumerate(heads):
                            kc, row0 = head // 8, head % 8 // 2 * 2 * HD
                            rows_ = slice(row0, row0 + 2 * HD)
                            ins = pe.matmul(ps[:, g % 2, h * L:(h + 1) * L], qz[rows_, head % 2, kc, t * P:(t + 1) * P],
                                            skT[rows_, kc, b * S:b * S + L], start=False, stop=True, skip_group_check=True)
                        ins.then_inc(s_ps.sem, 1)

                    def turn(g):
                        pe.wait_ge(s_p.sem, s_p.at(it, g + 1))
                        if g:
                            in_sbuf(pe, it, g - 1)
                        for i in range(4):
                            ins = pe.transpose(ps[:, 2, i * P:(i + 1) * P], p2[:, g % 2, i * P:(i + 1) * P], ident[:, :])
                        ins.then_inc(pT_ps.sem, 1)

                    def weigh(g):
                        t, heads, nb = PORTIONS[g]
                        in_sbuf(pe, it, g)
                        if g == 0:
                            pe.wait_ge(sv_sb.sem, sv_sb.at(it))
                        if heads[0] == 0 and t:
                            pe.wait_ge(o_sb.sem, o_sb.at(it, t))
                        for i in range(4):
                            h, kb = heads[i // nb], i % nb
                            o = (t % 2) * D + h * HD
                            ins = pe.matmul(ps[:, 3, o:o + HD], PT[:, g % 3, i * P:(i + 1) * P],
                                            sv[:, 2 * (t // 2) + kb, h * HD:(h + 1) * HD], start=(kb == 0), stop=(kb == nb - 1))
                        ins.then_inc(pT_used.sem, 1)

                    for g in range(G + 2):
                        if g < G:
                            scores(g)
                        yield
                        if 1 <= g <= G:
                            turn(g - 1)
                        yield
                        if g >= 2:
                            weigh(g - 2)
                        yield

                def project(b):
                    yield 0
                    pe.wait_ge(o_sb.sem, o_sb.at(b))
                    if not (isinstance(b, int) and b + 2 >= NBLK):
                        pe.wait_ge(a_mul.sem, a_mul.at(b + 2))
                    pe.wait_ge(pos_sb.sem, pos_sb.at(b - 1))
                    to_features(ot, X, oT_ps)
                    yield 2
                    pe.wait_ge(oT_sb.sem, oT_sb.at(b))
                    token_rows(b, lambda t: [(oT, W["fWo"])], X, ao_ps)

                def route(b):
                    yield 30
                    pe.wait_ge(ln2.out.sem, ln2.out.at(b))
                    if not (isinstance(b, int) and b + 3 >= NBLK):
                        pe.wait_ge(a_mul.sem, a_mul.at(b + 3))
                    to_features(h2n, X, h2T_ps)
                    yield 32
                    pe.wait_ge(h2T_sb.sem, h2T_sb.at(b))
                    for t in range(TB):
                        for kc in range(KC):
                            ins = pe.matmul(ps[:, X, t * E:(t + 1) * E], h2T[:, kc, t * P:(t + 1) * P], wr[:, kc, :], start=(kc == 0), stop=(kc == KC - 1))
                    ins.then_inc(rl_ps.sem, 1)
                    yield 34
                    pe.wait_ge(rm_sb.sem, rm_sb.at(b))
                    for t in range(TB):
                        o = ps[:, X, t * E:(t + 1) * E]
                        for u in range(t):
                            pe.matmul(o, onesb[:, :], rm[:, u, :], start=(u == 0), stop=False)
                        pe.matmul(o, lower[:, :], rm[:, t, :], start=(t == 0), stop=True)
                    for t in range(TB):
                        ins = pe.matmul(ps[:, X, TB * E:TB * E + E], onesb[:, :], rm[:, t, :], start=(t == 0), stop=(t == TB - 1))
                    ins.then_inc(pos_ps.sem, 1)

                blocks(pe, attention, project, route, gated, cross)

        with ExitStack() as back:
            def bb(name, shape, dt=F32):
                return back.enter_context(nc.sbuf_tensor(name, shape, dt))

            def bsig(name, per=1):
                return Count(back.enter_context(nc.semaphore(name)), per)

            RING = 4
            NW = 8
            WC = (KC * F + FT * D) // NW
            whi = bb("w_hi", [P, 2, KC * F + FT * D], F32R)
            wlo = bb("w_lo", [P, 2, KC * F + FT * D], F32R)
            b1e = bb("b1_of_expert", [P, 2, FT])
            b2e = bb("b2_of_expert", [P, 2, D])
            b2w = bb("b2_weighted", [P, 2, D])
            li = bb("list_in", [P, 2, 2], I32)
            lis = bb("list_out", [P, 2, 2], I32)
            hg = bb("h_gathered", [P, 2, D])
            hT = bb("h_T", [P, KC, TE])
            hh = bb("h_hi", [P, KC, TE], F32R)
            hl = bb("h_lo", [P, KC, TE], F32R)
            mid = bb("mid", [P, RING, TE])
            midh = bb("mid_hi", [P, RING, TE], F32R)
            midl = bb("mid_lo", [P, RING, TE], F32R)
            y = bb("y", [P, 2, D])
            OB = 4
            rt = bb("r_tok", [P, OB, TB, D])
            ost = bb("out_st", [P, 2, TB, 6])
            omv = bb("out_mv", [P, 2, TB, 2])
            ove = bb("out_ve", [P, 2, TB])
            ors = bb("out_rstd", [P, 2, TB])
            ob = bb("out_buf", [P, OB, TB, D])

            w_split_hi = bsig("w_split_hi", NW)
            b2_set = bsig("b2_set")
            b2w_set = bsig("b2w_set", 2)
            w_split_lo = bsig("w_split_lo", NW)
            b1_set = bsig("b1_set")
            li_in = bsig("li_in", 16)
            hg_in = bsig("hg_in", 32)
            T_ps = bsig("T_ps")
            hT_sb = bsig("hT_sb_e", KC)
            h_hi = bsig("h_hi_set")
            h_lo = bsig("h_lo_set")
            up_ps = bsig("up_ps", FT)
            mid_sb = bsig("mid_sb", FT)
            mid_hi = bsig("mid_hi_set", FT)
            mid_lo = bsig("mid_lo_set", FT)
            mid_used = bsig("mid_used", FT)
            y_sb = bsig("y_sb", 2)
            lis_in = bsig("lis_in", 16)
            sc_done = bsig("sc_done", 32)
            r_in = [bsig(f"r_in_{j}", 16) for j in range(OB)]
            o_st = bsig("o_st", TB)
            o_mv = bsig("o_mv", TB)
            o_ve = bsig("o_ve")
            o_rstd = bsig("o_rstd")
            o_out = bsig("o_out", TB)
            stored = [bsig(f"stored_{j}", 16) for j in range(OB)]
            all_scattered = bsig("all_scattered")
            enlisted_0 = bsig("enlisted_0", 16 * TB)
            enlisted = bsig("enlisted", 16 * TB * (E - 1))
            may_load = bsig("may_load")
            block = back.enter_context(nc.Block())

            def w1_of(w, j):
                return w[:, j, 0:KC * F].rearrange("p (k f) -> p k f", k=KC)

            def w2_of(w, j):
                return w[:, j, KC * F:].rearrange("p (f d) -> p f d", f=FT)

            def experts(eng, run, first=0):
                for e in range(2 * first):
                    run(e, e % 2, False)
                with eng.Fori(first, E // 2 - 1) as half:
                    for j in range(2):
                        run(half * 2 + j, j, False)
                for j in range(2):
                    run(E - 2 + j, j, j == 1)

            def tiles_of(eng, e):
                mine = eng.value_load(tiles[0:1, 0, bass.ds(e, 1)], min_val=2, max_val=CAP // TE)
                before = eng.value_load(tiles[0:1, 1, bass.ds(e, 1)], min_val=0, max_val=E * CAP // TE)
                return mine, before

            def list_part(e, k):
                return lists[bass.ds(e * CAP + k * TE, TE), :].rearrange("(h p) c -> p h c", p=P)

            @block.sync
            def _(sp):
                sp.dma_start(lis[:, :, :], unused_in[0:TE, :].rearrange("(h p) c -> p h c", p=P)).then_inc(lis_in.sem, 16)
                sp.wait_ge(lis_in.sem, 16)
                sp.dma_start(lis[:, :, :], unused_in[0:TE, :].rearrange("(h p) c -> p h c", p=P)).then_inc(lis_in.sem, 16)

                def load_list(e, k, n):
                    sp.wait_ge(may_load.sem, may_load.at(n))
                    sp.wait_ge(T_ps.sem, T_ps.at(n))
                    sp.dma_start(li[:, :, :], list_part(e, k)).then_inc(li_in.sem, 16)

                def expert(e, j, last):
                    mine, before = tiles_of(sp, e)
                    with sp.Fori(0, mine) as k:
                        load_list(e, k, before + k)
                    if last:
                        load_list(0, 0, before + mine)

                experts(sp, expert)
                sp.wait_ge(all_scattered.sem, 1)
                for j in range(OB):
                    sp.nop().then_inc(stored[j].sem, 16)
                with sp.Fori(0, NBLK // OB) as i:
                    for j in range(OB):
                        sp.wait_ge(stored[j].sem, stored[j].at(i))
                        sp.dma_start(rt[:, j], r_rows[bass.ds((i * OB + j) * BLK, BLK), :].rearrange("(t p) d -> p t d", p=P)).then_inc(r_in[j].sem, 16)
                for j in range(OB):
                    sp.wait_ge(stored[j].sem, 16 * NBLK // OB + 16)

            @block.gpsimd
            def _(pool):
                pool.memset(y[:, :, :], 0.0).then_inc(y_sb.sem, 2 * y_sb.per)
                pool.nop().then_inc(T_ps.sem, 1)
                scatter(pool, range(0, TB * E, E), enlisted_0.sem)
                pool.wait_ge(enlisted_0.sem, enlisted_0.per)
                pool.nop().then_inc(may_load.sem, 2)
                pool.wait_ge(y_sb.sem, 2 * y_sb.per)
                pool.wait_ge(lis_in.sem, 2 * 16)
                for h in range(2):
                    pool.indirect_dma_start(r_rows, bass.IndirectOffsetOnAxis(lis[:, h, 0:1], 0), y[:, h, :], None,
                                            compute_op=ALU.add).then_inc(sc_done.sem, 16)

                def load_rows(n):
                    wait_apart(pool, (li_in.sem, li_in.at(n)))
                    for h in range(2):
                        pool.indirect_dma_start(hg[:, h, :], None, h_rows, bass.IndirectOffsetOnAxis(li[:, h, 0:1], 0)).then_inc(hg_in.sem, 16)

                def add_rows(n):
                    wait_apart(pool, (y_sb.sem, y_sb.at(n)), (lis_in.sem, lis_in.at(n)), (sc_done.sem, sc_done.at(n)))
                    for h in range(2):
                        pool.indirect_dma_start(r_rows, bass.IndirectOffsetOnAxis(lis[:, h, 0:1], 0), y[:, h, :], None,
                                                compute_op=ALU.add).then_inc(sc_done.sem, 16)

                def expert(e, j, last):
                    mine, before = tiles_of(pool, e)
                    def tile(k):
                        add_rows(before + k)
                        load_rows(before + k + 1)

                    if isinstance(e, int) and e == 0:
                        scatter(pool, others[:len(others) // 3], enlisted.sem)
                        tile(0)
                        scatter(pool, others[len(others) // 3:], enlisted.sem)
                        pool.wait_ge(enlisted.sem, enlisted.per)
                        pool.nop().then_inc(may_load.sem, E * CAP // TE)
                        with pool.Fori(1, mine) as k:
                            tile(k)
                    else:
                        with pool.Fori(0, mine) as k:
                            tile(k)
                    if last:
                        end = before + mine
                        add_rows(end)
                        add_rows(end + 1)
                        wait_apart(pool, (sc_done.sem, sc_done.at(end + 2)), (hg_in.sem, hg_in.at(end)))
                        pool.memset(ors[:, 0, :], 0.0).then_inc(all_scattered.sem, 1)

                load_rows(0)
                others = [t * E + e for e in range(1, E) for t in range(TB)]
                experts(pool, expert, first=1)
                pool.wait_ge(all_scattered.sem, 1)
                with pool.Fori(0, NBLK // 2) as i:
                    for j in range(2):
                        pool.wait_ge(o_ve.sem, o_ve.at(i * 2 + j))
                        pool.tensor_tensor(ors[:, j, :], ove[:, j, :], eps_t[:, :], ALU.pow).then_inc(o_rstd.sem, 1)

            @block.scalar
            def _(act):
                act.nop().then_inc(mid_sb.sem, RING)

                def split_hi(e, j, c):
                    if c == 0:
                        act.activation(b2e[:, j, :], raw_b2[:, :], ACT.Copy).then_inc(b2_set.sem, 1)
                    act.activation(whi[:, j, c * WC:(c + 1) * WC], raw[:, c * WC:(c + 1) * WC], ACT.Copy).then_inc(w_split_hi.sem, 1)

                def h_out_of_psum(n):
                    act.wait_ge(T_ps.sem, T_ps.at(n) + 1)
                    for kc in range(KC):
                        act.activation(hT[:, kc, :], ps[:, 4, kc * TE:(kc + 1) * TE], ACT.Identity, bias=cols[:, COLS.index("b2"), kc:kc + 1],
                                       scale=cols[:, COLS.index("g2"), kc:kc + 1]).then_inc(hT_sb.sem, 1)

                act.wait_ge(w_in.sem, w_in.at(0))
                for c in range(NW):
                    split_hi(0, 0, c)
                h_out_of_psum(0)

                def tile(e, k, n, j, split=None):
                    for f in range(FT):
                        act.wait_ge(up_ps.sem, up_ps.at(n, f + 1))
                        act.wait_ge(mid_lo.sem, mid_lo.at(n, f + 1))
                        act.activation(mid[:, f % RING, :], ps[:, f % RING, 0:TE], ACT.Gelu, bias=b1e[:, j, f:f + 1]).then_inc(mid_sb.sem, 1)
                        if split:
                            split(f)
                    h_out_of_psum(n + 1)
                    act.wait_ge(sc_done.sem, sc_done.at(n + 2))
                    act.dma_start(lis[:, :, :], list_part(e, k)).then_inc(lis_in.sem, 16)

                def expert(e, j, last):
                    mine, before = tiles_of(act, e)
                    act.activation(b1e[:, j, :], eb1[:, bass.ds(e, 1), :].rearrange("p o f -> p (o f)"), ACT.Copy).then_inc(b1_set.sem, 1)
                    act.wait_ge(b1_set.sem, b1_set.at(e))
                    if last:
                        tile(e, 0, before, j)
                    else:
                        act.wait_ge(w_in.sem, w_in.at(e + 1))
                        act.wait_ge(mid_used.sem, before * FT + RING)
                        act.wait_ge(b2w_set.sem, before * b2w_set.per)
                        tile(e, 0, before, j, lambda c: split_hi(e + 1, 1 - j, c))
                        if not isinstance(e, int):
                            act.wait_ge(w_split_lo.sem, w_split_lo.at(e + 1))
                            load_expert(act, e + 2)
                    with act.Fori(1, mine) as k:
                        tile(e, k, before + k, j)

                act.wait_ge(w_split_lo.sem, w_split_lo.at(0))
                load_expert(act, 1)
                experts(act, expert)
                with act.Fori(0, NBLK // OB) as i:
                    for j in range(OB):
                        act.wait_ge(o_out.sem, o_out.at(i * OB + j))
                        act.dma_start(out[bass.ds((i * OB + j) * TB, TB)].rearrange("t p d -> p t d"), ob[:, j]).then_inc(stored[j].sem, 16)

            @block.vector
            def _(dve):
                dve.nop().then_inc(mid_lo.sem, RING)

                def split_lo(e, j, c):
                    dve.wait_ge(w_split_hi.sem, w_split_hi.at(e, c + 1))
                    w = slice(c * WC, (c + 1) * WC)
                    dve.tensor_tensor(wlo[:, j, w], raw[:, w], whi[:, j, w].bitcast(F32), ALU.subtract).then_inc(w_split_lo.sem, 1)

                def split_h(n):
                    dve.wait_ge(hT_sb.sem, hT_sb.at(n))
                    dve.tensor_copy(hh[:, :, :], hT[:, :, :]).then_inc(h_hi.sem, 1)
                    dve.wait_ge(h_hi.sem, h_hi.at(n))
                    dve.tensor_tensor(hl[:, :, :], hT[:, :, :], hh[:, :, :].bitcast(F32), ALU.subtract).then_inc(h_lo.sem, 1)

                for c in range(NW):
                    split_lo(0, 0, c)
                split_h(0)

                def tile(e, n, j, split=None):
                    for f in range(FT):
                        dve.wait_ge(mid_sb.sem, mid_sb.at(n, f + 1) + RING)
                        dve.wait_ge(mid_used.sem, mid_used.at(n, f + 1))
                        dve.tensor_copy(midh[:, f % RING, :], mid[:, f % RING, :]).then_inc(mid_hi.sem, 1)
                        dve.wait_ge(mid_hi.sem, mid_hi.at(n, f + 1))
                        dve.tensor_tensor(midl[:, f % RING, :], mid[:, f % RING, :], midh[:, f % RING, :].bitcast(F32),
                                          ALU.subtract).then_inc(mid_lo.sem, 1)
                        if split and f:
                            split(f - 1)
                    split_h(n + 1)
                    if split:
                        split(FT - 1)
                    dve.wait_ge(b2_set.sem, b2_set.at(e))
                    dve.wait_ge(lis_in.sem, lis_in.at(n + 2))
                    for h in range(2):
                        dve.tensor_scalar(b2w[:, h, :], b2e[:, j, :], lis[:, h, 1:2].bitcast(F32), None, ALU.mult).then_inc(b2w_set.sem, 1)
                    dve.wait_ge(b2w_set.sem, b2w_set.at(n))
                    dve.wait_ge(mid_used.sem, mid_used.at(n) + RING)
                    for h in range(2):
                        dve.scalar_tensor_tensor(y[:, h, :], ps[:, 5, h * D:(h + 1) * D], lis[:, h, 1:2].bitcast(F32), b2w[:, h, :],
                                                 ALU.mult, ALU.add).then_inc(y_sb.sem, 1)

                def expert(e, j, last):
                    mine, before = tiles_of(dve, e)
                    tile(e, before, j, None if last else lambda c: split_lo(e + 1, 1 - j, c))
                    with dve.Fori(1, mine) as k:
                        tile(e, before + k, j)

                experts(dve, expert)
                with dve.Fori(0, NBLK // OB) as i:
                    def out_stats(j):
                        k = i * OB + j
                        dve.wait_ge(r_in[j].sem, r_in[j].at(i))
                        for t in range(TB):
                            dve.bn_stats(ost[:, j % 2, t, :], rt[:, j, t, :]).then_inc(o_st.sem, 1)
                        for t in range(TB):
                            wait_apart(dve, (o_st.sem, o_st.at(k, t + 1)))
                            dve.bn_aggr(omv[:, j % 2, t, :], ost[:, j % 2, t, :]).then_inc(o_mv.sem, 1)
                        dve.wait_ge(o_mv.sem, o_mv.at(k))
                        dve.tensor_scalar(ove[:, j % 2, :], omv[:, j % 2, :, 1], EPS, None, ALU.add).then_inc(o_ve.sem, 1)

                    def out_rows(j):
                        k = i * OB + j
                        dve.wait_ge(o_rstd.sem, o_rstd.at(k))
                        dve.wait_ge(stored[j].sem, stored[j].at(i))
                        for t in range(TB):
                            dve.tensor_scalar(ob[:, j, t, :], rt[:, j, t, :], omv[:, j % 2, t, 0:1], ors[:, j % 2, t:t + 1],
                                              ALU.subtract, ALU.mult).then_inc(o_out.sem, 1)

                    for j in range(OB):
                        out_stats(j)
                        if j:
                            out_rows(j - 1)
                    out_rows(OB - 1)

            @block.tensor
            def _(pe):
                pe.nop().then_inc(mid_used.sem, RING)

                def turn(n):
                    pe.wait_ge(hg_in.sem, hg_in.at(n))
                    for h in range(2):
                        for kc in range(KC):
                            ins = pe.transpose(ps[:, 4, kc * TE + h * P:kc * TE + (h + 1) * P], hg[:, h, kc * P:(kc + 1) * P], ident[:, :])
                    ins.then_inc(T_ps.sem, 1)

                turn(0)

                def tile(n, j):
                    def up(f):
                        pe.wait_ge(mid_sb.sem, mid_sb.at(n, f + 1))
                        fs = slice(f * P, (f + 1) * P)
                        terms = ((w1_of(whi, j), hh), (w1_of(wlo, j), hh), (w1_of(whi, j), hl))
                        for i, (w, h) in enumerate(terms):
                            for kc in range(KC):
                                ins = pe.matmul(ps[:, f % RING, 0:TE], w[:, kc, fs], h[:, kc, :],
                                                start=(i == 0 and kc == 0), stop=(i == 2 and kc == KC - 1))
                        ins.then_inc(up_ps.sem, 1)

                    def down(f):
                        pe.wait_ge(mid_lo.sem, mid_lo.at(n, f + 1) + RING)
                        if f == 0:
                            pe.wait_ge(y_sb.sem, y_sb.at(n))
                        for h in range(2):
                            hs = slice(h * P, (h + 1) * P)
                            terms = ((midh, w2_of(whi, j)), (midh, w2_of(wlo, j)), (midl, w2_of(whi, j)))
                            for i, (m, w) in enumerate(terms):
                                ins = pe.matmul(ps[:, 5, h * D:(h + 1) * D], m[:, f % RING, hs], w[:, f, :],
                                                start=(f == 0 and i == 0 and h == 0), stop=(f == FT - 1 and i == 2),
                                                skip_group_check=True)
                        ins.then_inc(mid_used.sem, 1)

                    pe.wait_ge(h_lo.sem, h_lo.at(n))
                    LEAD = 3
                    for f in range(LEAD):
                        up(f)
                    for f in range(FT):
                        if f + LEAD < FT:
                            up(f + LEAD)
                        if f + LEAD == FT - 1:
                            turn(n + 1)
                        down(f)

                def expert(e, j, last):
                    mine, before = tiles_of(pe, e)
                    wait_apart(pe, (w_split_lo.sem, w_split_lo.at(e)))
                    with pe.Fori(0, mine) as k:
                        tile(before + k, j)

                experts(pe, expert)


def kernel(**inputs):
    import numpy as np
    import concourse.bacc as bacc
    from concourse import mybir as mb
    from concourse.bass_utils import run_bass_kernel_spmd as run

    g = {k: np.asarray(v) for k, v in inputs.items()}
    f32 = np.float32
    a, xa, ff = "L0_attn_", "L0_xattn_", "L0_ffn_"
    halves = np.arange(D) // HD % 2
    w_sim = g[xa + "w_sim"]
    vec = {
        "bq": g[a + "bq"], "bk": g[a + "bk"], "gamma": g[a + "gamma"], "beta": g[a + "beta"],
        "w2": w_sim[D:2 * D], "w3": w_sim[2 * D:],
        "g1": g[ff + "ln1_g"], "b1": g[ff + "ln1_b"], "g2": g[ff + "ln2_g"], "b2": g[ff + "ln2_b"],
        "fbq": g[ff + "bq"], "fbk": g[ff + "bk"],
        "even": (halves == 0).astype(f32), "odd": (halves == 1).astype(f32),
    }
    cols = np.stack([vec[n].reshape(KC, P) for n in COLS]).transpose(2, 0, 1)
    rvec = {"bv": g[a + "bv"], "bqa": g[a + "bqa"], "bka": g[a + "bka"], "bqv": g[xa + "b_qv"],
            "fbv": g[ff + "bv"], "bo": g[ff + "bo"], "br": g[ff + "br"], "bs": g[xa + "b_sim"],
            "w1": w_sim[:D]}
    rows = np.broadcast_to(np.concatenate([rvec[n] for n in ROWS]), (P, sum(ROWS.values())))
    Wf = g[xa + "W_qv"]
    mat = {"Wq": g[a + "Wq"], "Wqa": g[a + "Wqa"], "Wk": g[a + "Wk"], "Wka": g[a + "Wka"], "Wv": g[a + "Wv"],
           "fWq": g[ff + "Wq"], "fWk": g[ff + "Wk"], "fWv": g[ff + "Wv"], "fWo": g[ff + "Wo"]}
    for i in range(4):
        mat[f"Wf{i}"] = Wf[i * D:(i + 1) * D]
    mats = np.stack([mat[n] for n in MATS])
    ident = np.eye(P, dtype=f32)
    t = np.arange(P)
    le = t[:, None] <= t[None, :]
    tri = np.stack([le / (t + 1.0), np.ones((P, P)) / (t + P + 1.0), le / (t + P + 1.0)], 1).astype(f32)
    mask = np.where(t[None, :] > t[:, None], -1e30, 0.0).astype(np.dtype(mb.dt.np(mb.dt.bfloat16)))[:, None, :]
    spare = E * CAP + (np.arange(TB * E)[None, :] * P + t[:, None]).astype(f32)
    start = np.tile(np.arange(E) * CAP, TB)[None, :].astype(f32)
    unused = np.zeros((E * CAP, 2), np.int32)
    unused[:, 0] = T + np.arange(E * CAP) % PAD
    arrays = {
        "x": g["x"].reshape(NT, P, D), "ctx": g["ctx_1024"], "mats": mats, "cols": cols, "rows": rows,
        "wr": g[ff + "Wr"], "ident": ident, "tri": tri, "mask": mask,
        "lower": (t[:, None] < t[None, :]).astype(mask.dtype), "slots": np.stack([spare, start - spare], 1),
        "ids": (t[:, None] + P * np.arange(TB)[None, :]).astype(f32), "unused": unused, "zeros": np.zeros((PAD, D), f32),
        "w1": g[ff + "e_w1"], "w2": g[ff + "e_w2"],
        "eb1": g[ff + "e_b1"].reshape(E, FT, P).transpose(2, 0, 1), "eb2": np.broadcast_to(g[ff + "e_b2"][:, None, :], (E, P, D)),
    }
    arrays = {k: np.ascontiguousarray(v) for k, v in arrays.items()}
    nc = bacc.Bacc("TRN2", target_bir_lowering=False, num_devices=1)
    args = [nc.dram_tensor(k, v.shape, mb.dt.from_np(v.dtype), kind="ExternalInput").ap() for k, v in arrays.items()]
    args.append(nc.dram_tensor("out", (NT, P, D), F32, kind="ExternalOutput").ap())
    decoder_kernel(nc, *args)
    r = run(nc, [arrays], core_ids=[0])
    return r.results[0]["out"].reshape(B, S, D)
```
